# Optimizing a Trainium2 kernel written in Bass

```python
import numpy as np
import jax
import jax.numpy as jnp

def _softmax(x, axis=-1):
    return jax.nn.softmax(x, axis=axis)

def _gelu(x):
    return jax.nn.gelu(x, approximate=True)

def _silu(x):
    return jax.nn.silu(x)

def _sigmoid(x):
    return jax.nn.sigmoid(x)

def _layernorm(x, axis=-1, eps=1e-05):
    m = jnp.mean(x, axis=axis, keepdims=True)
    v = jnp.var(x, axis=axis, keepdims=True)
    return (x - m) / jnp.sqrt(v + eps)

def _scatter_add(tgt, idx, src, axis=0):
    return tgt.at[idx].add(src)

def _segment_sum(src, seg, n):
    return jax.ops.segment_sum(src, seg, n)
kernel_name = 'mk_decoder_preln_d2_seqx_r8_207b35'

def setup_inputs(seed: int=0):
    np.random.seed(seed)
    _w = jnp.asarray

    def _rec_inputs():
        import jax
        import jax.numpy as jnp
        _rk = jax.random.key(seed)
        x = 0.000341 + 1 * jax.random.normal(jax.random.fold_in(_rk, 1), (16, 128, 256), jnp.float32)
        _lenS = 128 - jax.random.randint(jax.random.fold_in(_rk, 7), (16,), 0, max(1, 128 // 4) + 1, jnp.int32)
        _lenS2 = 128 - jax.random.randint(jax.random.fold_in(_rk, 8), (16,), 0, max(1, 128 // 4) + 1, jnp.int32)
        _ctx_2048P = jax.random.normal(jax.random.fold_in(_rk, 11), (16, 16, 256), jnp.float32)
        _ctx_2048c = jax.random.dirichlet(jax.random.fold_in(_rk, 511), 0.3 * jnp.ones((16,), jnp.float32), (16, 128))
        _ctx_2048t = jnp.einsum('bsk,bkd->bsd', _ctx_2048c, _ctx_2048P)
        _ctx_2048t = _ctx_2048t * jax.lax.rsqrt(jnp.mean(jnp.square(_ctx_2048t)) + 1e-12) * 0.953939
        ctx_2048 = -1.47943e-05 + 1.00017 * (_ctx_2048t + 0.3 * jax.random.normal(jax.random.fold_in(_rk, 611), (16, 128, 256), jnp.float32))
        return (x, ctx_2048)
    x, ctx_2048 = _rec_inputs()

    def _L0_attn_setup():
        import jax, jax.numpy as jnp
        import numpy as np
        BLOCK = 32
        NUM_HEADS = 16
        HEAD_DIM = 128
        FP4_GRID = jnp.array([0.0, 0.5, 1.0, 1.5, 2.0, 3.0, 4.0, 6.0], dtype=jnp.float32)

        def quantize_to_mxfp4(w, block_size=BLOCK):
            D, F = w.shape
            blocks = w.reshape(D // block_size, block_size, F)
            amax = jnp.max(jnp.abs(blocks), axis=1)
            e = jnp.floor(jnp.log2(jnp.maximum(amax, 1e-12) / 6.0))
            scale = jnp.exp2(e)
            v = blocks / scale[:, None, :]
            idx = jnp.argmin(jnp.abs(jnp.abs(v)[..., None] - FP4_GRID), axis=-1)
            codes = jnp.sign(v) * FP4_GRID[idx]
            return (codes.reshape(D, F).astype(jnp.float32), scale.astype(jnp.float32))

        def _mxfp4_matmul(x, codes, scales, block_size=BLOCK):
            w = codes * jnp.repeat(scales, block_size, axis=0)
            return x @ w
        key = jax.random.key(seed)
        ks = jax.random.split(key, 9)
        B, S, D = (2, 256, 256)
        feat = NUM_HEADS * HEAD_DIM
        x = jax.random.normal(ks[0], (B, S, D), dtype=jnp.float32)

        def make_w(k, din, dout):
            w = jax.random.normal(k, (din, dout), dtype=jnp.float32) * (1.0 / np.sqrt(din))
            return quantize_to_mxfp4(w, BLOCK)
        wq_codes, wq_scales = make_w(ks[1], D, feat)
        wk_codes, wk_scales = make_w(ks[2], D, feat)
        wv_codes, wv_scales = make_w(ks[3], D, feat)
        wo_codes, wo_scales = make_w(ks[4], feat, D)
        bq = jnp.zeros((feat,), jnp.float32)
        bk = jnp.zeros((feat,), jnp.float32)
        bv = jnp.zeros((feat,), jnp.float32)
        bo = jnp.zeros((D,), jnp.float32)
        return {'x': x, 'wq_codes': wq_codes, 'wq_scales': wq_scales, 'bq': bq, 'wk_codes': wk_codes, 'wk_scales': wk_scales, 'bk': bk, 'wv_codes': wv_codes, 'wv_scales': wv_scales, 'bv': bv, 'wo_codes': wo_codes, 'wo_scales': wo_scales, 'bo': bo}
    _L0_attn_all = _L0_attn_setup()
    _L0_attn_in = {k: v for k, v in _L0_attn_all.items() if k in ('wq_codes', 'wq_scales', 'bq', 'wk_codes', 'wk_scales', 'bk', 'wv_codes', 'wv_scales', 'bv', 'wo_codes', 'wo_scales', 'bo')}
    del _L0_attn_all

    def _L0_xattn_setup():
        import jax, jax.numpy as jnp
        import numpy as np

        def _wkv(time_decay, time_first, k, v):
            w = -jnp.exp(time_decay)
            u = time_first
            B, T, C = k.shape
            aa = jnp.zeros((B, C), dtype=k.dtype)
            bb = jnp.zeros((B, C), dtype=k.dtype)
            pp = jnp.full((B, C), -1e+38, dtype=k.dtype)

            def step(carry, kv_t):
                aa, bb, pp = carry
                kt, vt = kv_t
                ww = u + kt
                q = jnp.maximum(pp, ww)
                e1 = jnp.exp(pp - q)
                e2 = jnp.exp(ww - q)
                y_t = (e1 * aa + e2 * vt) / (e1 * bb + e2)
                ww2 = pp + w
                q2 = jnp.maximum(ww2, kt)
                e1b = jnp.exp(ww2 - q2)
                e2b = jnp.exp(kt - q2)
                new_carry = (e1b * aa + e2b * vt, e1b * bb + e2b, q2)
                return (new_carry, y_t)
            ks = jnp.transpose(k, (1, 0, 2))
            vs = jnp.transpose(v, (1, 0, 2))
            _, ys = jax.lax.scan(step, (aa, bb, pp), (ks, vs))
            return jnp.transpose(ys, (1, 0, 2))
        key = jax.random.key(seed)
        k1, k2, k3, k4 = jax.random.split(key, 4)
        B, T, C = (8, 128, 256)
        return {'batch_size': B, 'seq_len': T, 'embedding_dim': C, 'time_decay': jax.random.normal(k1, (C,), dtype=jnp.float32), 'time_first': jax.random.normal(k2, (C,), dtype=jnp.float32), 'k': jax.random.normal(k3, (B, T, C), dtype=jnp.float32), 'v': jax.random.normal(k4, (B, T, C), dtype=jnp.float32)}
    _L0_xattn_all = _L0_xattn_setup()
    _L0_xattn_in = {k: v for k, v in _L0_xattn_all.items() if k in ('time_decay', 'time_first')}
    del _L0_xattn_all

    def _L0_ffn_setup():
        import jax, jax.numpy as jnp
        import numpy as np
        EPS = 1e-05

        def rms_norm(x):
            return x * jax.lax.rsqrt(jnp.mean(x * x, axis=-1, keepdims=True) + EPS)

        def act_quant(x):
            scale = 127.0 / jnp.clip(jnp.max(jnp.abs(x), axis=-1, keepdims=True), 1e-05)
            q = jnp.clip(jnp.round(x * scale), -128.0, 127.0) / scale
            return x + jax.lax.stop_gradient(q - x)

        def weight_quant(w):
            scale = 1.0 / jnp.clip(jnp.mean(jnp.abs(w)), 1e-05)
            q = jnp.clip(jnp.round(w * scale), -1.0, 1.0) / scale
            return w + jax.lax.stop_gradient(q - w)

        def bitlinear158(x, w, b):
            xq = act_quant(rms_norm(x))
            wq = weight_quant(w)
            return jnp.einsum('bsd,od->bso', xq, wq) + b

        def layer_norm(x, g, b):
            mu = jnp.mean(x, axis=-1, keepdims=True)
            var = jnp.mean((x - mu) ** 2, axis=-1, keepdims=True)
            return (x - mu) * jax.lax.rsqrt(var + EPS) * g + b
        key = jax.random.key(seed)
        ks = jax.random.split(key, 3)
        d, inner = (256, 1024)
        x = jax.random.normal(ks[0], (4, 256, d), dtype=jnp.float32)
        w1 = jax.random.normal(ks[1], (inner, d), dtype=jnp.float32) * 0.02
        b1 = jnp.zeros((inner,), jnp.float32)
        ln_g = jnp.ones((inner,), jnp.float32)
        ln_b = jnp.zeros((inner,), jnp.float32)
        w2 = jax.random.normal(ks[2], (d, inner), dtype=jnp.float32) * 0.02
        b2 = jnp.zeros((d,), jnp.float32)
        return {'x': x, 'w1': w1, 'b1': b1, 'ln_g': ln_g, 'ln_b': ln_b, 'w2': w2, 'b2': b2}
    _L0_ffn_all = _L0_ffn_setup()
    _L0_ffn_in = {k: v for k, v in _L0_ffn_all.items() if k in ('w1', 'b1', 'ln_g', 'ln_b', 'w2', 'b2')}
    del _L0_ffn_all

    def _L1_attn_setup():
        import jax, jax.numpy as jnp
        import numpy as np
        from jax import lax
        D_MODEL, D_STATE, DT_RANK = (256, 16, 128)
        B_SZ, SEQLEN = (4, 256)

        def _s6_forward(hidden_states, x_proj_weight, dt_proj_weight, dt_proj_bias, A_log, D, out_proj_weight, out_proj_bias):
            b, L, d = hidden_states.shape
            W = x_proj_weight.T
            r = dt_proj_weight.shape[1]
            n = (W.shape[1] - r) // 2
            dt_down = W[:, :r]
            WB = W[:, r:r + n]
            WC = W[:, r + n:]
            Bm = jnp.einsum('bld,dn->bln', hidden_states, WB)
            Cm = jnp.einsum('bld,dn->bln', hidden_states, WC)
            dt_w = dt_proj_weight @ dt_down.T
            dt = jnp.einsum('bld,ed->ble', hidden_states, dt_w)
            A = -jnp.exp(A_log)
            delta = jax.nn.softplus(dt + dt_proj_bias)

            def step(h, inp):
                delta_t, B_t, C_t, x_t = inp
                dA = jnp.exp(delta_t[..., None] * A)
                h = h * dA + (delta_t * x_t)[..., None] * B_t[:, None, :]
                y_t = jnp.einsum('bdn,bn->bd', h, C_t)
                return (h, y_t)
            h0 = jnp.zeros((b, d, n), hidden_states.dtype)
            xs = (delta.transpose(1, 0, 2), Bm.transpose(1, 0, 2), Cm.transpose(1, 0, 2), hidden_states.transpose(1, 0, 2))
            _, ys = lax.scan(step, h0, xs)
            y = ys.transpose(1, 0, 2)
            out = jax.nn.relu(y @ out_proj_weight.T + out_proj_bias)
            out = out + D * hidden_states
            return out
        key = jax.random.key(seed)
        ks = jax.random.split(key, 8)
        dt_init_std = DT_RANK ** (-0.5)
        return {'hidden_states': jax.random.normal(ks[0], (B_SZ, SEQLEN, D_MODEL), jnp.float32), 'x_proj_weight': jax.random.normal(ks[1], (DT_RANK + 2 * D_STATE, D_MODEL), jnp.float32) * D_MODEL ** (-0.5), 'dt_proj_weight': jax.random.uniform(ks[2], (D_MODEL, DT_RANK), jnp.float32, -dt_init_std, dt_init_std), 'dt_proj_bias': jax.random.normal(ks[3], (D_MODEL,), jnp.float32) * 0.5 - 4.0, 'A_log': jnp.log(jax.random.uniform(ks[4], (D_MODEL, D_STATE), jnp.float32) * D_STATE + 1.0), 'D': jax.random.uniform(ks[5], (D_MODEL,), jnp.float32) * 0.8, 'out_proj_weight': jax.random.normal(ks[6], (D_MODEL, D_MODEL), jnp.float32) * D_MODEL ** (-0.5), 'out_proj_bias': jax.random.normal(ks[7], (D_MODEL,), jnp.float32) * 0.02}
    _L1_attn_all = _L1_attn_setup()
    _L1_attn_in = {k: v for k, v in _L1_attn_all.items() if k in ('x_proj_weight', 'dt_proj_weight', 'dt_proj_bias', 'A_log', 'D', 'out_proj_weight', 'out_proj_bias')}
    del _L1_attn_all

    def _L1_xattn_setup():
        import jax, jax.numpy as jnp
        import numpy as np
        key = jax.random.key(seed)
        k1, k2, k3, k4, k5 = jax.random.split(key, 5)
        B, D_MODEL, L = (2, 128, 256)
        HEAD_DIM = 8
        H = D_MODEL // HEAD_DIM
        return {'k': jax.random.normal(k1, (B, D_MODEL, L), dtype=jnp.float32), 'v': jax.random.normal(k2, (B, D_MODEL, L), dtype=jnp.float32), 'q': jax.random.normal(k3, (B, D_MODEL, L), dtype=jnp.float32), 'ssm_kernel': jax.random.normal(k4, (H, L), dtype=jnp.float32), 'D': jax.random.normal(k5, (H,), dtype=jnp.float32), 'head_dim': HEAD_DIM}
    _L1_xattn_all = _L1_xattn_setup()
    _L1_xattn_in = {k: v for k, v in _L1_xattn_all.items() if k in ('ssm_kernel', 'D')}
    del _L1_xattn_all

    def _L1_ffn_setup():
        import jax, jax.numpy as jnp
        import numpy as np
        H = 256
        E = 16
        K = 4
        I = 176
        IS = 176 * 2
        B, S = (1, 128)
        key = jax.random.key(seed)
        ks = jax.random.split(key, 9)
        scale = 0.02
        return {'hidden_states': jax.random.normal(ks[0], (B, S, H), dtype=jnp.float32), 'gate_w': jax.random.normal(ks[1], (E, H), dtype=jnp.float32) * scale, 'w_gate': jax.random.normal(ks[2], (E, H, I), dtype=jnp.float32) * scale, 'w_up': jax.random.normal(ks[3], (E, H, I), dtype=jnp.float32) * scale, 'w_down': jax.random.normal(ks[4], (E, I, H), dtype=jnp.float32) * scale, 'sw_gate': jax.random.normal(ks[5], (H, IS), dtype=jnp.float32) * scale, 'sw_up': jax.random.normal(ks[6], (H, IS), dtype=jnp.float32) * scale, 'sw_down': jax.random.normal(ks[7], (IS, H), dtype=jnp.float32) * scale}
    _L1_ffn_all = _L1_ffn_setup()
    _L1_ffn_in = {k: v for k, v in _L1_ffn_all.items() if k in ('gate_w', 'w_gate', 'w_up', 'w_down', 'sw_gate', 'sw_up', 'sw_down')}
    del _L1_ffn_all
    return {'x': x, 'ctx_2048': ctx_2048, 'L0_attn_wq_codes': _L0_attn_in['wq_codes'], 'L0_attn_wq_scales': _L0_attn_in['wq_scales'], 'L0_attn_bq': _L0_attn_in['bq'], 'L0_attn_wk_codes': _L0_attn_in['wk_codes'], 'L0_attn_wk_scales': _L0_attn_in['wk_scales'], 'L0_attn_bk': _L0_attn_in['bk'], 'L0_attn_wv_codes': _L0_attn_in['wv_codes'], 'L0_attn_wv_scales': _L0_attn_in['wv_scales'], 'L0_attn_bv': _L0_attn_in['bv'], 'L0_attn_wo_codes': _L0_attn_in['wo_codes'], 'L0_attn_wo_scales': _L0_attn_in['wo_scales'], 'L0_attn_bo': _L0_attn_in['bo'], 'L0_xattn_time_decay': _L0_xattn_in['time_decay'], 'L0_xattn_time_first': _L0_xattn_in['time_first'], 'L0_ffn_w1': _L0_ffn_in['w1'], 'L0_ffn_b1': _L0_ffn_in['b1'], 'L0_ffn_ln_g': _L0_ffn_in['ln_g'], 'L0_ffn_ln_b': _L0_ffn_in['ln_b'], 'L0_ffn_w2': _L0_ffn_in['w2'], 'L0_ffn_b2': _L0_ffn_in['b2'], 'L1_attn_x_proj_weight': _L1_attn_in['x_proj_weight'], 'L1_attn_dt_proj_weight': _L1_attn_in['dt_proj_weight'], 'L1_attn_dt_proj_bias': _L1_attn_in['dt_proj_bias'], 'L1_attn_A_log': _L1_attn_in['A_log'], 'L1_attn_D': _L1_attn_in['D'], 'L1_attn_out_proj_weight': _L1_attn_in['out_proj_weight'], 'L1_attn_out_proj_bias': _L1_attn_in['out_proj_bias'], 'L1_xattn_ssm_kernel': _L1_xattn_in['ssm_kernel'], 'L1_xattn_D': _L1_xattn_in['D'], 'L1_ffn_gate_w': _L1_ffn_in['gate_w'], 'L1_ffn_w_gate': _L1_ffn_in['w_gate'], 'L1_ffn_w_up': _L1_ffn_in['w_up'], 'L1_ffn_w_down': _L1_ffn_in['w_down'], 'L1_ffn_sw_gate': _L1_ffn_in['sw_gate'], 'L1_ffn_sw_up': _L1_ffn_in['sw_up'], 'L1_ffn_sw_down': _L1_ffn_in['sw_down']}

def reference(x, ctx_2048, L0_attn_wq_codes, L0_attn_wq_scales, L0_attn_bq, L0_attn_wk_codes, L0_attn_wk_scales, L0_attn_bk, L0_attn_wv_codes, L0_attn_wv_scales, L0_attn_bv, L0_attn_wo_codes, L0_attn_wo_scales, L0_attn_bo, L0_xattn_time_decay, L0_xattn_time_first, L0_ffn_w1, L0_ffn_b1, L0_ffn_ln_g, L0_ffn_ln_b, L0_ffn_w2, L0_ffn_b2, L1_attn_x_proj_weight, L1_attn_dt_proj_weight, L1_attn_dt_proj_bias, L1_attn_A_log, L1_attn_D, L1_attn_out_proj_weight, L1_attn_out_proj_bias, L1_xattn_ssm_kernel, L1_xattn_D, L1_ffn_gate_w, L1_ffn_w_gate, L1_ffn_w_up, L1_ffn_w_down, L1_ffn_sw_gate, L1_ffn_sw_up, L1_ffn_sw_down):
    import jax
    import jax.numpy as jnp

    def _L0_attn_ref(x, wq_codes, wq_scales, bq, wk_codes, wk_scales, bk, wv_codes, wv_scales, bv, wo_codes, wo_scales, bo):
        import jax, jax.numpy as jnp
        import numpy as np
        BLOCK = 32
        NUM_HEADS = 16
        HEAD_DIM = 128
        FP4_GRID = jnp.array([0.0, 0.5, 1.0, 1.5, 2.0, 3.0, 4.0, 6.0], dtype=jnp.float32)

        def quantize_to_mxfp4(w, block_size=BLOCK):
            D, F = w.shape
            blocks = w.reshape(D // block_size, block_size, F)
            amax = jnp.max(jnp.abs(blocks), axis=1)
            e = jnp.floor(jnp.log2(jnp.maximum(amax, 1e-12) / 6.0))
            scale = jnp.exp2(e)
            v = blocks / scale[:, None, :]
            idx = jnp.argmin(jnp.abs(jnp.abs(v)[..., None] - FP4_GRID), axis=-1)
            codes = jnp.sign(v) * FP4_GRID[idx]
            return (codes.reshape(D, F).astype(jnp.float32), scale.astype(jnp.float32))

        def _mxfp4_matmul(x, codes, scales, block_size=BLOCK):
            w = codes * jnp.repeat(scales, block_size, axis=0)
            return x @ w
        B, S, D = x.shape
        q = _mxfp4_matmul(x, wq_codes, wq_scales) + bq
        k = _mxfp4_matmul(x, wk_codes, wk_scales) + bk
        v = _mxfp4_matmul(x, wv_codes, wv_scales) + bv
        q = q.reshape(B, S, NUM_HEADS, HEAD_DIM)
        k = k.reshape(B, S, NUM_HEADS, HEAD_DIM)
        v = v.reshape(B, S, NUM_HEADS, HEAD_DIM)
        scores = jnp.einsum('bqhd,bkhd->bhqk', q, k) / jnp.sqrt(jnp.float32(HEAD_DIM))
        attn = jax.nn.softmax(scores, axis=-1)
        out = jnp.einsum('bhqk,bkhd->bqhd', attn, v).reshape(B, S, NUM_HEADS * HEAD_DIM)
        return _mxfp4_matmul(out, wo_codes, wo_scales) + bo

    def _L0_xattn_ref(batch_size, seq_len, embedding_dim, time_decay, time_first, k, v):
        import jax, jax.numpy as jnp
        import numpy as np

        def _wkv(time_decay, time_first, k, v):
            w = -jnp.exp(time_decay)
            u = time_first
            B, T, C = k.shape
            aa = jnp.zeros((B, C), dtype=k.dtype)
            bb = jnp.zeros((B, C), dtype=k.dtype)
            pp = jnp.full((B, C), -1e+38, dtype=k.dtype)

            def step(carry, kv_t):
                aa, bb, pp = carry
                kt, vt = kv_t
                ww = u + kt
                q = jnp.maximum(pp, ww)
                e1 = jnp.exp(pp - q)
                e2 = jnp.exp(ww - q)
                y_t = (e1 * aa + e2 * vt) / (e1 * bb + e2)
                ww2 = pp + w
                q2 = jnp.maximum(ww2, kt)
                e1b = jnp.exp(ww2 - q2)
                e2b = jnp.exp(kt - q2)
                new_carry = (e1b * aa + e2b * vt, e1b * bb + e2b, q2)
                return (new_carry, y_t)
            ks = jnp.transpose(k, (1, 0, 2))
            vs = jnp.transpose(v, (1, 0, 2))
            _, ys = jax.lax.scan(step, (aa, bb, pp), (ks, vs))
            return jnp.transpose(ys, (1, 0, 2))
        assert seq_len <= 128
        return _wkv(time_decay, time_first, k, v)

    def _L0_ffn_ref(x, w1, b1, ln_g, ln_b, w2, b2):
        import jax, jax.numpy as jnp
        import numpy as np
        EPS = 1e-05

        def rms_norm(x):
            return x * jax.lax.rsqrt(jnp.mean(x * x, axis=-1, keepdims=True) + EPS)

        def act_quant(x):
            scale = 127.0 / jnp.clip(jnp.max(jnp.abs(x), axis=-1, keepdims=True), 1e-05)
            q = jnp.clip(jnp.round(x * scale), -128.0, 127.0) / scale
            return x + jax.lax.stop_gradient(q - x)

        def weight_quant(w):
            scale = 1.0 / jnp.clip(jnp.mean(jnp.abs(w)), 1e-05)
            q = jnp.clip(jnp.round(w * scale), -1.0, 1.0) / scale
            return w + jax.lax.stop_gradient(q - w)

        def bitlinear158(x, w, b):
            xq = act_quant(rms_norm(x))
            wq = weight_quant(w)
            return jnp.einsum('bsd,od->bso', xq, wq) + b

        def layer_norm(x, g, b):
            mu = jnp.mean(x, axis=-1, keepdims=True)
            var = jnp.mean((x - mu) ** 2, axis=-1, keepdims=True)
            return (x - mu) * jax.lax.rsqrt(var + EPS) * g + b
        h = jax.nn.silu(bitlinear158(x, w1, b1))
        h = jax.nn.gelu(h, approximate=False)
        h = layer_norm(h, ln_g, ln_b)
        return bitlinear158(h, w2, b2)

    def _L1_attn_ref(hidden_states, x_proj_weight, dt_proj_weight, dt_proj_bias, A_log, D, out_proj_weight, out_proj_bias):
        import jax, jax.numpy as jnp
        import numpy as np
        from jax import lax
        D_MODEL, D_STATE, DT_RANK = (256, 16, 128)
        B_SZ, SEQLEN = (4, 256)

        def _s6_forward(hidden_states, x_proj_weight, dt_proj_weight, dt_proj_bias, A_log, D, out_proj_weight, out_proj_bias):
            b, L, d = hidden_states.shape
            W = x_proj_weight.T
            r = dt_proj_weight.shape[1]
            n = (W.shape[1] - r) // 2
            dt_down = W[:, :r]
            WB = W[:, r:r + n]
            WC = W[:, r + n:]
            Bm = jnp.einsum('bld,dn->bln', hidden_states, WB)
            Cm = jnp.einsum('bld,dn->bln', hidden_states, WC)
            dt_w = dt_proj_weight @ dt_down.T
            dt = jnp.einsum('bld,ed->ble', hidden_states, dt_w)
            A = -jnp.exp(A_log)
            delta = jax.nn.softplus(dt + dt_proj_bias)

            def step(h, inp):
                delta_t, B_t, C_t, x_t = inp
                dA = jnp.exp(delta_t[..., None] * A)
                h = h * dA + (delta_t * x_t)[..., None] * B_t[:, None, :]
                y_t = jnp.einsum('bdn,bn->bd', h, C_t)
                return (h, y_t)
            h0 = jnp.zeros((b, d, n), hidden_states.dtype)
            xs = (delta.transpose(1, 0, 2), Bm.transpose(1, 0, 2), Cm.transpose(1, 0, 2), hidden_states.transpose(1, 0, 2))
            _, ys = lax.scan(step, h0, xs)
            y = ys.transpose(1, 0, 2)
            out = jax.nn.relu(y @ out_proj_weight.T + out_proj_bias)
            out = out + D * hidden_states
            return out
        return _s6_forward(hidden_states, x_proj_weight, dt_proj_weight, dt_proj_bias, A_log, D, out_proj_weight, out_proj_bias)

    def _L1_xattn_ref(k, v, q, ssm_kernel, D, head_dim):
        import jax, jax.numpy as jnp
        import numpy as np
        B, HD, L = k.shape
        H = HD // head_dim
        fft_size = 2 * L
        k_ = k.reshape(B, H, head_dim, L)
        v_ = v.reshape(B, H, head_dim, L)
        q_ = q.reshape(B, H, head_dim, L)
        kv = jnp.einsum('bhil,bhjl->bijhl', k_, v_)
        kv_f = jnp.fft.rfft(kv, n=fft_size)
        kernel_f = jnp.fft.rfft(ssm_kernel, n=fft_size)
        y = jnp.fft.irfft(kv_f * kernel_f, n=fft_size)[..., :L]
        out = y + kv * D[None, None, None, :, None]
        out = jnp.einsum('bijhl,bhil->bjhl', out, q_)
        out = jnp.transpose(out, (0, 2, 1, 3)).reshape(B, H * head_dim, L)
        return out.astype(k.dtype)

    def _L1_ffn_ref(hidden_states, gate_w, w_gate, w_up, w_down, sw_gate, sw_up, sw_down):
        import jax, jax.numpy as jnp
        import numpy as np
        H = 256
        E = 16
        K = 4
        I = 176
        IS = 176 * 2
        B, S = (1, 128)
        orig_shape = hidden_states.shape
        x = hidden_states.reshape(-1, H)
        T = x.shape[0]
        logits = jnp.einsum('th,eh->te', x, gate_w)
        scores = jax.nn.softmax(logits, axis=-1)
        topk_w, topk_idx = jax.lax.top_k(scores, K)
        topk_w = topk_w / jnp.sum(topk_w, axis=-1, keepdims=True)
        combine = jnp.zeros((T, E), dtype=x.dtype)
        combine = combine.at[jnp.arange(T)[:, None], topk_idx].add(topk_w)
        g = jnp.einsum('th,ehi->tei', x, w_gate)
        u = jnp.einsum('th,ehi->tei', x, w_up)
        a = jax.nn.silu(g) * u
        a = a * combine[:, :, None]
        y = jnp.einsum('tei,eih->th', a, w_down)
        sg = x @ sw_gate
        su = x @ sw_up
        y = y + jax.nn.silu(sg) * su @ sw_down
        return y.reshape(orig_shape)
    x = x + _L0_attn_ref(_layernorm(x, axis=-1), L0_attn_wq_codes, L0_attn_wq_scales, L0_attn_bq, L0_attn_wk_codes, L0_attn_wk_scales, L0_attn_bk, L0_attn_wv_codes, L0_attn_wv_scales, L0_attn_bv, L0_attn_wo_codes, L0_attn_wo_scales, L0_attn_bo)
    x = x + _L0_xattn_ref(16, 128, 256, L0_xattn_time_decay, L0_xattn_time_first, _layernorm(x, axis=-1), ctx_2048)
    x = x + _L0_ffn_ref(_layernorm(x, axis=-1), L0_ffn_w1, L0_ffn_b1, L0_ffn_ln_g, L0_ffn_ln_b, L0_ffn_w2, L0_ffn_b2)
    x = x + _L1_attn_ref(_layernorm(x, axis=-1), L1_attn_x_proj_weight, L1_attn_dt_proj_weight, L1_attn_dt_proj_bias, L1_attn_A_log, L1_attn_D, L1_attn_out_proj_weight, L1_attn_out_proj_bias)
    x = x + _L1_xattn_ref(ctx_2048, ctx_2048, _layernorm(x, axis=-1), L1_xattn_ssm_kernel, L1_xattn_D, 8)
    x = x + _L1_ffn_ref(_layernorm(x, axis=-1), L1_ffn_gate_w, L1_ffn_w_gate, L1_ffn_w_up, L1_ffn_w_down, L1_ffn_sw_gate, L1_ffn_sw_up, L1_ffn_sw_down)
    return x

_drawn_inputs = setup_inputs


def setup_inputs(seed=0):
    import zlib

    import numpy as np

    out = dict(_drawn_inputs(seed))
    spreads = {'L0_attn_bq': (0.0, 0.677),
     'L0_attn_bk': (0.0, 0.8),
     'L0_attn_bv': (0.0, 0.1),
     'L0_attn_bo': (0.0, 0.1),
     'L0_ffn_b1': (0.0, 0.1),
     'L0_ffn_ln_g': (1.0, 0.2),
     'L0_ffn_ln_b': (0.0, 0.1),
     'L0_ffn_b2': (0.0, 0.1)}
    factors = {'L0_attn_wq_scales': 3.542,
     'L0_attn_wk_scales': 3.51,
     'L1_attn_out_proj_bias': 5.939,
     'L1_ffn_gate_w': 8.0,
     'L1_ffn_w_gate': 8.0,
     'L1_ffn_w_up': 8.0,
     'L1_ffn_w_down': 8.0,
     'L1_ffn_sw_gate': 8.0,
     'L1_ffn_sw_up': 8.0,
     'L1_ffn_sw_down': 8.0}
    for name, (base, spread) in spreads.items():
        noise = np.random.default_rng([zlib.crc32(name.encode()), seed]).standard_normal(out[name].shape)
        drawn = base * np.exp(spread * noise) if base else spread * noise
        out[name] = jnp.asarray(drawn.astype(out[name].dtype))
    for name, factor in factors.items():
        out[name] = (out[name] * factor).astype(out[name].dtype)
    return out
```

```python
import concourse.bass as bass
from concourse import mybir
from contextlib import ExitStack

F32 = mybir.dt.float32
F32R = mybir.dt.float32r
BF16 = mybir.dt.bfloat16
ALU = mybir.AluOpType
ACT = mybir.ActivationFunctionType
AX = mybir.AxisListType

NB, T, D = 16, 128, 256
P = 128
CH = D // P
NG = 4
GB = NB // NG
GT = GB * T
EPS = 1e-5
ROUND = 1.5 * 2.0 ** 23
FAR = -1e38


def wait(eng, sem, value):
    if not (isinstance(value, int) and value <= 0):
        eng.wait_ge(sem, value)


class Chain:

    def __init__(self, eng, sem):
        self.eng, self.sem, self.n = eng, sem, 0

    def __call__(self, instruction):
        self.n += 1
        instruction.then_inc(self.sem, 1)
        self.eng.wait_ge(self.sem, self.n)


class Space:

    def __init__(self, nc, ctx, stage):
        self.nc, self.ctx, self.stage, self.sems = nc, ctx, stage, []
        ctx.callback(self.clear)

    def sb(self, name, shape, dt=F32):
        return self.ctx.enter_context(self.nc.sbuf_tensor(f"{self.stage}_{name}", shape, dt))

    def ps(self, name, shape, dt=F32):
        return self.ctx.enter_context(self.nc.psum_tensor(f"{self.stage}_{name}", shape, dt))

    def sem(self, name):
        self.sems.append(self.nc.alloc_semaphore(f"{self.stage}_{name}"))
        return self.sems[-1]

    def clear(self):
        if self.sems:
            self.nc.clear_and_free_semaphores(self.sems)
            self.nc.all_engine_barrier()


def stage_load(nc, x, ctx_in, X, CT, ident, identb, anti, eps, ones):
    with ExitStack() as ctx:
        s = Space(nc, ctx, "load")
        C = s.sb("ctx", [P, NB, D])
        bank = [s.ps(f"bank{k}", [P, GB, CH, T]) for k in range(2)]
        x_in, c_in, made, turned, kept = (s.sem(n) for n in ("x_in", "c_in", "made", "turned", "kept"))
        with nc.Block() as block:

            @block.sync
            def _(sp):
                sp.dma_start(C[:, :, :], ctx_in.rearrange("b s d -> s b d")).then_inc(c_in, 16)
                sp.dma_start(X[:, :, :], x.rearrange("b s d -> s b d")).then_inc(x_in, 16)
                sp.wait_ge(x_in, 16)

            @block.gpsimd
            def _(pool):
                pool.memset(ident[:, :], 0.0).then_inc(made, 1)
                pool.memset(anti[:, :], 0.0).then_inc(made, 1)
                pool.memset(eps[:, :], EPS)
                pool.memset(ones[:, :], 1.0)
                pool.wait_ge(made, 2)
                pool.affine_select(out=ident[:, :], in_=ident[:, :], compare_op=ALU.not_equal, fill=1.0,
                                   base=0, pattern=[[-1, P]], channel_multiplier=1).then_inc(made, 1)
                pool.affine_select(out=anti[:, :], in_=anti[:, :], compare_op=ALU.not_equal, fill=1.0,
                                   base=1 - P, pattern=[[1, P]], channel_multiplier=1).then_inc(made, 1)

            @block.tensor
            def _(pe):
                pe.wait_ge(c_in, 16)
                pe.wait_ge(made, 4)
                for g in range(NG):
                    wait(pe, kept, g - 1)
                    for b in range(GB):
                        for c in range(CH):
                            last = nc.tensor.transpose(bank[g % 2][:, b, c, :], C[:, GB * g + b, c * P:(c + 1) * P],
                                                       ident[:, :])
                    last.then_inc(turned, 1)

            @block.vector
            def _(dve):
                dve.wait_ge(made, 4)
                nc.vector.tensor_copy(identb[:, :], ident[:, :])

            @block.scalar
            def _(act):
                for g in range(NG):
                    act.wait_ge(turned, g + 1)
                    nc.scalar.activation(CT[:, :, GB * g:GB * g + GB, :],
                                         bank[g % 2][:, :, :, :].rearrange("p b c t -> p c b t"),
                                         ACT.Copy).then_inc(kept, 1)


def stage_renorm(nc, name, X, ident, eps, YT=None, XT=None, XH=None, XL=None, out=None, ahead=()):
    with ExitStack() as ctx:
        s = Space(nc, ctx, name)
        norm = XT is not None or XH is not None
        back = [s.ps(f"back{k}", [P, GB, D]) for k in range(2)]
        fore = [s.ps(f"fore{k}", [P, GB, CH, T]) for k in range(2)]
        xn = s.sb("xn", [P, 2, GB, D])
        st = s.sb("st", [P, NB, 6])
        mv = s.sb("mv", [P, NB, 2])
        sd = s.sb("sd", [P, NB])
        (y_turned, added, stats, aggregated, rooted, inverted, normed, n_turned, head_kept, rest_kept, stored) = (
            s.sem(n) for n in ("y_turned", "added", "stats", "aggregated", "rooted", "inverted", "normed",
                               "n_turned", "head_kept", "rest_kept", "stored"))
        with nc.Block() as block:

            @block.sync
            def _(sp):
                for first in ahead[0:1]:
                    first(sp)
                if out is not None:
                    for g in range(NG):
                        sp.wait_ge(added, g + 1)
                        sp.dma_start(out[GB * g:GB * g + GB].rearrange("b s d -> s b d"),
                                     X[:, GB * g:GB * g + GB, :]).then_inc(stored, 16)
                    sp.wait_ge(stored, 16 * NG)

            @block.gpsimd
            def _(pool):
                for first in ahead[1:2]:
                    first(pool)

            @block.tensor
            def _(pe):
                for g in range(NG + 1):
                    if g < NG and YT is not None:
                        wait(pe, added, g - 1)
                        for b in range(GB):
                            for c in range(CH):
                                last = nc.tensor.transpose(back[g % 2][:, b, c * P:(c + 1) * P],
                                                           YT[:, c, GB * g + b, :], ident[:, :])
                        last.then_inc(y_turned, 1)
                    if g and norm:
                        pe.wait_ge(normed, g)
                        wait(pe, head_kept, g - 2)
                        wait(pe, rest_kept, g - 2 if XL is not None else 0)
                        for b in range(GB):
                            for c in range(CH):
                                last = nc.tensor.transpose(fore[(g - 1) % 2][:, b, c, :],
                                                           xn[:, (g - 1) % 2, b, c * P:(c + 1) * P], ident[:, :])
                        last.then_inc(n_turned, 1)

            @block.vector
            def _(dve):
                for g in range(NG + 2):
                    part = slice(GB * g, GB * g + GB)
                    if g < NG:
                        if YT is not None:
                            dve.wait_ge(y_turned, g + 1)
                            nc.vector.tensor_tensor(X[:, part, :], X[:, part, :], back[g % 2][:, :, :],
                                                    ALU.add).then_inc(added, 1)
                            dve.wait_ge(added, g + 1)
                        if norm:
                            for b in range(GB * g, GB * g + GB):
                                nc.vector.bn_stats(st[:, b, :], X[:, b, :]).then_inc(stats, 1)
                            dve.wait_ge(stats, GB * (g + 1))
                            for b in range(GB * g, GB * g + GB):
                                nc.vector.bn_aggr(mv[:, b, :], st[:, b, :]).then_inc(aggregated, 1)
                    if norm and 1 <= g <= NG:
                        h = g - 1
                        dve.wait_ge(rooted, h + 1)
                        nc.vector.reciprocal(sd[:, GB * h:GB * g], sd[:, GB * h:GB * g]).then_inc(inverted, 1)
                        dve.wait_ge(inverted, h + 1)
                        wait(dve, n_turned, h - 1)
                        for b in range(GB):
                            t = GB * h + b
                            last = nc.vector.tensor_scalar(xn[:, h % 2, b, :], X[:, t, :], mv[:, t, 0:1],
                                                           sd[:, t:t + 1], ALU.subtract, ALU.mult)
                        last.then_inc(normed, 1)
                    if XL is not None and g >= 2:
                        h = g - 2
                        dve.wait_ge(head_kept, h + 1)
                        nc.vector.tensor_tensor(
                            XL[:, :, GB * h:GB * h + GB, :], fore[h % 2][:, :, :, :].rearrange("p b c t -> p c b t"),
                            XH[:, :, GB * h:GB * h + GB, :].bitcast(F32), ALU.subtract).then_inc(rest_kept, 1)

            @block.scalar
            def _(act):
                if norm:
                    for g in range(NG + 1):
                        if g < NG:
                            act.wait_ge(aggregated, GB * (g + 1))
                            nc.scalar.activation(sd[:, GB * g:GB * g + GB], mv[:, GB * g:GB * g + GB, 1], ACT.Sqrt,
                                                 bias=eps[:, :]).then_inc(rooted, 1)
                        if g:
                            h = g - 1
                            act.wait_ge(n_turned, g)
                            to = XT if XH is None else XH
                            nc.scalar.activation(to[:, :, GB * h:GB * h + GB, :],
                                                 fore[h % 2][:, :, :, :].rearrange("p b c t -> p c b t"),
                                                 ACT.Copy).then_inc(head_kept, 1)


def stage_store(nc, X, out):
    with ExitStack() as ctx:
        stored = Space(nc, ctx, "store").sem("stored")
        with nc.Block() as block:

            @block.sync
            def _(sp):
                sp.dma_start(out.rearrange("b s d -> s b d"), X[:, :, :]).then_inc(stored, 16)
                sp.wait_ge(stored, 16)


def stage_attention(nc, codes_q, scales_q, bq, codes_k, scales_k, bk, codes_v, scales_v, bv, codes_o, scales_o, bo,
                    XH, XL, YT, ident, before):
    HEADS, DH, BLOCK = 16, 128, 32
    PAIRS, UNITS = HEADS // 2, 2 * NG
    KB = P // BLOCK
    PIECES, PW = 8, 2 * DH
    SCALE = float(DH) ** -0.5
    LAST = PAIRS * UNITS
    with ExitStack() as ctx:
        s = Space(nc, ctx, "attn")
        codes = s.sb("codes", [P, 2, PIECES, PW])
        scales = s.sb("scales", [P, 2, PIECES, PW])
        WH = s.sb("weight_head", [P, 2, PIECES, PW], F32R)
        WL = s.sb("weight_rest", [P, 2, PIECES, PW], F32R)
        bq_sb, bk_sb, bo_sb = s.sb("bq", [P, HEADS]), s.sb("bk", [P, HEADS]), s.sb("bo", [P, CH])
        bq_pair = s.sb("bq_pair", [P, 2, 2])
        bv_sb = s.sb("bv", [P, HEADS * DH])
        QT, KT, PR, PT = (s.sb(n, [P, 2, GB, T]) for n in ("queries", "keys", "probs", "probs_turned"))
        V = s.sb("values", [P, 2, GB, 2, DH])
        OH, OL = s.sb("heads_head", [P, 2, GT], F32R), s.sb("heads_rest", [P, 2, GT], F32R)
        NM, SM, RS = (s.sb(n, [P, 2, GB]) for n in ("neg_max", "sums", "inverse_sums"))
        (bias_in, biases_set, weight_whole, weight_head, weight_rest,
         v_made, q_made, k_made, s_made, t_made, o_made, out_made,
         v_kept, q_kept, k_kept, t_kept, oh_kept, ol_kept, y_kept,
         max_made, exp_made, inverse_made, probs_made) = (s.sem(n) for n in (
             "bias_in", "biases_set", "weight_whole", "weight_head", "weight_rest",
             "v_made", "q_made", "k_made", "s_made", "t_made", "o_made", "out_made",
             "v_kept", "q_kept", "k_kept", "t_kept", "oh_kept", "ol_kept", "y_kept",
             "max_made", "exp_made", "inverse_made", "probs_made"))
        bq_picked = s.sem("bq_picked")
        codes_in = [s.sem(f"codes_in{w}") for w in range(2)]

        def over_pairs(eng, body):
            body(0, 0)
            body(1, 1)
            with eng.Fori(1, PAIRS // 2) as i:
                body(2 * i, 0)
                body(2 * i + 1, 1)

        DMAS = 4 + 4 * KB
        def load(sp, pair, w):
            wait(sp, weight_rest, (pair - 1) * PIECES)
            cols = bass.ds(pair * PW, PW)
            for m, (code, scale) in enumerate(((codes_q, scales_q), (codes_k, scales_k), (codes_v, scales_v))):
                sp.dma_start(codes[:, w, 2 * m:2 * m + 2, :],
                             code.rearrange("(c p) f -> p c f", p=P)[:, :, cols]).then_inc(codes_in[w], 16)
                for k in range(KB):
                    sp.dma_start(scales[BLOCK * k:BLOCK * (k + 1), w, 2 * m:2 * m + 2, :],
                                 scale.rearrange("(c k) f -> k c f", k=KB)[k, :, cols]
                                 .partition_broadcast(BLOCK)).then_inc(codes_in[w], 16)
            sp.dma_start(codes[:, w, 6:8, :],
                         codes_o.rearrange("(a j p) f -> a p j f", j=2, p=P)[pair]).then_inc(codes_in[w], 16)
            for k in range(KB):
                sp.dma_start(scales[BLOCK * k:BLOCK * (k + 1), w, 6:8, :],
                             scales_o.rearrange("(a j k) f -> a k j f", j=2, k=KB)[pair, k]
                             .partition_broadcast(BLOCK)).then_inc(codes_in[w], 16)

        def whole(pool, pair, w, k):
            if k == 0:
                pool.wait_ge(codes_in[w], 8 * DMAS * (pair + 2 - w))
            nc.gpsimd.tensor_tensor(codes[:, w, k, :], codes[:, w, k, :], scales[:, w, k, :],
                                    ALU.mult).then_inc(weight_whole, 1)

        def rest(pool, pair, w, k):
            pool.wait_ge(weight_head, pair * PIECES + k + 1)
            nc.gpsimd.tensor_tensor(WL[:, w, k, :], codes[:, w, k, :], WH[:, w, k, :].bitcast(F32),
                                    ALU.subtract).then_inc(weight_rest, 1)

        def pieces(u):
            return ((0,), (1, 2), *((k,) for k in range(3, PIECES)), ())[u]

        def ahead_sync(sp):
            load(sp, 0, 0)
            sp.dma_start(bq_sb[:, :], bq).then_inc(bias_in, 16)
            sp.dma_start(bk_sb[:, :], bk).then_inc(bias_in, 16)
            sp.dma_start(bo_sb[:, :], bo).then_inc(bias_in, 16)
            sp.dma_start(bv_sb[:, :], bv.partition_broadcast(P)).then_inc(bias_in, 16)

        def ahead_pool(pool):
            for k in range(PIECES):
                whole(pool, 0, 0, k)
            for k in range(PIECES):
                pool.wait_ge(weight_whole, k + 1)
                nc.gpsimd.tensor_copy(WH[:, 0, k, :], codes[:, 0, k, :]).then_inc(weight_head, 1)
            for k in range(PIECES):
                rest(pool, 0, 0, k)

        before((ahead_sync, ahead_pool))
        q_bank, k_bank, v_bank, s_bank, t_bank, o_bank = (
            s.ps(n, [P, GT]) for n in ("q_bank", "k_bank", "v_bank", "s_bank", "t_bank", "o_bank"))
        y_bank = s.ps("y_bank", [P, CH, GT])

        with nc.Block() as block:

            @block.sync
            def _(sp):
                load(sp, 1, 1)
                with sp.Fori(1, PAIRS // 2) as i:
                    load(sp, 2 * i, 0)
                    load(sp, 2 * i + 1, 1)

            @block.gpsimd
            def _(pool):
                def body(pair, w, more=True):
                    for u in range(UNITS):
                        n, j = pair * UNITS + u, u % 2
                        if more:
                            for k in pieces(u):
                                whole(pool, pair + 1, 1 - w, k)
                        pool.wait_ge(inverse_made, n + 1)
                        nc.gpsimd.tensor_tensor(PR[:, j, :, :], PR[:, j, :, :],
                                                RS[:, j, :].unsqueeze(2).to_broadcast([P, GB, T]),
                                                ALU.mult).then_inc(probs_made, 1)
                        if more:
                            for k in pieces(u):
                                rest(pool, pair + 1, 1 - w, k)

                body(0, 0)
                with pool.Fori(0, PAIRS // 2 - 1) as i:
                    body(2 * i + 1, 1)
                    body(2 * i + 2, 0)
                body(PAIRS - 1, 1, more=False)

            @block.tensor
            def _(pe):
                def product(out, a_head, a_rest, b_head, b_rest, first, last):
                    nc.tensor.matmul(out, a_head, b_head, start=first, stop=False)
                    nc.tensor.matmul(out, a_rest, b_head, start=False, stop=False)
                    return nc.tensor.matmul(out, a_head, b_rest, start=False, stop=last)

                def project_out(n, m, w, j):
                    wait(pe, oh_kept, n + 1)
                    wait(pe, ol_kept, n + 1)
                    if j == 0:
                        wait(pe, y_kept, m)
                    for c in range(CH):
                        cols = slice(c * P, (c + 1) * P)
                        last = product(y_bank[:, c, :], WH[:, w, 6 + j, cols], WL[:, w, 6 + j, cols],
                                       OH[:, j, :], OL[:, j, :], j == 0, j == 1)
                    last.then_inc(out_made, 1)

                def turn(n, j):
                    pe.wait_ge(probs_made, n + 1)
                    wait(pe, t_kept, n)
                    for b in range(GB):
                        last = nc.tensor.transpose(t_bank[:, b * T:(b + 1) * T], PR[:, j, b, :], ident[:, :])
                    last.then_inc(t_made, 1)

                def apply(n, g, j):
                    pe.wait_ge(t_kept, n + 1)
                    pe.wait_ge(v_kept, n + 2 - j)
                    wait(pe, ol_kept, n)
                    for b in range(GB):
                        last = nc.tensor.matmul(o_bank[:, b * T:(b + 1) * T], V[:, g % 2, b, j, :], PT[:, j, b, :],
                                                start=True, stop=True)
                    last.then_inc(o_made, 1)

                def body(pair, w):
                    pe.wait_ge(weight_head, (pair + 1) * PIECES)
                    pe.wait_ge(weight_rest, (pair + 1) * PIECES)
                    for u in range(UNITS):
                        n, g, j = pair * UNITS + u, u // 2, u % 2
                        whole = not (isinstance(pair, int) and pair == 0)
                        wait(pe, v_kept, n)
                        for k in range(2):
                            b = GB * g + 2 * j + k
                            for c in range(CH):
                                nc.tensor.matmul(v_bank[:, k * PW:(k + 1) * PW], XH[:, c, b, :], WH[:, w, 4 + c, :],
                                                 start=c == 0, stop=False)
                                nc.tensor.matmul(v_bank[:, k * PW:(k + 1) * PW], XL[:, c, b, :], WH[:, w, 4 + c, :],
                                                 start=False, stop=False)
                                last = nc.tensor.matmul(v_bank[:, k * PW:(k + 1) * PW], XH[:, c, b, :],
                                                        WL[:, w, 4 + c, :], start=False, stop=c == CH - 1)
                        last.then_inc(v_made, 1)
                        for bank, at, kept, made in ((q_bank, 0, q_kept, q_made), (k_bank, 2, k_kept, k_made)):
                            wait(pe, kept, n)
                            for c in range(CH):
                                cols = slice(j * DH, (j + 1) * DH)
                                last = product(bank[:, :], WH[:, w, at + c, cols], WL[:, w, at + c, cols],
                                               XH[:, c, GB * g:GB * g + GB, :], XL[:, c, GB * g:GB * g + GB, :],
                                               c == 0, c == CH - 1)
                            last.then_inc(made, 1)
                        if whole or u >= 2:
                            project_out(n - 2, pair * NG + u // 2 - 1, w if u >= 2 else 1 - w, j)
                        if whole or u >= 1:
                            turn(n - 1, 1 - j)
                        pe.wait_ge(q_kept, n + 1)
                        pe.wait_ge(k_kept, n + 1)
                        wait(pe, exp_made, n)
                        for b in range(GB):
                            last = nc.tensor.matmul(s_bank[:, b * T:(b + 1) * T], QT[:, j, b, :], KT[:, j, b, :],
                                                    start=True, stop=True)
                        last.then_inc(s_made, 1)
                        if whole or u >= 1:
                            apply(n - 1, (u - 1) % UNITS // 2, 1 - j)

                over_pairs(pe, body)
                project_out(LAST - 2, LAST // 2 - 1, 1, 0)
                turn(LAST - 1, 1)
                apply(LAST - 1, NG - 1, 1)
                project_out(LAST - 1, LAST // 2 - 1, 1, 1)

            @block.vector
            def _(dve):
                def head(pair, w, k):
                    dve.wait_ge(weight_whole, pair * PIECES + k + 1)
                    wait(dve, k_made, (pair - 1) * UNITS)
                    if k >= 6:
                        wait(dve, out_made, (pair - 1) * UNITS)
                    nc.vector.tensor_copy(WH[:, w, k, :], codes[:, w, k, :]).then_inc(weight_head, 1)

                def keep_out(n, m, g):
                    dve.wait_ge(out_made, n + 1)
                    wait(dve, y_kept, m)
                    nc.vector.tensor_tensor(YT[:, :, GB * g:GB * g + GB, :], YT[:, :, GB * g:GB * g + GB, :],
                                            y_bank[:, :, :].rearrange("p c (b t) -> p c b t", b=GB),
                                            ALU.add).then_inc(y_kept, 1)

                def rest_of_heads(n, j):
                    dve.wait_ge(oh_kept, n + 1)
                    wait(dve, out_made, n - 1)
                    nc.vector.tensor_tensor(OL[:, j, :], o_bank[:, :], OH[:, j, :].bitcast(F32),
                                            ALU.subtract).then_inc(ol_kept, 1)

                dve.wait_ge(bias_in, 64)
                nc.vector.tensor_scalar(bq_sb[:, :], bq_sb[:, :], SCALE, None, ALU.mult).then_inc(biases_set, 1)
                for c in range(CH):
                    nc.vector.tensor_copy(YT[:, c, :, :].rearrange("p b t -> p (b t)"),
                                          bo_sb[:, c:c + 1].to_broadcast([P, NB * T])).then_inc(biases_set, 1)
                dve.wait_ge(biases_set, 1 + CH)

                def body(pair, w, more=True):
                    for u in range(UNITS):
                        n, g, j = pair * UNITS + u, u // 2, u % 2
                        whole = not (isinstance(pair, int) and pair == 0)
                        dve.wait_ge(v_made, n + 1)
                        wait(dve, o_made, n - j - 2)
                        nc.vector.tensor_tensor(
                            V[:, g % 2, 2 * j:2 * j + 2, :, :].rearrange("p k a d -> p k (a d)"),
                            v_bank[:, :].rearrange("p (k f) -> p k f", k=2),
                            bv_sb[:, bass.ds(pair * PW, PW)].unsqueeze(1).to_broadcast([P, 2, PW]),
                            ALU.add).then_inc(v_kept, 1)
                        dve.wait_ge(k_made, n + 1)
                        wait(dve, s_made, n - 1)
                        nc.vector.tensor_scalar(KT[:, j, :, :], k_bank[:, :].rearrange("p (b t) -> p b t", b=GB),
                                                bk_sb[:, bass.ds(pair * 2 + j, 1)], None,
                                                ALU.add).then_inc(k_kept, 1)
                        if j == 1 and (whole or u >= 2):
                            keep_out(n - 2, pair * NG + g - 1, (g - 1) % NG)
                        dve.wait_ge(s_made, n + 1)
                        wait(dve, exp_made, n - 1)
                        nc.vector.tensor_reduce(NM[:, j, :], s_bank[:, :].rearrange("p (b t) -> p b t", b=GB),
                                                AX.X, ALU.max, negate=True).then_inc(max_made, 1)
                        if more:
                            for k in pieces(u):
                                head(pair + 1, 1 - w, k)
                        dve.wait_ge(exp_made, n + 1)
                        wait(dve, probs_made, n - 1)
                        nc.vector.reciprocal(RS[:, j, :], SM[:, j, :]).then_inc(inverse_made, 1)
                        if whole or u >= 1:
                            rest_of_heads(n - 1, 1 - j)

                body(0, 0)
                with dve.Fori(0, PAIRS // 2 - 1) as i:
                    body(2 * i + 1, 1)
                    body(2 * i + 2, 0)
                body(PAIRS - 1, 1, more=False)
                rest_of_heads(LAST - 1, 1)
                keep_out(LAST - 1, LAST // 2 - 1, NG - 1)

            @block.scalar
            def _(act):
                def keep_turned(n, j):
                    act.wait_ge(t_made, n + 1)
                    wait(act, o_made, n - 1)
                    nc.scalar.activation(PT[:, j, :, :], t_bank[:, :].rearrange("p (b t) -> p b t", b=GB),
                                         ACT.Copy).then_inc(t_kept, 1)

                def head_of_heads(n, j):
                    act.wait_ge(o_made, n + 1)
                    wait(act, out_made, n - 1)
                    nc.scalar.activation(OH[:, j, :], o_bank[:, :], ACT.Copy).then_inc(oh_kept, 1)

                act.wait_ge(biases_set, 1)

                def body(pair, w):
                    nc.scalar.activation(bq_pair[:, w, :], bq_sb[:, bass.ds(pair * 2, 2)], ACT.Copy).then_inc(bq_picked, 1)
                    act.wait_ge(bq_picked, pair + 1)
                    for u in range(UNITS):
                        n, j = pair * UNITS + u, u % 2
                        whole = not (isinstance(pair, int) and pair == 0)
                        act.wait_ge(q_made, n + 1)
                        wait(act, s_made, n - 1)
                        nc.scalar.activation(QT[:, j, :, :], q_bank[:, :].rearrange("p (b t) -> p b t", b=GB),
                                             ACT.Identity, bias=bq_pair[:, w, j:j + 1],
                                             scale=SCALE).then_inc(q_kept, 1)
                        if whole or u >= 1:
                            keep_turned(n - 1, 1 - j)
                        act.wait_ge(max_made, n + 1)
                        wait(act, t_made, n - 1)
                        wait(act, inverse_made, n - 1)
                        for b in range(GB):
                            last = nc.scalar.activation(PR[:, j, b, :], s_bank[:, b * T:(b + 1) * T], ACT.Exp,
                                                        bias=NM[:, j, b:b + 1], accum_out=SM[:, j, b:b + 1])
                        last.then_inc(exp_made, 1)
                        if whole or u >= 1:
                            head_of_heads(n - 1, 1 - j)

                over_pairs(act, body)
                keep_turned(LAST - 1, 1)
                head_of_heads(LAST - 1, 1)


def stage_wkv(nc, time_decay, time_first, XT, CT, YT):
    HALF = NB // 2
    N = HALF * T
    CHUNKS = CH * 2
    with ExitStack() as ctx:
        s = Space(nc, ctx, "wkv")
        w_sb, u_sb = s.sb("decay", [P, CH]), s.sb("first", [P, CH])
        decay = s.sb("decays", [P, CH, HALF, T])
        peak = s.sb("peak", [P, 2, N + 1])
        to_peak, e_old, e_new, y_old, y_new, value, spare = (
            s.sb(n, [P, 2, N]) for n in ("to_peak", "e_old", "e_new", "y_old", "y_new", "value", "spare"))
        num, den = s.sb("num", [P, 2, N + 1]), s.sb("den", [P, 2, N + 1])
        (in_, w_set, ordered, peaked, old_made, new_made, forgot, top_made, y_new_made, y_old_made,
         carried, weighed, value_made, fresh_made, num_made, den_made, aged) = (s.sem(n) for n in (
             "in", "w_set", "ordered", "peaked", "old_made", "new_made", "forgot", "top_made", "y_new_made",
             "y_old_made", "carried", "weighed", "value_made", "fresh_made", "num_made", "den_made", "aged"))

        def flat(tensor, k):
            h = k % 2
            return tensor[:, k // 2, HALF * h:HALF * h + HALF, :].rearrange("p b t -> p (b t)")

        def starts(buffer):
            return buffer.rearrange("p (b t) -> p b t", b=HALF)[:, :, 0]

        with nc.Block() as block:

            @block.sync
            def _(sp):
                sp.dma_start(w_sb[:, :], time_decay).then_inc(in_, 16)
                sp.dma_start(u_sb[:, :], time_first).then_inc(in_, 16)

            @block.scalar
            def _(act):
                act.wait_ge(in_, 32)
                nc.scalar.activation(w_sb[:, :], w_sb[:, :], ACT.Exp).then_inc(w_set, 1)
                for k in range(CHUNKS):
                    r = k % 2
                    act.wait_ge(forgot, k + 1)
                    nc.scalar.activation(e_old[:, r, :], e_old[:, r, :], ACT.Exp).then_inc(carried, 1)
                    act.wait_ge(new_made, k + 1)
                    nc.scalar.activation(e_new[:, r, :], e_new[:, r, :], ACT.Exp).then_inc(carried, 1)
                    act.wait_ge(y_new_made, k + 1)
                    nc.scalar.activation(y_new[:, r, :], y_new[:, r, :], ACT.Exp).then_inc(weighed, 1)
                    act.wait_ge(y_old_made, k + 1)
                    nc.scalar.activation(y_old[:, r, :], y_old[:, r, :], ACT.Exp).then_inc(weighed, 1)

            @block.gpsimd
            def _(pool):
                def exponents(k):
                    r = k % 2
                    pool.wait_ge(peaked, k + 1)
                    wait(pool, den_made, k - 1)
                    nc.gpsimd.tensor_tensor(e_new[:, r, :], flat(XT, k), peak[:, r, 1:N + 1],
                                            ALU.subtract).then_inc(new_made, 1)
                    pool.wait_ge(top_made, k + 1)
                    nc.gpsimd.tensor_tensor(y_old[:, r, :], peak[:, r, 0:N], to_peak[:, r, :],
                                            ALU.subtract).then_inc(y_old_made, 1)

                def products(k):
                    r = k % 2
                    pool.wait_ge(carried, 2 * k + 2)
                    nc.gpsimd.tensor_tensor(value[:, r, :], e_new[:, r, :], flat(CT, k), ALU.mult).then_inc(value_made, 1)
                    pool.wait_ge(weighed, 2 * k + 2)
                    nc.gpsimd.tensor_tensor(spare[:, r, :], y_new[:, r, :], flat(CT, k), ALU.mult).then_inc(fresh_made, 1)
                    pool.wait_ge(den_made, k + 1)
                    pool.wait_ge(value_made, k + 1)
                    nc.gpsimd.tensor_tensor(e_new[:, r, :], y_old[:, r, :], den[:, r, 0:N], ALU.mult).then_inc(aged, 1)

                for k in range(CHUNKS + 1):
                    if k < CHUNKS:
                        exponents(k)
                    if k:
                        products(k - 1)

            @block.vector
            def _(dve):
                step = Chain(dve, ordered)
                dve.wait_ge(w_set, 1)
                step(nc.vector.tensor_scalar(w_sb[:, :], w_sb[:, :], -1.0, None, ALU.mult))
                for c in range(CH):
                    step(nc.vector.tensor_copy(decay[:, c, :, :].rearrange("p b t -> p (b t)"),
                                               w_sb[:, c:c + 1].to_broadcast([P, N])))
                step(nc.vector.memset(decay[:, :, :, 0], FAR))
                for r in range(2):
                    nc.vector.memset(peak[:, r, 0:1], FAR)
                    nc.vector.memset(num[:, r, 0:1], 0.0)
                    step(nc.vector.memset(den[:, r, 0:1], 0.0))

                def before_exp(k):
                    r, c = k % 2, k // 2
                    keys = flat(XT, k)
                    wait(dve, aged, k - 1)
                    nc.vector.tensor_tensor_scan(peak[:, r, 1:N + 1], decay[:, c, :, :].rearrange("p b t -> p (b t)"),
                                                 keys, FAR, ALU.add, ALU.max).then_inc(peaked, 1)
                    dve.wait_ge(peaked, k + 1)
                    nc.vector.scalar_tensor_tensor(e_old[:, r, :], peak[:, r, 0:N], w_sb[:, c:c + 1],
                                                   peak[:, r, 1:N + 1], ALU.add, ALU.subtract).then_inc(old_made, 1)
                    dve.wait_ge(old_made, k + 1)
                    dve.wait_ge(new_made, k + 1)
                    step(nc.vector.memset(starts(peak[:, r, 0:N]), FAR))
                    nc.vector.memset(starts(e_old[:, r, :]), FAR).then_inc(forgot, 1)
                    nc.vector.scalar_tensor_tensor(to_peak[:, r, :], keys, u_sb[:, c:c + 1], peak[:, r, 0:N],
                                                   ALU.add, ALU.max).then_inc(top_made, 1)
                    dve.wait_ge(top_made, k + 1)
                    nc.vector.scalar_tensor_tensor(y_new[:, r, :], keys, u_sb[:, c:c + 1], to_peak[:, r, :],
                                                   ALU.add, ALU.subtract).then_inc(y_new_made, 1)

                def after_exp(k):
                    r = k % 2
                    dve.wait_ge(carried, 2 * k + 2)
                    nc.vector.tensor_tensor_scan(den[:, r, 1:N + 1], e_old[:, r, :], e_new[:, r, :], 0.0,
                                                 ALU.mult, ALU.add).then_inc(den_made, 1)
                    dve.wait_ge(value_made, k + 1)
                    step(nc.vector.tensor_tensor_scan(num[:, r, 1:N + 1], e_old[:, r, :], value[:, r, :], 0.0,
                                                      ALU.mult, ALU.add))
                    dve.wait_ge(weighed, 2 * k + 2)
                    step(nc.vector.tensor_tensor(value[:, r, :], y_old[:, r, :], num[:, r, 0:N], ALU.mult))
                    dve.wait_ge(fresh_made, k + 1)
                    step(nc.vector.tensor_tensor(value[:, r, :], value[:, r, :], spare[:, r, :], ALU.add))
                    dve.wait_ge(aged, k + 1)
                    step(nc.vector.tensor_tensor(to_peak[:, r, :], e_new[:, r, :], y_new[:, r, :], ALU.add))
                    step(nc.vector.reciprocal(to_peak[:, r, :], to_peak[:, r, :]))
                    step(nc.vector.tensor_tensor(flat(YT, k), value[:, r, :], to_peak[:, r, :], ALU.mult))

                for k in range(CHUNKS + 1):
                    if k < CHUNKS:
                        before_exp(k)
                    if k:
                        after_exp(k - 1)


def stage_ternary_ffn(nc, w1, b1, ln_g, ln_b, w2, b2, X, YT, ident, identb, eps, ones):
    H = 1024
    HC = H // P
    LEVELS = 127.0
    COUNT = float(H * D)
    with ExitStack() as ctx:
        s = Space(nc, ctx, "ffn")
        HB = s.sb("hidden", [P, NB, H])
        W1, W2 = s.sb("w1", [P, HC, D]), s.sb("w2", [P, CH, H])
        B1, B2, G, B = s.sb("b1", [P, H]), s.sb("b2", [P, D]), s.sb("gain", [P, H]), s.sb("shift", [P, H])
        Q1, Q2 = s.sb("w1_ternary", [P, HC, D], BF16), s.sb("w2_ternary", [P, CH, H], BF16)
        W1T, W2T = s.sb("w1_turned", [P, CH, H], BF16), s.sb("w2_turned", [P, HC, D], BF16)
        size, unit, scale = s.sb("size", [P, 2]), s.sb("unit", [P, 2]), s.sb("scale", [P, 2])
        st, mv = s.sb("st", [P, NB, 6]), s.sb("mv", [P, NB, 2])
        hst, hmv = s.sb("hst", [P, NB, 2, 6]), s.sb("hmv", [P, NB, 2])
        rstd, high, low, size1, fac1, dq1 = (s.sb(n, [P, NB]) for n in ("rstd", "high", "low", "size1", "fac1", "dq1"))
        hrstd, ssq, size2, fac2, dq2, root = (s.sb(n, [P, NB]) for n in ("hrstd", "ssq", "size2", "fac2", "dq2", "root"))
        steps = s.sb("steps", [P, 2, D])
        q = s.sb("q", [P, 2, D], BF16)
        qT = s.sb("q_turned", [P, 2, CH, T], BF16)
        wide, square = s.sb("wide", [P, H]), s.sb("square", [P, H])
        shift = s.sb("shift_by_mean", [P, NB])
        q2 = s.sb("q2", [P, 2, H], BF16)
        q2T = s.sb("q2_turned", [P, 2, HC, T], BF16)
        (in1, in2, in_rows, sized, ternary, turned, kept, whole_kept, rooted, step_done, rounded, q_turned, q_kept,
         z_made, z_kept, silu_done, gelu_done, stats, aggregated, residual_read, shifted, h_normed, squared, measured,
         widened, rounded2, q2_turned, q2_kept, y_made, y_kept) = (s.sem(n) for n in (
             "in1", "in2", "in_rows", "sized", "ternary", "turned", "kept", "whole_kept", "rooted", "step", "rounded",
             "q_turned", "q_kept", "z_made", "z_kept", "silu", "gelu", "stats", "aggregated", "residual_read", "shifted",
             "h_normed", "squared", "measured", "widened", "rounded2", "q2_turned", "q2_kept", "y_made", "y_kept"))

        y_turned, y_added, w2_ternary, w2_turned, w2_kept, scaled, shift_made, centred, gained = (s.sem(n) for n in (
            "y_turned", "y_added", "w2_ternary", "w2_turned", "w2_kept", "scaled", "shift_made", "centred", "gained"))

        with ExitStack() as banks, nc.Block() as block:
            back = [banks.enter_context(nc.psum_tensor(f"ffn_back{k}", [P, GB, D], F32)) for k in range(2)]
            w_bank = [banks.enter_context(nc.psum_tensor(f"ffn_w_bank{k}", [P, H], BF16)) for k in range(CH)]
            sum_bank = banks.enter_context(nc.psum_tensor("ffn_sum_bank", [P, 2], F32))

            @block.sync
            def _(sp):
                sp.dma_start(W1[:, :, :], w1.rearrange("(o p) d -> p o d", p=P)).then_inc(in1, 16)
                sp.dma_start(W2[:, :, :], w2.rearrange("(o p) h -> p o h", p=P)).then_inc(in2, 16)
                for to, row in ((B1, b1), (B2, b2), (G, ln_g), (B, ln_b)):
                    sp.dma_start(to[:, :], row.partition_broadcast(P)).then_inc(in_rows, 16)
                sp.wait_ge(in_rows, 64)

            @block.scalar
            def _(act):
                act.wait_ge(in1, 16)
                nc.scalar.activation(HB[:, 0:2, :], W1[:, :, :].rearrange("p (k o) d -> p k (o d)", k=2), ACT.Abs,
                                     accum_out=size[:, 0:1]).then_inc(sized, 1)
                act.wait_ge(in2, 16)
                nc.scalar.activation(HB[:, 2:4, :], W2[:, :, :], ACT.Abs, accum_out=size[:, 1:2]).then_inc(sized, 1)
                for c in range(CH):
                    act.wait_ge(turned, 2 + c)
                    nc.scalar.activation(W1T[:, c, :], w_bank[c][:, :], ACT.Copy).then_inc(kept, 1)

            @block.tensor
            def _(pe):
                def turn_back(g):
                    wait(pe, y_added, g - 1)
                    for b in range(GB):
                        for c in range(CH):
                            last = nc.tensor.transpose(back[g % 2][:, b, c * P:(c + 1) * P], YT[:, c, GB * g + b, :],
                                                       ident[:, :])
                    last.then_inc(y_turned, 1)

                turn_back(0)
                turn_back(1)
                pe.wait_ge(sized, 2)
                nc.tensor.matmul(sum_bank[:, :], ones[:, :], size[:, :], start=True, stop=True).then_inc(turned, 1)
                turn_back(2)
                turn_back(3)
                pe.wait_ge(ternary, 1)
                for c in range(CH):
                    for o in range(HC):
                        last = nc.tensor.transpose(w_bank[c][:, o * P:(o + 1) * P], Q1[:, o, c * P:(c + 1) * P],
                                                   identb[:, :])
                    last.then_inc(turned, 1)

            @block.vector
            def _(dve):
                step = Chain(dve, step_done)

                def update(g):
                    part = slice(GB * g, GB * g + GB)
                    dve.wait_ge(y_turned, g + 1)
                    nc.vector.tensor_tensor(X[:, part, :], X[:, part, :], back[g % 2][:, :, :],
                                            ALU.add).then_inc(y_added, 1)
                    dve.wait_ge(y_added, g + 1)
                    for b in range(GB * g, GB * g + GB):
                        nc.vector.bn_stats(st[:, b, :], X[:, b, :]).then_inc(stats, 1)
                    nc.vector.tensor_reduce(high[:, part], X[:, part, :], AX.X, ALU.max).then_inc(stats, 1)
                    nc.vector.tensor_reduce(low[:, part], X[:, part, :], AX.X, ALU.min).then_inc(stats, 1)

                update(0)
                update(1)
                dve.wait_ge(turned, 1)
                step(nc.vector.tensor_scalar(unit[:, :], sum_bank[:, :], 1.0 / COUNT, 1e-5, ALU.mult, ALU.max))
                nc.vector.reciprocal(scale[:, :], unit[:, :]).then_inc(scaled, 1)
                dve.wait_ge(scaled, 1)
                step(nc.vector.tensor_scalar(W1[:, :, :], W1[:, :, :], scale[:, 0:1], ROUND, ALU.mult, ALU.add))
                step(nc.vector.tensor_scalar(W1[:, :, :], W1[:, :, :], ROUND, 1.0, ALU.subtract, ALU.min))
                nc.vector.tensor_scalar(Q1[:, :, :], W1[:, :, :], -1.0, None, ALU.max).then_inc(ternary, 1)
                update(2)
                update(3)

        with ExitStack() as banks, nc.Block() as block:
            turn_bank = [banks.enter_context(nc.psum_tensor(f"ffn_turn_bank{k}", [P, H], BF16)) for k in range(2)]
            z_bank = [banks.enter_context(nc.psum_tensor(f"ffn_z_bank{k}", [P, H], F32)) for k in range(2)]
            y_bank = [banks.enter_context(nc.psum_tensor(f"ffn_y_bank{k}", [P, D], F32)) for k in range(2)]

            def tiles(eng, body):
                body(0, 0)
                body(1, 1)
                with eng.Fori(1, NB // 2) as i:
                    body(2 * i, 0)
                    body(2 * i + 1, 1)

            def lagging(first, second):
                def body(n, r):
                    first(n, r)
                    if not (isinstance(n, int) and n == 0):
                        second(n - 1, 1 - r)
                return body

            def leading(first, second):
                def body(n, r):
                    first(n, r)
                    if not (isinstance(n, int) and n < 2):
                        second(n - 2, r)
                return body

            @block.vector
            def _(dve):
                step = Chain(dve, step_done)
                step.n = 1 + 2
                dve.wait_ge(stats, NB + 2 * NG)
                for b in range(NB):
                    nc.vector.bn_aggr(mv[:, b, :], st[:, b, :]).then_inc(aggregated, 1)
                dve.wait_ge(aggregated, NB)
                mean, var = mv[:, :, 0], mv[:, :, 1]
                step(nc.vector.tensor_tensor(high[:, :], high[:, :], mean, ALU.subtract))
                step(nc.vector.tensor_tensor(low[:, :], mean, low[:, :], ALU.subtract))
                step(nc.vector.tensor_tensor(size1[:, :], high[:, :], low[:, :], ALU.max))
                dve.wait_ge(rooted, 1)
                step(nc.vector.reciprocal(rstd[:, :], root[:, :]))
                step(nc.vector.tensor_tensor(low[:, :], var, rstd[:, :], ALU.mult))
                nc.vector.tensor_tensor(low[:, :], low[:, :], rstd[:, :], ALU.mult).then_inc(measured, 1)
                dve.wait_ge(rooted, 2)
                step(nc.vector.reciprocal(high[:, :], root[:, :]))
                step(nc.vector.tensor_tensor(rstd[:, :], rstd[:, :], high[:, :], ALU.mult))
                step(nc.vector.tensor_tensor(size1[:, :], size1[:, :], rstd[:, :], ALU.mult))
                step(nc.vector.tensor_scalar(dq1[:, :], size1[:, :], 1e-5, 1.0 / LEVELS, ALU.max, ALU.mult))
                step(nc.vector.reciprocal(fac1[:, :], dq1[:, :]))
                step(nc.vector.tensor_tensor(fac1[:, :], fac1[:, :], rstd[:, :], ALU.mult))
                step(nc.vector.tensor_scalar(dq1[:, :], dq1[:, :], unit[:, 0:1], None, ALU.mult))

                def quantise(n, r):
                    wait(dve, q_turned, n - 1)
                    nc.vector.tensor_scalar(steps[:, r, :], X[:, n, :], mv[:, n, 0:1], fac1[:, bass.ds(n, 1)],
                                            ALU.subtract, ALU.mult).then_inc(residual_read, 1)
                    dve.wait_ge(residual_read, n + 1)
                    nc.vector.tensor_scalar(q[:, r, :], steps[:, r, :], ROUND, ROUND,
                                            ALU.add, ALU.subtract).then_inc(rounded, 1)

                def dequantise(n, r):
                    dve.wait_ge(z_made, n + 1)
                    nc.vector.scalar_tensor_tensor(HB[:, n, :], z_bank[r][:, :], dq1[:, bass.ds(n, 1)], B1[:, :],
                                                   ALU.mult, ALU.add).then_inc(z_kept, 1)

                tiles(dve, leading(quantise, dequantise))
                dequantise(NB - 2, 0)
                dequantise(NB - 1, 1)

                def gather(n, r):
                    dve.wait_ge(gelu_done, n + 1)
                    for k in range(2):
                        nc.vector.bn_stats(hst[:, n, k, :], HB[:, n, k * H // 2:(k + 1) * H // 2]).then_inc(stats, 1)
                tiles(dve, gather)
                dve.wait_ge(stats, NB + 2 * NG + 2 * NB)
                for b in range(NB):
                    nc.vector.bn_aggr(hmv[:, b, :], hst[:, b, :, :].rearrange("p k n -> p (k n)")).then_inc(aggregated, 1)
                dve.wait_ge(rooted, 3)
                step(nc.vector.reciprocal(hrstd[:, :], root[:, :]))
                nc.vector.scalar_tensor_tensor(shift[:, :], hmv[:, :, 0], -1.0, hrstd[:, :], ALU.mult,
                                               ALU.mult).then_inc(shift_made, 1)

                def normalise(n, r):
                    dve.wait_ge(gained, n + 1)
                    nc.vector.tensor_tensor(HB[:, n, :], HB[:, n, :], B[:, :], ALU.add).then_inc(h_normed, 1)
                    dve.wait_ge(h_normed, n + 1)
                    nc.vector.tensor_reduce(size2[:, bass.ds(n, 1)], HB[:, n, :], AX.X, ALU.max,
                                            apply_absolute_value=True).then_inc(measured, 1)
                tiles(dve, normalise)
                dve.wait_ge(measured, 1 + NB)
                dve.wait_ge(rooted, 4)
                step(nc.vector.reciprocal(hrstd[:, :], root[:, :]))
                step(nc.vector.tensor_tensor(size2[:, :], size2[:, :], hrstd[:, :], ALU.mult))
                step(nc.vector.tensor_scalar(dq2[:, :], size2[:, :], 1e-5, 1.0 / LEVELS, ALU.max, ALU.mult))
                step(nc.vector.reciprocal(fac2[:, :], dq2[:, :]))
                step(nc.vector.tensor_tensor(fac2[:, :], fac2[:, :], hrstd[:, :], ALU.mult))
                step(nc.vector.tensor_scalar(dq2[:, :], dq2[:, :], unit[:, 1:2], None, ALU.mult))
                dve.wait_ge(shifted, 1)

                def quantise2(n, r):
                    wait(dve, q2_turned, n - 1)
                    wait(dve, rounded2, n)
                    nc.vector.tensor_scalar(wide[:, :], HB[:, n, :], fac2[:, bass.ds(n, 1)], ROUND,
                                            ALU.mult, ALU.add).then_inc(widened, 1)
                    dve.wait_ge(widened, n + 1)
                    nc.vector.tensor_scalar(q2[:, r, :], wide[:, :], ROUND, None, ALU.subtract).then_inc(rounded2, 1)

                def add(n, r):
                    dve.wait_ge(y_made, n + 1)
                    nc.vector.scalar_tensor_tensor(X[:, n, :], y_bank[r][:, :], dq2[:, bass.ds(n, 1)], X[:, n, :],
                                                   ALU.mult, ALU.add).then_inc(y_kept, 1)

                tiles(dve, leading(quantise2, add))
                add(NB - 2, 0)
                add(NB - 1, 1)

            @block.gpsimd
            def _(pool):
                pool.wait_ge(scaled, 1)
                nc.gpsimd.tensor_scalar(W2[:, :, :], W2[:, :, :], scale[:, 1:2], ROUND, ALU.mult,
                                        ALU.add).then_inc(w2_ternary, 1)
                pool.wait_ge(w2_ternary, 1)
                nc.gpsimd.tensor_scalar(W2[:, :, :], W2[:, :, :], ROUND, 1.0, ALU.subtract,
                                        ALU.min).then_inc(w2_ternary, 1)
                pool.wait_ge(w2_ternary, 2)
                nc.gpsimd.tensor_scalar(Q2[:, :, :], W2[:, :, :], -1.0, None, ALU.max).then_inc(w2_ternary, 1)
                pool.wait_ge(residual_read, NB)
                nc.gpsimd.tensor_tensor(X[:, :, :], X[:, :, :], B2[:, :].unsqueeze(1).to_broadcast([P, NB, D]),
                                        ALU.add).then_inc(shifted, 1)
                for n in range(NB):
                    pool.wait_ge(centred, n + 1)
                    nc.gpsimd.tensor_tensor(HB[:, n, :], HB[:, n, :], G[:, :], ALU.mult).then_inc(gained, 1)

            @block.tensor
            def _(pe):
                def turn(n, r):
                    pe.wait_ge(rounded, n + 1)
                    wait(pe, q_kept, n - 1)
                    for c in range(CH):
                        last = nc.tensor.transpose(turn_bank[r][:, c * T:(c + 1) * T], q[:, r, c * P:(c + 1) * P],
                                                   identb[:, :])
                    last.then_inc(q_turned, 1)

                def up(n, r):
                    pe.wait_ge(q_kept, n + 1)
                    wait(pe, z_kept, n - 1)
                    for k in range(2):
                        cols = slice(k * H // 2, (k + 1) * H // 2)
                        for c in range(CH):
                            last = nc.tensor.matmul(z_bank[r][:, cols], qT[:, r, c, :], W1T[:, c, cols],
                                                    start=c == 0, stop=c == CH - 1)
                    last.then_inc(z_made, 1)

                def turn2(n, r):
                    pe.wait_ge(rounded2, n + 1)
                    wait(pe, q2_kept, n - 1)
                    for c in range(HC):
                        last = nc.tensor.transpose(turn_bank[r][:, c * T:(c + 1) * T], q2[:, r, c * P:(c + 1) * P],
                                                   identb[:, :])
                    last.then_inc(q2_turned, 1)

                def down(n, r):
                    pe.wait_ge(q2_kept, n + 1)
                    wait(pe, y_kept, n - 1)
                    for c in range(HC):
                        last = nc.tensor.matmul(y_bank[r][:, :], q2T[:, r, c, :], W2T[:, c, :],
                                                start=c == 0, stop=c == HC - 1)
                    last.then_inc(y_made, 1)

                tiles(pe, lagging(turn, up))
                up(NB - 1, 1)
                pe.wait_ge(q_kept, NB)
                pe.wait_ge(w2_ternary, 3)
                for o in range(CH):
                    for c in range(HC):
                        last = nc.tensor.transpose(turn_bank[o][:, c * P:(c + 1) * P], Q2[:, o, c * P:(c + 1) * P],
                                                   identb[:, :])
                    last.then_inc(w2_turned, 1)
                pe.wait_ge(w2_kept, CH)
                tiles(pe, lagging(turn2, down))
                down(NB - 1, 1)

            @block.scalar
            def _(act):
                act.wait_ge(aggregated, NB)
                nc.scalar.activation(root[:, :], mv[:, :, 1], ACT.Sqrt, bias=eps[:, :]).then_inc(rooted, 1)
                act.wait_ge(measured, 1)
                nc.scalar.activation(root[:, :], low[:, :], ACT.Sqrt, bias=eps[:, :]).then_inc(rooted, 1)

                def keep(n, r):
                    wait(act, z_made, n - 1)
                    act.wait_ge(q_turned, n + 1)
                    nc.scalar.activation(qT[:, r, :, :], turn_bank[r][:, 0:CH * T].rearrange("p (c t) -> p c t", c=CH),
                                         ACT.Copy).then_inc(q_kept, 1)

                def silu(n, r):
                    act.wait_ge(z_kept, n + 1)
                    act.wait_ge(rooted, 2)
                    nc.scalar.activation(HB[:, n, :], HB[:, n, :], ACT.Silu).then_inc(silu_done, 1)

                def gelu(n, r):
                    nc.scalar.activation(HB[:, n, :], HB[:, n, :], ACT.Gelu).then_inc(gelu_done, 1)

                tiles(act, lagging(keep, silu))
                silu(NB - 1, 1)
                for o in range(CH):
                    act.wait_ge(w2_turned, o + 1)
                    nc.scalar.activation(W2T[:, :, o * P:(o + 1) * P],
                                         turn_bank[o][:, :].rearrange("p (c o) -> p c o", c=HC),
                                         ACT.Copy).then_inc(w2_kept, 1)
                act.wait_ge(silu_done, NB)
                tiles(act, gelu)
                act.wait_ge(aggregated, 2 * NB)
                nc.scalar.activation(root[:, :], hmv[:, :, 1], ACT.Sqrt, bias=eps[:, :]).then_inc(rooted, 1)

                def centre(n):
                    nc.scalar.activation(HB[:, n, :], HB[:, n, :], ACT.Identity, bias=shift[:, n:n + 1],
                                         scale=hrstd[:, n:n + 1]).then_inc(centred, 1)

                def squares(n):
                    wait(act, squared, n)
                    act.wait_ge(h_normed, n + 1)
                    nc.scalar.activation(square[:, :], HB[:, n, :], ACT.Square,
                                         accum_out=ssq[:, n:n + 1]).then_inc(squared, 1)

                act.wait_ge(shift_made, 1)
                for n in range(NB + 3):
                    if n < NB:
                        centre(n)
                    if n >= 3:
                        squares(n - 3)
                act.wait_ge(squared, NB)
                nc.scalar.activation(root[:, :], ssq[:, :], ACT.Sqrt, bias=eps[:, :], scale=1.0 / H).then_inc(rooted, 1)

                def keep2(n, r):
                    wait(act, y_made, n - 1)
                    act.wait_ge(q2_turned, n + 1)
                    nc.scalar.activation(q2T[:, r, :, :], turn_bank[r][:, :].rearrange("p (c t) -> p c t", c=HC),
                                         ACT.Copy).then_inc(q2_kept, 1)
                tiles(act, keep2)


def stage_s6(nc, x_proj, dt_proj, dt_bias, A_log, D_skip, out_proj, out_bias, XT, YT, ident):
    STATES, RANK = 16, 128
    BC = 2 * STATES
    with ExitStack() as ctx:
        s = Space(nc, ctx, "s6")
        XP, XP2 = s.sb("x_proj", [RANK, D]), s.sb("x_proj_bc", [BC, D])
        DP, WO = s.sb("dt_proj", [P, CH, RANK]), s.sb("out_proj", [P, CH, D])
        DPT, WBC = s.sb("dt_proj_turned", [RANK, D]), s.sb("bc_turned", [P, CH, BC])
        WDT, WOT = s.sb("dt_weight", [P, CH, D]), s.sb("out_proj_turned", [P, CH, D])
        bias, ob, skip = s.sb("dt_bias", [P, CH]), s.sb("out_bias", [P, CH]), s.sb("skip", [P, CH])
        A = s.sb("a", [P, CH, STATES])
        delta, dx = s.sb("delta", [P, CH, NB, T]), s.sb("dx", [P, CH, NB, T])
        positive = s.sb("positive", [P, 2, CH, GT])
        parts = s.sb("bc_parts", [2 * BC, NB * T], F32R)
        eye = s.sb("eye", [2 * BC, BC], F32R)
        (in_, turned, kept, a_made, step_done, dt_made, bc_made, sized, exped, split, logged, summed, dx_made, cut) = (
            s.sem(n) for n in ("in", "turned", "kept", "a_made", "step", "dt_made", "bc_made", "sized", "exped",
                               "split", "logged", "summed", "dx_made", "cut"))

        with ExitStack() as banks, nc.Block() as block:
            w_bank = [banks.enter_context(nc.psum_tensor(f"s6_w_bank{k}", [P, 512], F32)) for k in range(3)]
            dt_bank = [banks.enter_context(nc.psum_tensor(f"s6_dt_bank{k}", [P, CH, GT], F32)) for k in range(2)]
            bc_bank = banks.enter_context(nc.psum_tensor("s6_bc_bank", [BC, GT], F32))

            @block.sync
            def _(sp):
                for to, source in ((XP[:, :], x_proj[0:RANK, :]), (XP2[:, :], x_proj[RANK:RANK + BC, :]),
                                   (DP[:, :, :], dt_proj.rearrange("(c p) r -> p c r", p=P)),
                                   (WO[:, :, :], out_proj.rearrange("(c p) d -> p c d", p=P)),
                                   (A[:, :, :], A_log.rearrange("(c p) n -> p c n", p=P)),
                                   (bias[:, :], dt_bias), (ob[:, :], out_bias), (skip[:, :], D_skip)):
                    sp.dma_start(to, source).then_inc(in_, 16)

            @block.tensor
            def _(pe):
                pe.wait_ge(in_, 128)
                for c in range(CH):
                    nc.tensor.transpose(w_bank[0][:, c * P:(c + 1) * P], DP[:, c, :], ident[:, :])
                for c in range(CH):
                    last = nc.tensor.transpose(w_bank[0][:, D + c * BC:D + (c + 1) * BC], XP2[:, c * P:(c + 1) * P],
                                               ident[0:BC, 0:BC])
                last.then_inc(turned, 1)
                for o in range(CH):
                    for c in range(CH):
                        last = nc.tensor.transpose(w_bank[1][:, c * D + o * P:c * D + (o + 1) * P],
                                                   WO[:, o, c * P:(c + 1) * P], ident[:, :])
                last.then_inc(turned, 1)
                pe.wait_ge(kept, 1)
                for c in range(CH):
                    last = nc.tensor.matmul(w_bank[2][:, c * D:(c + 1) * D], XP[:, c * P:(c + 1) * P], DPT[:, :],
                                            start=True, stop=True)
                last.then_inc(turned, 1)
                pe.wait_ge(kept, 4)
                for g in range(NG):
                    wait(pe, split, 2 * g)
                    for c in range(CH):
                        last = nc.tensor.matmul(bc_bank[:, :], WBC[:, c, :], XT[:, c, GB * g:GB * g + GB, :],
                                                start=c == 0, stop=c == CH - 1)
                    last.then_inc(bc_made, 1)
                    wait(pe, sized, 2 * (g - 1))
                    wait(pe, cut, 2 * (g - 1))
                    for e in range(CH):
                        for c in range(CH):
                            last = nc.tensor.matmul(dt_bank[g % 2][:, e, :], WDT[:, c, e * P:(e + 1) * P],
                                                    XT[:, c, GB * g:GB * g + GB, :], start=c == 0, stop=c == CH - 1)
                    last.then_inc(dt_made, 1)

            @block.scalar
            def _(act):
                act.wait_ge(turned, 1)
                nc.scalar.activation(DPT[:, :], w_bank[0][:, 0:D], ACT.Copy).then_inc(kept, 1)
                nc.scalar.activation(WBC[:, :, :], w_bank[0][:, D:D + CH * BC].rearrange("p (c n) -> p c n", c=CH),
                                     ACT.Copy).then_inc(kept, 1)
                act.wait_ge(turned, 2)
                nc.scalar.activation(WOT[:, :, :], w_bank[1][:, :].rearrange("p (c d) -> p c d", c=CH),
                                     ACT.Copy).then_inc(kept, 1)
                act.wait_ge(turned, 3)
                nc.scalar.activation(WDT[:, :, :], w_bank[2][:, :].rearrange("p (c d) -> p c d", c=CH),
                                     ACT.Copy).then_inc(kept, 1)
                act.wait_ge(in_, 128)
                nc.scalar.activation(A[:, :, :], A[:, :, :], ACT.Exp).then_inc(a_made, 1)
                for g in range(NG):
                    tokens = slice(g * GT, (g + 1) * GT)
                    act.wait_ge(bc_made, g + 1)
                    nc.scalar.activation(parts[0:BC, tokens], bc_bank[:, :], ACT.Copy).then_inc(split, 1)
                    here = delta[:, :, GB * g:GB * g + GB, :]
                    act.wait_ge(dt_made, g + 1)
                    for c in range(CH):
                        nc.scalar.activation(here[:, c].rearrange("p b t -> p (b t)"), dt_bank[g % 2][:, c, :], ACT.Abs,
                                             bias=bias[:, c:c + 1]).then_inc(sized, 1)
                    act.wait_ge(sized, 2 * (g + 1))
                    nc.scalar.activation(here, here, ACT.Exp, scale=-1.0).then_inc(exped, 1)
                    act.wait_ge(exped, g + 1)
                    nc.scalar.activation(here, here, ACT.Ln, bias=1.0).then_inc(logged, 1)

            @block.vector
            def _(dve):
                step = Chain(dve, step_done)
                dve.wait_ge(a_made, 1)
                step(nc.vector.tensor_scalar(A[:, :, :], A[:, :, :], -1.0, None, ALU.mult))
                for k in range(2):
                    step(nc.vector.tensor_copy(eye[k * BC:(k + 1) * BC, :],
                                               ident[k * BC:(k + 1) * BC, k * BC:(k + 1) * BC]))

                def softplus_end(g):
                    here = slice(GB * g, GB * g + GB)
                    dve.wait_ge(logged, g + 1)
                    dve.wait_ge(cut, 2 * (g + 1))
                    nc.vector.tensor_tensor(delta[:, :, here, :], delta[:, :, here, :],
                                            positive[:, g % 2, :, :].rearrange("p c (b t) -> p c b t", b=GB),
                                            ALU.add).then_inc(summed, 1)

                for g in range(NG):
                    here = slice(GB * g, GB * g + GB)
                    dve.wait_ge(split, 2 * g + 1)
                    nc.vector.tensor_tensor(parts[BC:2 * BC, g * GT:(g + 1) * GT], bc_bank[:, :],
                                            parts[0:BC, g * GT:(g + 1) * GT].bitcast(F32),
                                            ALU.subtract).then_inc(split, 1)
                    dve.wait_ge(dt_made, g + 1)
                    dve.wait_ge(sized, 2 * (g + 1))
                    wait(dve, summed, g - 1)
                    for c in range(CH):
                        nc.vector.tensor_scalar(positive[:, g % 2, c, :], dt_bank[g % 2][:, c, :], bias[:, c:c + 1], 0.0,
                                                ALU.add, ALU.max).then_inc(cut, 1)
                    if g:
                        softplus_end(g - 1)
                softplus_end(NG - 1)

            @block.gpsimd
            def _(pool):
                for g in range(NG):
                    here = slice(GB * g, GB * g + GB)
                    pool.wait_ge(summed, g + 1)
                    nc.gpsimd.tensor_tensor(dx[:, :, here, :], delta[:, :, here, :], XT[:, :, here, :],
                                            ALU.mult).then_inc(dx_made, 1)

        RING = 4
        UNITS = NG * STATES
        decay, u = (s.sb(n, [P, RING, CH, GT]) for n in ("decay", "u"))
        h, hc = (s.sb(n, [P, 2, CH, GT]) for n in ("h", "hc"))
        b_rows = s.sb("b_rows", [P, 2 * RING, GT])
        AHEAD = 3
        y, r = s.sb("y", [P, CH, GT]), s.sb("r", [P, CH, GT])
        (b_made, c_made, b_kept, decayed, cleared, u_made, scanned, weighed, y_made, y_kept, o_made, o_kept, added) = (
            s.sem(n) for n in ("b_made", "c_made", "b_kept", "decayed", "cleared", "u_made", "scanned", "weighed",
                               "y_made", "y_kept", "o_made", "o_kept", "added"))
        b_bank = [s.ps(f"b_bank{k}", [P, GT]) for k in range(2)]
        c_bank = [s.ps(f"c_bank{k}", [P, GT]) for k in range(2)]
        y_bank, o_bank = s.ps("y_bank", [P, CH, GT]), s.ps("o_bank", [P, CH, GT])

        with nc.Block() as block:

            @block.tensor
            def _(pe):
                def spread(k, first, bank, free, made):
                    g, n = k // STATES, k % STATES
                    wait(pe, free, k - 1)
                    nc.tensor.matmul(bank[n % 2][:, :], eye[:, first + n:first + n + 1].to_broadcast([2 * BC, P]),
                                     parts[:, g * GT:(g + 1) * GT], start=True, stop=True).then_inc(made, 1)

                def sum_states(n, k):
                    pe.wait_ge(weighed, k + 1)
                    for c in range(CH):
                        last = nc.tensor.matmul(y_bank[:, c, :], ident[:, :], hc[:, n % 2, c, :],
                                                start=n == 0, stop=n == STATES - 1)
                    last.then_inc(y_made, 1)

                def project(g):
                    pe.wait_ge(y_kept, g + 1)
                    wait(pe, o_kept, g)
                    for e in range(CH):
                        for c in range(CH):
                            last = nc.tensor.matmul(o_bank[:, e, :], WOT[:, c, e * P:(e + 1) * P], y[:, c, :],
                                                    start=c == 0, stop=c == CH - 1)
                    last.then_inc(o_made, 1)

                for k in range(-AHEAD - 1, UNITS):
                    if k + AHEAD + 1 < UNITS:
                        spread(k + AHEAD + 1, 0, b_bank, b_kept, b_made)
                    if 0 <= k + 1 < UNITS:
                        spread(k + 1, STATES, c_bank, weighed, c_made)
                    if k >= 0:
                        g, n = k // STATES, k % STATES
                        if n == 0:
                            wait(pe, y_kept, g)
                        sum_states(n, k)
                        if n == 1 and g:
                            project(g - 1)
                project(NG - 1)

            @block.scalar
            def _(act):
                def keep_y(g):
                    wait(act, o_made, g)
                    act.wait_ge(y_made, (g + 1) * STATES)
                    nc.scalar.activation(y[:, :, :], y_bank[:, :, :], ACT.Copy).then_inc(y_kept, 1)

                def relu(g):
                    wait(act, added, g)
                    act.wait_ge(o_made, g + 1)
                    for e in range(CH):
                        last = nc.scalar.activation(r[:, e, :], o_bank[:, e, :], ACT.Relu, bias=ob[:, e:e + 1])
                    last.then_inc(o_kept, 1)

                def keep_b(k):
                    act.wait_ge(b_made, k + 1)
                    wait(act, u_made, k - 2 * RING + 1)
                    nc.scalar.activation(b_rows[:, k % (2 * RING), :], b_bank[k % 2][:, :], ACT.Copy).then_inc(b_kept, 1)

                act.wait_ge(cleared, 1)
                for k in range(UNITS):
                    g, n = k // STATES, k % STATES
                    keep_b(k)
                    wait(act, scanned, k - RING + 1)
                    for c in range(CH):
                        last = nc.scalar.activation(
                            decay[:, k % RING, c, :].rearrange("p (b t) -> p b t", b=GB)[:, :, 1:T],
                            delta[:, c, GB * g:GB * g + GB, 1:T], ACT.Exp, scale=A[:, c, n:n + 1])
                    last.then_inc(decayed, 1)
                    if n == 6 and g:
                        relu(g - 1)
                    if n == 2 and g:
                        keep_y(g - 1)
                keep_y(NG - 1)
                relu(NG - 1)

            @block.gpsimd
            def _(pool):
                pool.memset(decay[:, :, :, :].rearrange("p r c (b t) -> p (r c b) t", b=GB)[:, :, 0:1],
                            0.0).then_inc(cleared, 1)

                def body(g):
                    for n in range(STATES):
                        k = g * STATES + n
                        wait(pool, scanned, k - RING + 1)
                        pool.wait_ge(b_kept, k + 1)
                        pool.wait_ge(cleared, 1)
                        nc.gpsimd.tensor_tensor(
                            u[:, n % RING, :, :].rearrange("p c (b t) -> p c b t", b=GB),
                            dx[:, :, bass.ds(g * GB, GB), :],
                            b_rows[:, n % (2 * RING), :].rearrange("p (b t) -> p b t", b=GB).unsqueeze(1)
                            .to_broadcast([P, CH, GB, T]), ALU.mult).then_inc(u_made, 1)
                for g in range(NG):
                    body(g)

            @block.vector
            def _(dve):
                def finish(g):
                    dve.wait_ge(o_kept, g + 1)
                    here = bass.ds(g * GB, GB)
                    for c in range(CH):
                        last = nc.vector.scalar_tensor_tensor(
                            YT[:, c, here, :], XT[:, c, here, :], skip[:, c:c + 1],
                            r[:, c, :].rearrange("p (b t) -> p b t", b=GB), ALU.mult, ALU.add)
                    last.then_inc(added, 1)

                def body(g):
                    for n in range(STATES):
                        k = g * STATES + n
                        dve.wait_ge(decayed, k + 1)
                        dve.wait_ge(u_made, k + 1)
                        wait(dve, weighed, k - 1)
                        nc.vector.tensor_tensor_scan(
                            h[:, n % 2, :, :].rearrange("p c t -> p (c t)"),
                            decay[:, n % RING, :, :].rearrange("p c t -> p (c t)"),
                            u[:, n % RING, :, :].rearrange("p c t -> p (c t)"), 0.0, ALU.mult, ALU.add).then_inc(scanned, 1)
                        dve.wait_ge(scanned, k + 1)
                        dve.wait_ge(c_made, k + 1)
                        wait(dve, y_made, k - 1)
                        nc.vector.tensor_tensor(hc[:, n % 2, :, :], h[:, n % 2, :, :],
                                                c_bank[n % 2][:, :].unsqueeze(1).to_broadcast([P, CH, GT]),
                                                ALU.mult).then_inc(weighed, 1)
                        if n == 8 and g:
                            finish(g - 1)

                for g in range(NG):
                    body(g)
                finish(NG - 1)


def stage_long_conv(nc, kernels, D_skip, XT, CT, YT, anti, ident):
    HD = 8
    HEADS = T // HD
    PAIRS = HD * (HD + 1) // 2
    HALF = NB // 2
    QB = 4
    STEPS = CH * NB // QB
    at = [d * HD - d * (d - 1) // 2 for d in range(HD)]
    with ExitStack() as ctx:
        s = Space(nc, ctx, "conv")
        hankel = s.sb("hankel", [P, HEADS, D])
        toeplitz = s.sb("toeplitz", [P, HEADS, D])
        skip = s.sb("skip", [P, HEADS])
        kv = s.sb("kv", [P, CH, NB, HEADS, PAIRS])
        weighed = s.sb("weighed", [P, 2, QB * HEADS, HD, HD])
        kv_rows = [kv[:, c, :, :, :].rearrange("p b h n -> p (b h) n") for c in range(CH)]
        xt_rows = [XT[:, c, :, :].rearrange("p b (h i) -> p (b h) i", i=HD) for c in range(CH)]
        ct_rows = [CT[:, c, :, :].rearrange("p b (h i) -> p (b h) i", i=HD) for c in range(CH)]
        yt_rows = [YT[:, c, :, :].rearrange("p b (h j) -> p (b h) j", j=HD) for c in range(CH)]
        bank = [s.ps(f"bank{k}", [P, 2, 512]) for k in range(4)]
        in_, flipped, ready, paired, made, kept, query_old, query_new, summed = (
            s.sem(n) for n in ("in", "flipped", "ready", "paired", "made", "kept", "query_old", "query_new", "summed"))
        UNITS = 2 * HEADS
        FLIPS = HEADS // 4

        with nc.Block() as block:

            @block.sync
            def _(sp):
                sp.dma_start(hankel[:, :, :], bass.AP(tensor=kernels.tensor, offset=1,
                                                      ap=[[1, P], [P + D, HEADS], [1, D]])).then_inc(in_, 16)
                sp.dma_start(skip[:, :], D_skip.partition_broadcast(P)).then_inc(in_, 16)

            @block.tensor
            def _(pe):
                pe.wait_ge(in_, 32)
                for k in range(FLIPS):
                    wait(pe, ready, 4 * (k - 3))
                    for j in range(2):
                        last = nc.tensor.matmul(bank[k % 4][:, j, :], anti[:, :],
                                                hankel[:, 4 * k + 2 * j:4 * k + 2 * j + 2, :], start=True, stop=True)
                    last.then_inc(flipped, 1)
                pe.wait_ge(ready, HEADS)
                for unit in range(UNITS):
                    half, h = unit // HEADS, unit % HEADS
                    pe.wait_ge(paired, CH * (half + 1))
                    wait(pe, kept, unit - 3)
                    here = slice(HALF * half, HALF * half + HALF)
                    out = bank[unit % 4]
                    low, high = kv[:, 0, here, h, :], kv[:, 1, here, h, :]
                    n = HALF * PAIRS
                    nc.tensor.matmul(out[:, 0, 0:n], toeplitz[:, h, 0:P], low, start=True, stop=True)
                    nc.tensor.matmul(out[:, 1, 0:n], toeplitz[:, h, P:D], low, start=True, stop=False)
                    nc.tensor.matmul(out[:, 1, 0:n], toeplitz[:, h, 0:P], high, start=False, stop=True).then_inc(made, 1)

            @block.scalar
            def _(act):
                for unit in range(UNITS):
                    half, h = unit // HEADS, unit % HEADS
                    act.wait_ge(made, unit + 1)
                    nc.scalar.activation(
                        kv[:, :, HALF * half:HALF * half + HALF, h, :],
                        bank[unit % 4][:, :, 0:HALF * PAIRS].rearrange("p c (b n) -> p c b n", b=HALF),
                        ACT.Copy).then_inc(kept, 1)

            def step_of(k):
                quarter, c = k // CH, k % CH
                return c, slice(QB * HEADS * quarter, QB * HEADS * (quarter + 1)), QB * (quarter + 1)

            @block.vector
            def _(dve):
                dve.wait_ge(in_, 32)
                for k in range(FLIPS):
                    dve.wait_ge(flipped, k + 1)
                    for h in range(4 * k, 4 * k + 4):
                        source = bank[k % 4][:, (h % 4) // 2, (h % 2) * D:(h % 2 + 1) * D]
                        nc.vector.tensor_copy(toeplitz[:, h, P:D], source[:, P:D])
                        nc.vector.scalar_tensor_tensor(toeplitz[:, h, 0:P], ident[:, :], skip[:, h:h + 1],
                                                       source[:, 0:P], ALU.mult, ALU.add).then_inc(ready, 1)
                for half in range(2):
                    rows = slice(half * HALF * HEADS, (half + 1) * HALF * HEADS)
                    for c in range(CH):
                        for d in range(HD):
                            last = nc.vector.tensor_tensor(kv_rows[c][:, rows, at[d]:at[d] + HD - d],
                                                           ct_rows[c][:, rows, 0:HD - d], ct_rows[c][:, rows, d:HD],
                                                           ALU.mult)
                        last.then_inc(paired, 1)
                for k in range(STEPS):
                    c, rows, upto = step_of(k)
                    dve.wait_ge(kept, HEADS * (1 + (upto > HALF)))
                    for d in range(HD):
                        out = weighed[:, k % 2, :, d:HD, 0:HD - d]
                        diagonal = bass.AP(tensor=out.tensor, offset=out.offset,
                                           ap=[out.ap[0], out.ap[1], [HD + 1, HD - d]])
                        last = nc.vector.tensor_tensor(diagonal, kv_rows[c][:, rows, at[d]:at[d] + HD - d],
                                                       xt_rows[c][:, rows, 0:HD - d], ALU.mult)
                    last.then_inc(query_old, 1)
                    dve.wait_ge(query_old, k + 1)
                    dve.wait_ge(query_new, k + 1)
                    nc.vector.tensor_reduce(yt_rows[c][:, rows, :], weighed[:, k % 2, :, :, :], AX.X,
                                            ALU.add).then_inc(summed, 1)

            @block.gpsimd
            def _(pool):
                for k in range(STEPS):
                    c, rows, upto = step_of(k)
                    pool.wait_ge(kept, HEADS * (1 + (upto > HALF)))
                    wait(pool, summed, k - 1)
                    for d in range(1, HD):
                        out = weighed[:, k % 2, :, 0:HD - d, d:HD]
                        diagonal = bass.AP(tensor=out.tensor, offset=out.offset,
                                           ap=[out.ap[0], out.ap[1], [HD + 1, HD - d]])
                        last = nc.gpsimd.tensor_tensor(diagonal, kv_rows[c][:, rows, at[d]:at[d] + HD - d],
                                                       xt_rows[c][:, rows, d:HD], ALU.mult)
                    last.then_inc(query_new, 1)


def stage_experts(nc, gate_w, up_gate, up_value, down, rows_of, XH, XL, YT, ident, eps):
    EXPERTS, TOP, ROWS = 16, 4, 32
    UNUSED, CHOSEN = -1.0, -2.0
    TILES, BLOCKS = 5, 5
    UNITS = NG * TILES
    BH = TILES * P
    UP, VALUE, DOWN, WIDTH = 0, CH * BH, 2 * CH * BH, 2 * CH * BH + TILES * D
    PIECES = 16
    PW = WIDTH // PIECES
    LAST = BLOCKS * UNITS
    with ExitStack() as ctx:
        s = Space(nc, ctx, "moe")
        raw, raw_rows = s.sb("raw", [P, WIDTH]), s.sb("raw_rows", [2 * ROWS, BH])
        WH, WL = s.sb("weight_head", [P, 2, WIDTH], F32R), s.sb("weight_rest", [P, 2, WIDTH], F32R)
        pick = s.sb("pick", [2 * ROWS, 2, BH], F32R)
        parts = s.sb("combine_parts", [2 * ROWS, NB * T], F32R)
        weights_in, rows_in, rows_set, head_set, rest_set = (
            s.sem(n) for n in ("weights_in", "rows_in", "rows_set", "head_set", "rest_set"))

        def load(sp, block):
            wait(sp, rest_set, block * PIECES)
            wait(sp, rows_set, block)
            cols = bass.ds(block * BH, BH)
            for at, source in ((UP, up_gate), (VALUE, up_value)):
                sp.dma_start(raw[:, at:at + CH * BH].rearrange("p (c f) -> p c f", c=CH),
                             source.rearrange("(c p) f -> p c f", p=P)[:, :, cols]).then_inc(weights_in, 16)
            sp.dma_start(raw[:, DOWN:WIDTH].rearrange("p (t f) -> p t f", t=TILES),
                         down.rearrange("(a t p) f -> a p t f", t=TILES, p=P)[block]).then_inc(weights_in, 16)
            for k in range(2):
                sp.dma_start(raw_rows[k * ROWS:(k + 1) * ROWS, :], rows_of[:, cols]).then_inc(rows_in, 16)

        def set_rows(act, block, w):
            act.wait_ge(rows_in, 32 * (block + 1))
            nc.scalar.activation(pick[:, w, :], raw_rows[:, :], ACT.Copy).then_inc(rows_set, 1)

        def set_head(act, block, w, k):
            act.wait_ge(weights_in, 48 * (block + 1))
            nc.scalar.activation(WH[:, w, k * PW:(k + 1) * PW], raw[:, k * PW:(k + 1) * PW],
                                 ACT.Copy).then_inc(head_set, 1)

        def set_rest(pool, block, w, k):
            pool.wait_ge(head_set, block * PIECES + k + 1)
            nc.gpsimd.tensor_tensor(WL[:, w, k * PW:(k + 1) * PW], raw[:, k * PW:(k + 1) * PW],
                                    WH[:, w, k * PW:(k + 1) * PW].bitcast(F32), ALU.subtract).then_inc(rest_set, 1)

        with ExitStack() as part, nc.Block() as block:
            def sb(name, shape, dt=F32):
                return part.enter_context(nc.sbuf_tensor(f"moe_{name}", shape, dt))

            gw = sb("gate_w", [EXPERTS, D])
            gh, gl = sb("gate_head", [P, CH, EXPERTS], F32R), sb("gate_rest", [P, CH, EXPERTS], F32R)
            padded, replaced = sb("score", [P, NB, EXPERTS + 8 - TOP]), sb("replaced", [P, NB, EXPERTS + 8 - TOP])
            score, top = padded[:, :, 0:EXPERTS], sb("top", [P, NB, 8])
            chosen, logits = sb("chosen", [P, NB, ROWS]), sb("logits", [EXPERTS, NG, GT])
            row, row2, row3 = sb("row", [P, NB]), sb("row2", [P, NB]), sb("row3", [P, NB])
            g_bank = part.enter_context(nc.psum_tensor("moe_g_bank", [P, CH * EXPERTS], F32))
            e_bank = [part.enter_context(nc.psum_tensor(f"moe_e_bank{k}", [EXPERTS, GT], F32)) for k in range(2)]
            l_bank = part.enter_context(nc.psum_tensor("moe_l_bank", [P, NB, EXPERTS], F32))
            c_bank = [part.enter_context(nc.psum_tensor(f"moe_c_bank{k}", [ROWS, GT], F32)) for k in range(NG)]
            gate_in, gate_turned, gate_kept, logits_made, step_done, shifted, exped, by_expert, e_kept, ranked, combined, turned, split = (
                s.sem(n) for n in ("gate_in", "gate_turned", "gate_kept", "logits_made", "step", "shifted", "exped",
                                   "by_expert", "e_kept", "ranked", "combined", "turned", "split"))

            @block.sync
            def _(sp):
                sp.dma_start(gw[:, :], gate_w).then_inc(gate_in, 16)
                load(sp, 0)

            @block.gpsimd
            def _(pool):
                for k in range(PIECES):
                    set_rest(pool, 0, 0, k)

            @block.tensor
            def _(pe):
                pe.wait_ge(gate_in, 16)
                for c in range(CH):
                    last = nc.tensor.transpose(g_bank[:, c * EXPERTS:(c + 1) * EXPERTS], gw[:, c * P:(c + 1) * P],
                                               ident[0:EXPERTS, 0:EXPERTS])
                last.then_inc(gate_turned, 1)
                pe.wait_ge(gate_kept, 2)
                for g in range(NG):
                    wait(pe, e_kept, g - 1)
                    here = slice(GB * g, GB * g + GB)
                    for c in range(CH):
                        nc.tensor.matmul(e_bank[g % 2][:, :], gh[:, c, :], XH[:, c, here, :], start=c == 0, stop=False)
                        nc.tensor.matmul(e_bank[g % 2][:, :], gh[:, c, :], XL[:, c, here, :], start=False, stop=False)
                        last = nc.tensor.matmul(e_bank[g % 2][:, :], gl[:, c, :], XH[:, c, here, :],
                                                start=False, stop=c == CH - 1)
                    last.then_inc(by_expert, 1)
                for g in range(NG):
                    pe.wait_ge(e_kept, g + 1)
                    for b in range(GB):
                        last = nc.tensor.transpose(l_bank[:, GB * g + b, :], logits[:, g, b * T:(b + 1) * T],
                                                   ident[0:EXPERTS, 0:EXPERTS])
                last.then_inc(logits_made, 1)
                pe.wait_ge(combined, 1)
                for g in range(NG):
                    for b in range(GB):
                        last = nc.tensor.transpose(c_bank[g][:, b * T:(b + 1) * T], chosen[:, GB * g + b, :], ident[:, :])
                    last.then_inc(turned, 1)

            @block.scalar
            def _(act):
                act.wait_ge(gate_turned, 1)
                nc.scalar.activation(gh[:, :, :], g_bank[:, :].rearrange("p (c e) -> p c e", c=CH),
                                     ACT.Copy).then_inc(gate_kept, 1)
                for g in range(NG):
                    act.wait_ge(by_expert, g + 1)
                    nc.scalar.activation(logits[:, g, :], e_bank[g % 2][:, :], ACT.Copy).then_inc(e_kept, 1)
                set_rows(act, 0, 0)
                for k in range(2):
                    set_head(act, 0, 0, k)
                act.wait_ge(shifted, 1)
                nc.scalar.activation(score, score, ACT.Exp).then_inc(exped, 1)
                for k in range(2, PIECES):
                    set_head(act, 0, 0, k)
                for g in range(NG):
                    act.wait_ge(turned, g + 1)
                    nc.scalar.activation(parts[0:ROWS, g * GT:(g + 1) * GT], c_bank[g][:, :], ACT.Copy).then_inc(split, 1)

            @block.vector
            def _(dve):
                step = Chain(dve, step_done)
                dve.wait_ge(gate_kept, 1)
                nc.vector.tensor_tensor(gl[:, :, :], g_bank[:, :].rearrange("p (c e) -> p c e", c=CH),
                                        gh[:, :, :].bitcast(F32), ALU.subtract).then_inc(gate_kept, 1)
                wide = [P, NB, EXPERTS]
                nc.vector.memset(padded[:, :, EXPERTS:], UNUSED)
                nc.vector.memset(chosen[:, :, EXPERTS + 1:ROWS], 0.0)
                step(nc.vector.memset(chosen[:, :, EXPERTS:EXPERTS + 1], 1.0))
                dve.wait_ge(logits_made, 1)
                step(nc.vector.tensor_reduce(row[:, :], l_bank[:, :, :], AX.X, ALU.max))
                nc.vector.tensor_tensor(score, l_bank[:, :, :], row[:, :].unsqueeze(2).to_broadcast(wide),
                                        ALU.subtract).then_inc(shifted, 1)
                dve.wait_ge(exped, 1)
                step(nc.vector.tensor_reduce(row2[:, :], score, AX.X, ALU.add))
                step(nc.vector.reciprocal(row2[:, :], row2[:, :]))
                step(nc.vector.tensor_tensor(score, score, row2[:, :].unsqueeze(2).to_broadcast(wide),
                                             ALU.mult))
                for b in range(NB):
                    nc.vector.max(top[:, b, :], padded[:, b, 0:EXPERTS]).then_inc(ranked, 1)
                dve.wait_ge(ranked, NB)
                step(nc.vector.memset(top[:, :, TOP:8], UNUSED))
                for b in range(NB):
                    nc.vector.match_replace(replaced[:, b, :], top[:, b, :], padded[:, b, :], CHOSEN).then_inc(ranked, 1)
                dve.wait_ge(ranked, 2 * NB)
                step(nc.vector.scalar_tensor_tensor(score, replaced[:, :, 0:EXPERTS], CHOSEN, score,
                                                    ALU.is_equal, ALU.mult))
                step(nc.vector.tensor_reduce(row3[:, :], score, AX.X, ALU.add))
                step(nc.vector.reciprocal(row3[:, :], row3[:, :]))
                nc.vector.tensor_tensor(chosen[:, :, 0:EXPERTS], score,
                                        row3[:, :].unsqueeze(2).to_broadcast(wide), ALU.mult).then_inc(combined, 1)
                for g in range(NG):
                    dve.wait_ge(split, g + 1)
                    nc.vector.tensor_tensor(parts[ROWS:2 * ROWS, g * GT:(g + 1) * GT], c_bank[g][:, :],
                                            parts[0:ROWS, g * GT:(g + 1) * GT].bitcast(F32), ALU.subtract)

        silu, scaled, hidden = (s.sb(n, [P, 2, GT]) for n in ("silu", "scaled", "hidden"))
        HH, HL = s.sb("hidden_head", [P, 2, GT], F32R), s.sb("hidden_rest", [P, 2, GT], F32R)
        gate_bank, value_bank, weight_bank = (
            [s.ps(f"{n}{k}", [P, GT]) for k in range(2)] for n in ("gate_bank", "value_bank", "weight_bank"))
        y_bank = s.ps("y_bank", [P, CH, GT])
        gate_made, value_made, weight_made, silu_made, scaled_made, hidden_made, hh_made, hl_made, down_made, y_kept, cleared = (
            s.sem(n) for n in ("gate_made", "value_made", "weight_made", "silu_made", "scaled_made", "hidden_made",
                               "hh_made", "hl_made", "down_made", "y_kept", "cleared"))

        with nc.Block() as block:

            def blocks(eng, body):
                body(0, 0)
                with eng.Fori(0, BLOCKS // 2) as i:
                    body(2 * i + 1, 1)
                    body(2 * i + 2, 0)

            def begun(b, u, lag):
                return u >= lag or not isinstance(b, int) or b > 0

            @block.sync
            def _(sp):
                load(sp, 1)
                with sp.Fori(2, BLOCKS) as b:
                    load(sp, b)

            @block.tensor
            def _(pe):
                def product(out, a_head, a_rest, b_head, b_rest, first, last):
                    nc.tensor.matmul(out, a_head, b_head, start=first, stop=False)
                    nc.tensor.matmul(out, a_rest, b_head, start=False, stop=False)
                    return nc.tensor.matmul(out, a_head, b_rest, start=False, stop=last)

                def project(n, m, w, t, r):
                    pe.wait_ge(hh_made, n + 1)
                    pe.wait_ge(hl_made, n + 1)
                    if t == 0:
                        wait(pe, y_kept, m)
                    for c in range(CH):
                        cols = slice(DOWN + t * D + c * P, DOWN + t * D + (c + 1) * P)
                        last = product(y_bank[:, c, :], WH[:, w, cols], WL[:, w, cols], HH[:, r, :], HL[:, r, :],
                                       t == 0, t == TILES - 1)
                    last.then_inc(down_made, 1)

                def body(b, w):
                    pe.wait_ge(head_set, (b + 1) * PIECES)
                    pe.wait_ge(rest_set, (b + 1) * PIECES)
                    pe.wait_ge(rows_set, b + 1)
                    for u in range(UNITS):
                        n, g, t, r = b * UNITS + u, u // TILES, u % TILES, u % 2
                        for bank, at, free, made in ((gate_bank, UP, silu_made, gate_made),
                                                     (value_bank, VALUE, scaled_made, value_made)):
                            wait(pe, free, n - 1)
                            for c in range(CH):
                                cols = slice(at + c * BH + t * P, at + c * BH + (t + 1) * P)
                                last = product(bank[r][:, :], WH[:, w, cols], WL[:, w, cols],
                                               XH[:, c, GB * g:GB * g + GB, :], XL[:, c, GB * g:GB * g + GB, :],
                                               c == 0, c == CH - 1)
                            last.then_inc(made, 1)
                        wait(pe, hidden_made, n - 1)
                        nc.tensor.matmul(weight_bank[r][:, :], pick[:, w, t * P:(t + 1) * P],
                                         parts[:, g * GT:(g + 1) * GT], start=True, stop=True).then_inc(weight_made, 1)
                        if begun(b, u, 2):
                            v = (u - 2) % UNITS
                            project(n - 2, b * NG + (u - 2) // TILES, w if u >= 2 else 1 - w, v % TILES, r)

                blocks(pe, body)
                for u in range(UNITS - 2, UNITS):
                    project(LAST - UNITS + u, BLOCKS * NG - 1, 0, u % TILES, u % 2)

            @block.scalar
            def _(act):
                def head(n, r):
                    act.wait_ge(hidden_made, n + 1)
                    wait(act, down_made, n - 1)
                    nc.scalar.activation(HH[:, r, :], hidden[:, r, :], ACT.Copy).then_inc(hh_made, 1)

                def body(b, w, more=True):
                    for u in range(UNITS):
                        n, r = b * UNITS + u, u % 2
                        act.wait_ge(gate_made, n + 1)
                        wait(act, scaled_made, n - 1)
                        nc.scalar.activation(silu[:, r, :], gate_bank[r][:, :], ACT.Silu).then_inc(silu_made, 1)
                        if begun(b, u, 1):
                            head(n - 1, 1 - r)
                        if more and u == 3:
                            wait(act, down_made, b * UNITS)
                            set_rows(act, b + 1, 1 - w)
                        if more and u >= 4:
                            set_head(act, b + 1, 1 - w, u - 4)

                body(0, 0)
                with act.Fori(0, BLOCKS // 2 - 1) as i:
                    body(2 * i + 1, 1)
                    body(2 * i + 2, 0)
                body(BLOCKS - 2, 1)
                body(BLOCKS - 1, 0, more=False)
                head(LAST - 1, 1)

            @block.gpsimd
            def _(pool):
                def rest(n, r):
                    pool.wait_ge(hh_made, n + 1)
                    wait(pool, down_made, n - 1)
                    nc.gpsimd.tensor_tensor(HL[:, r, :], hidden[:, r, :], HH[:, r, :].bitcast(F32),
                                            ALU.subtract).then_inc(hl_made, 1)

                def body(b, w, more=True):
                    for u in range(UNITS):
                        n, r = b * UNITS + u, u % 2
                        if begun(b, u, 1):
                            rest(n - 1, 1 - r)
                        if more and u >= 4:
                            set_rest(pool, b + 1, 1 - w, u - 4)

                body(0, 0)
                with pool.Fori(0, BLOCKS // 2 - 1) as i:
                    body(2 * i + 1, 1)
                    body(2 * i + 2, 0)
                body(BLOCKS - 2, 1)
                body(BLOCKS - 1, 0, more=False)
                rest(LAST - 1, 1)

            @block.vector
            def _(dve):
                def keep(n, m, g):
                    here = YT[:, :, GB * g:GB * g + GB, :]
                    y = y_bank[:, :, :].rearrange("p c (b t) -> p c b t", b=GB)
                    dve.wait_ge(down_made, n + 1)
                    wait(dve, y_kept, m)
                    nc.vector.tensor_tensor(here, here, y, ALU.add).then_inc(y_kept, 1)

                def body(b, w):
                    for u in range(UNITS):
                        n, r = b * UNITS + u, u % 2
                        if u % TILES == 2 and begun(b, u, 3):
                            g = u // TILES - 1
                            keep(n - 3, b * NG + g, g % NG)
                        dve.wait_ge(silu_made, n + 1)
                        dve.wait_ge(value_made, n + 1)
                        wait(dve, hidden_made, n - 1)
                        nc.vector.tensor_tensor(scaled[:, r, :], silu[:, r, :], value_bank[r][:, :],
                                                ALU.mult).then_inc(scaled_made, 1)
                        dve.wait_ge(scaled_made, n + 1)
                        dve.wait_ge(weight_made, n + 1)
                        wait(dve, hl_made, n - 1)
                        nc.vector.tensor_tensor(hidden[:, r, :], scaled[:, r, :], weight_bank[r][:, :],
                                                ALU.mult).then_inc(hidden_made, 1)

                nc.vector.memset(YT[:, :, :, :], 0.0).then_inc(cleared, 1)
                dve.wait_ge(cleared, 1)
                blocks(dve, body)
                keep(LAST - 1, BLOCKS * NG - 1, NG - 1)


def build(nc, a, out):
    with ExitStack() as ctx:
        s = Space(nc, ctx, "all")
        X = s.sb("x", [P, NB, D])
        YT = s.sb("y", [P, CH, NB, T])
        ident, anti, identb = s.sb("ident", [P, P]), s.sb("anti", [P, P]), s.sb("identb", [P, P], BF16)
        eps, ones = s.sb("eps", [P, 1]), s.sb("ones", [P, P])
        with ExitStack() as layers:
            CT = layers.enter_context(nc.sbuf_tensor("context", [P, CH, NB, T], F32))
            stage_load(nc, a["x"], a["ctx_2048"], X, CT, ident, identb, anti, eps, ones)
            with ExitStack() as part:
                XH = part.enter_context(nc.sbuf_tensor("attn_xh", [P, CH, NB, T], F32R))
                XL = part.enter_context(nc.sbuf_tensor("attn_xl", [P, CH, NB, T], F32R))
                stage_attention(nc, *(a[f"L0_attn_{n}"] for n in ("wq_codes", "wq_scales", "bq", "wk_codes", "wk_scales",
                                                                  "bk", "wv_codes", "wv_scales", "bv", "wo_codes",
                                                                  "wo_scales", "bo")),
                                XH, XL, YT, ident,
                                before=lambda ahead: stage_renorm(nc, "norm0", X, ident, eps, XH=XH, XL=XL, ahead=ahead))
            with ExitStack() as part:
                XT = part.enter_context(nc.sbuf_tensor("wkv_xt", [P, CH, NB, T], F32))
                stage_renorm(nc, "norm1", X, ident, eps, YT=YT, XT=XT)
                stage_wkv(nc, a["L0_xattn_time_decay"], a["L0_xattn_time_first"], XT, CT, YT)
            stage_ternary_ffn(nc, *(a[f"L0_ffn_{n}"] for n in ("w1", "b1", "ln_g", "ln_b", "w2", "b2")),
                              X, YT, ident, identb, eps, ones)
            with ExitStack() as part:
                XT = part.enter_context(nc.sbuf_tensor("s6_xt", [P, CH, NB, T], F32))
                stage_renorm(nc, "norm3", X, ident, eps, XT=XT)
                stage_s6(nc, *(a[f"L1_attn_{n}"] for n in ("x_proj_weight", "dt_proj_weight", "dt_proj_bias", "A_log", "D",
                                                           "out_proj_weight", "out_proj_bias")), XT, YT, ident)
            with ExitStack() as part:
                XT = part.enter_context(nc.sbuf_tensor("conv_xt", [P, CH, NB, T], F32))
                stage_renorm(nc, "norm4", X, ident, eps, YT=YT, XT=XT)
                stage_long_conv(nc, a["L1_xattn_ssm_kernel"], a["L1_xattn_D"], XT, CT, YT, anti, ident)
        with ExitStack() as part:
            XH = part.enter_context(nc.sbuf_tensor("moe_xh", [P, CH, NB, T], F32R))
            XL = part.enter_context(nc.sbuf_tensor("moe_xl", [P, CH, NB, T], F32R))
            stage_renorm(nc, "norm5", X, ident, eps, YT=YT, XH=XH, XL=XL)
            stage_experts(nc, a["L1_ffn_gate_w"], a["moe_gate"], a["moe_value"], a["moe_down"], a["moe_rows"],
                          XH, XL, YT, ident, eps)
        stage_renorm(nc, "end", X, ident, eps, YT=YT, out=out)


def kernel(**inputs):
    import numpy as _np
    import concourse.bacc as _bacc
    from concourse import mybir as _mybir
    from concourse.bass_utils import run_bass_kernel_spmd as _run

    nc = _bacc.Bacc("TRN2", target_bir_lowering=False, num_devices=1)
    arrays, args = {}, {}
    columns = ("L0_attn_bq", "L0_attn_bk", "L0_attn_bo", "L0_xattn_time_decay", "L0_xattn_time_first",
               "L1_attn_dt_proj_bias", "L1_attn_D", "L1_attn_out_proj_bias")
    inputs = {name: _np.asarray(value) for name, value in inputs.items()}
    routed = [inputs.pop(f"L1_ffn_{n}") for n in ("w_gate", "w_up", "w_down")]
    shared = [inputs.pop(f"L1_ffn_{n}") for n in ("sw_gate", "sw_up", "sw_down")]
    experts, _, width = routed[0].shape
    units = experts * width + shared[0].shape[1]
    padded = -(-units // P) * P
    zeros = _np.zeros((D, padded - units), routed[0].dtype)
    for name, own, all_ in zip(("moe_gate", "moe_value"), routed, shared):
        inputs[name] = _np.concatenate([own.transpose(1, 0, 2).reshape(D, experts * width), all_, zeros], axis=1)
    inputs["moe_down"] = _np.concatenate([routed[2].reshape(experts * width, D), shared[2], zeros.T], axis=0)
    owner = _np.minimum(_np.arange(padded) // width, experts)
    inputs["moe_rows"] = (owner[None, :] == _np.arange(32)[:, None]).astype(_np.float32)
    for name, value in inputs.items():
        a = _np.asarray(value)
        if name in columns:
            a = a.reshape(-1, P).T
        if name == "L1_xattn_ssm_kernel":
            a = _np.pad(a, ((0, 0), (P, 0)))
        a = _np.ascontiguousarray(a)
        arrays[f"in_{name}"] = a
        args[name] = nc.dram_tensor(f"in_{name}", a.shape, _mybir.dt.from_np(a.dtype), kind="ExternalInput").ap()
    out = nc.dram_tensor("out", (NB, T, D), F32, kind="ExternalOutput").ap()
    build(nc, args, out)
    r = _run(nc, [arrays], core_ids=[0])
    return r.results[0]["out"]
```

```python
import concourse.bass as bass
from concourse import mybir
from contextlib import ExitStack

F32 = mybir.dt.float32
F32R = mybir.dt.float32r
BF16 = mybir.dt.bfloat16
ALU = mybir.AluOpType
ACT = mybir.ActivationFunctionType
AX = mybir.AxisListType

NB, T, D = 16, 128, 256
P = 128
CH = D // P
NG = 4
GB = NB // NG
GT = GB * T
EPS = 1e-5
ROUND = 1.5 * 2.0 ** 23
FAR = -1e38


def wait(eng, sem, value):
    if not (isinstance(value, int) and value <= 0):
        eng.wait_ge(sem, value)


class Chain:

    def __init__(self, eng, sem):
        self.eng, self.sem, self.n = eng, sem, 0

    def __call__(self, instruction):
        self.n += 1
        instruction.then_inc(self.sem, 1)
        self.eng.wait_ge(self.sem, self.n)


class Space:

    def __init__(self, nc, ctx, stage):
        self.nc, self.ctx, self.stage, self.sems = nc, ctx, stage, []
        ctx.callback(self.clear)

    def sb(self, name, shape, dt=F32):
        return self.ctx.enter_context(self.nc.sbuf_tensor(f"{self.stage}_{name}", shape, dt))

    def ps(self, name, shape, dt=F32):
        return self.ctx.enter_context(self.nc.psum_tensor(f"{self.stage}_{name}", shape, dt))

    def sem(self, name):
        self.sems.append(self.nc.alloc_semaphore(f"{self.stage}_{name}"))
        return self.sems[-1]

    def clear(self):
        if self.sems:
            self.nc.clear_and_free_semaphores(self.sems)
            self.nc.all_engine_barrier()


def stage_load(nc, x, ctx_in, X, C, x_in, c_in, ident, identb, anti, eps, ones):
    with ExitStack() as ctx:
        made = Space(nc, ctx, "load").sem("made")
        with nc.Block() as block:

            @block.sync
            def _(sp):
                for g in range(NG):
                    here = slice(GB * g, GB * g + GB)
                    sp.dma_start(X[:, here, :], x[here].rearrange("b s d -> s b d")).then_inc(x_in[g], 16)
                sp.dma_start(C[:, :, :], ctx_in.rearrange("b s d -> s b d")).then_inc(c_in, 16)

            @block.gpsimd
            def _(pool):
                pool.memset(ident[:, :], 0.0).then_inc(made, 1)
                pool.memset(anti[:, :], 0.0).then_inc(made, 1)
                pool.memset(eps[:, :], EPS)
                pool.memset(ones[:, :], 1.0)
                pool.wait_ge(made, 2)
                pool.affine_select(out=ident[:, :], in_=ident[:, :], compare_op=ALU.not_equal, fill=1.0,
                                   base=0, pattern=[[-1, P]], channel_multiplier=1).then_inc(made, 1)
                pool.affine_select(out=anti[:, :], in_=anti[:, :], compare_op=ALU.not_equal, fill=1.0,
                                   base=1 - P, pattern=[[1, P]], channel_multiplier=1).then_inc(made, 1)

            @block.vector
            def _(dve):
                dve.wait_ge(made, 4)
                nc.vector.tensor_copy(identb[:, :], ident[:, :])


def stage_renorm(nc, name, X, ident, eps, YT=None, XT=None, XH=None, XL=None, out=None, ahead=(), x_in=None, context=None):
    with ExitStack() as ctx:
        s = Space(nc, ctx, name)
        norm = XT is not None or XH is not None
        back = [s.ps(f"back{k}", [P, GB, D]) for k in range(2)]
        fore = [s.ps(f"fore{k}", [P, GB, CH, T]) for k in range(2)]
        xn = s.sb("xn", [P, 2, GB, D])
        c_turned, c_kept = s.sem("c_turned"), s.sem("c_kept")
        st = s.sb("st", [P, NB, 6])
        mv = s.sb("mv", [P, NB, 2])
        sd = s.sb("sd", [P, NB])
        (y_turned, added, stats, aggregated, rooted, inverted, normed, n_turned, head_kept, rest_kept, stored) = (
            s.sem(n) for n in ("y_turned", "added", "stats", "aggregated", "rooted", "inverted", "normed",
                               "n_turned", "head_kept", "rest_kept", "stored"))
        with nc.Block() as block:

            @block.sync
            def _(sp):
                for first in ahead[0:1]:
                    first(sp)
                if out is not None:
                    for g in range(NG):
                        sp.wait_ge(added, g + 1)
                        sp.dma_start(out[GB * g:GB * g + GB].rearrange("b s d -> s b d"),
                                     X[:, GB * g:GB * g + GB, :]).then_inc(stored, 16)
                    sp.wait_ge(stored, 16 * NG)

            @block.gpsimd
            def _(pool):
                for first in ahead[1:2]:
                    first(pool)

            @block.tensor
            def _(pe):
                lag = 2
                for g in range(NG + lag):
                    if g < NG and YT is not None:
                        wait(pe, added, g - 1)
                        for b in range(GB):
                            for c in range(CH):
                                last = nc.tensor.transpose(back[g % 2][:, b, c * P:(c + 1) * P],
                                                           YT[:, c, GB * g + b, :], ident[:, :])
                        last.then_inc(y_turned, 1)
                    if g >= lag and context is not None:
                        h = g - lag
                        C, c_in, _ = context
                        pe.wait_ge(c_in, 16)
                        wait(pe, c_kept, h - 1)
                        for b in range(GB):
                            for c in range(CH):
                                last = nc.tensor.transpose(back[h % 2][:, b, c * P:(c + 1) * P],
                                                           C[:, GB * h + b, c * P:(c + 1) * P], ident[:, :])
                        last.then_inc(c_turned, 1)
                    if g >= lag and norm:
                        h = g - lag
                        pe.wait_ge(normed, h + 1)
                        wait(pe, head_kept, h - 1)
                        wait(pe, rest_kept, h - 1 if XL is not None else 0)
                        for b in range(GB):
                            for c in range(CH):
                                last = nc.tensor.transpose(fore[h % 2][:, b, c, :], xn[:, h % 2, b, c * P:(c + 1) * P],
                                                           ident[:, :])
                        last.then_inc(n_turned, 1)

            @block.vector
            def _(dve):
                for g in range(NG + 2):
                    part = slice(GB * g, GB * g + GB)
                    if g < NG:
                        if YT is not None:
                            dve.wait_ge(y_turned, g + 1)
                            nc.vector.tensor_tensor(X[:, part, :], X[:, part, :], back[g % 2][:, :, :],
                                                    ALU.add).then_inc(added, 1)
                            dve.wait_ge(added, g + 1)
                        if x_in is not None:
                            dve.wait_ge(x_in[g], 16)
                        if norm:
                            for b in range(GB * g, GB * g + GB):
                                nc.vector.bn_stats(st[:, b, :], X[:, b, :]).then_inc(stats, 1)
                            dve.wait_ge(stats, GB * (g + 1))
                            for b in range(GB * g, GB * g + GB):
                                nc.vector.bn_aggr(mv[:, b, :], st[:, b, :]).then_inc(aggregated, 1)
                    if norm and 1 <= g <= NG:
                        h = g - 1
                        dve.wait_ge(rooted, h + 1)
                        nc.vector.reciprocal(sd[:, GB * h:GB * g], sd[:, GB * h:GB * g]).then_inc(inverted, 1)
                        dve.wait_ge(inverted, h + 1)
                        wait(dve, n_turned, h - 1)
                        for b in range(GB):
                            t = GB * h + b
                            last = nc.vector.tensor_scalar(xn[:, h % 2, b, :], X[:, t, :], mv[:, t, 0:1],
                                                           sd[:, t:t + 1], ALU.subtract, ALU.mult)
                        last.then_inc(normed, 1)
                    if XL is not None and g >= 2:
                        h = g - 2
                        dve.wait_ge(head_kept, h + 1)
                        nc.vector.tensor_tensor(
                            XL[:, :, GB * h:GB * h + GB, :], fore[h % 2][:, :, :, :].rearrange("p b c t -> p c b t"),
                            XH[:, :, GB * h:GB * h + GB, :].bitcast(F32), ALU.subtract).then_inc(rest_kept, 1)

            @block.scalar
            def _(act):
                if norm:
                    for g in range(NG + 1):
                        for first in ahead[2:3]:
                            first(g)
                        if g < NG:
                            act.wait_ge(aggregated, GB * (g + 1))
                            nc.scalar.activation(sd[:, GB * g:GB * g + GB], mv[:, GB * g:GB * g + GB, 1], ACT.Sqrt,
                                                 bias=eps[:, :]).then_inc(rooted, 1)
                        if g:
                            h = g - 1
                            act.wait_ge(n_turned, g)
                            to = XT if XH is None else XH
                            nc.scalar.activation(to[:, :, GB * h:GB * h + GB, :],
                                                 fore[h % 2][:, :, :, :].rearrange("p b c t -> p c b t"),
                                                 ACT.Copy).then_inc(head_kept, 1)
                        if g and context is not None:
                            h = g - 1
                            act.wait_ge(c_turned, g)
                            nc.scalar.activation(context[2][:, :, GB * h:GB * h + GB, :],
                                                 back[h % 2][:, :, :].rearrange("p b (c t) -> p c b t", c=CH),
                                                 ACT.Copy).then_inc(c_kept, 1)


def stage_attention(nc, codes_q, scales_q, bq, codes_k, scales_k, bk, codes_v, scales_v, bv, codes_o, scales_o, bo,
                    XH, XL, YT, ident, before):
    HEADS, DH, BLOCK = 16, 128, 32
    PAIRS, UNITS = HEADS // 2, 2 * NG
    KB = P // BLOCK
    PIECES, PW = 8, 2 * DH
    SCALE = float(DH) ** -0.5
    LAST = PAIRS * UNITS
    with ExitStack() as ctx:
        s = Space(nc, ctx, "attn")
        codes = s.sb("codes", [P, 2, PIECES, PW])
        scales = s.sb("scales", [P, 2, PIECES, PW])
        WH = s.sb("weight_head", [P, 2, PIECES, PW], F32R)
        WL = s.sb("weight_rest", [P, 2, PIECES, PW], F32R)
        bq_sb, bk_sb, bo_sb = s.sb("bq", [P, HEADS]), s.sb("bk", [P, HEADS]), s.sb("bo", [P, CH])
        bq_pair = s.sb("bq_pair", [P, 2, 2])
        bv_sb = s.sb("bv", [P, HEADS * DH])
        QT, KT, PR, PT = (s.sb(n, [P, 2, GB, T]) for n in ("queries", "keys", "probs", "probs_turned"))
        V = s.sb("values", [P, 2, GB, 2, DH])
        OH, OL = s.sb("heads_head", [P, 2, GT], F32R), s.sb("heads_rest", [P, 2, GT], F32R)
        NM, SM, RS = (s.sb(n, [P, 2, GB]) for n in ("neg_max", "sums", "inverse_sums"))
        (bias_in, biases_set, weight_whole, weight_head, weight_rest,
         v_made, q_made, k_made, s_made, t_made, o_made, out_made,
         v_kept, q_kept, k_kept, t_kept, oh_kept, ol_kept, y_kept,
         max_made, exp_made, inverse_made, probs_made) = (s.sem(n) for n in (
             "bias_in", "biases_set", "weight_whole", "weight_head", "weight_rest",
             "v_made", "q_made", "k_made", "s_made", "t_made", "o_made", "out_made",
             "v_kept", "q_kept", "k_kept", "t_kept", "oh_kept", "ol_kept", "y_kept",
             "max_made", "exp_made", "inverse_made", "probs_made"))
        bq_picked = s.sem("bq_picked")
        codes_in = [s.sem(f"codes_in{w}") for w in range(2)]

        def over_pairs(eng, body):
            body(0, 0)
            body(1, 1)
            with eng.Fori(1, PAIRS // 2) as i:
                body(2 * i, 0)
                body(2 * i + 1, 1)

        DMAS = 4 + 4 * KB
        def load(sp, pair, w):
            wait(sp, weight_rest, (pair - 1) * PIECES)
            cols = bass.ds(pair * PW, PW)
            for m, (code, scale) in enumerate(((codes_q, scales_q), (codes_k, scales_k), (codes_v, scales_v))):
                sp.dma_start(codes[:, w, 2 * m:2 * m + 2, :],
                             code.rearrange("(c p) f -> p c f", p=P)[:, :, cols]).then_inc(codes_in[w], 16)
                for k in range(KB):
                    sp.dma_start(scales[BLOCK * k:BLOCK * (k + 1), w, 2 * m:2 * m + 2, :],
                                 scale.rearrange("(c k) f -> k c f", k=KB)[k, :, cols]
                                 .partition_broadcast(BLOCK)).then_inc(codes_in[w], 16)
            sp.dma_start(codes[:, w, 6:8, :],
                         codes_o.rearrange("(a j p) f -> a p j f", j=2, p=P)[pair]).then_inc(codes_in[w], 16)
            for k in range(KB):
                sp.dma_start(scales[BLOCK * k:BLOCK * (k + 1), w, 6:8, :],
                             scales_o.rearrange("(a j k) f -> a k j f", j=2, k=KB)[pair, k]
                             .partition_broadcast(BLOCK)).then_inc(codes_in[w], 16)

        def whole(pool, pair, w, k):
            if k == 0:
                pool.wait_ge(codes_in[w], 8 * DMAS * (pair + 2 - w))
            nc.gpsimd.tensor_tensor(codes[:, w, k, :], codes[:, w, k, :], scales[:, w, k, :],
                                    ALU.mult).then_inc(weight_whole, 1)

        def rest(pool, pair, w, k):
            pool.wait_ge(weight_head, pair * PIECES + k + 1)
            nc.gpsimd.tensor_tensor(WL[:, w, k, :], codes[:, w, k, :], WH[:, w, k, :].bitcast(F32),
                                    ALU.subtract).then_inc(weight_rest, 1)

        def pieces(u):
            return ((0,), (1, 2), *((k,) for k in range(3, PIECES)), ())[u]

        def ahead_sync(sp):
            load(sp, 0, 0)
            sp.dma_start(bq_sb[:, :], bq).then_inc(bias_in, 16)
            sp.dma_start(bk_sb[:, :], bk).then_inc(bias_in, 16)
            sp.dma_start(bo_sb[:, :], bo).then_inc(bias_in, 16)
            sp.dma_start(bv_sb[:, :], bv.partition_broadcast(P)).then_inc(bias_in, 16)

        def ahead_pool(pool):
            for k in range(PIECES):
                whole(pool, 0, 0, k)
            for k in range(PIECES):
                rest(pool, 0, 0, k)

        def ahead_scalar(group):
            for k in {NG - 1: range(2), NG: range(2, PIECES)}.get(group, ()):
                nc.scalar.wait_ge(weight_whole, k + 1)
                nc.scalar.activation(WH[:, 0, k, :], codes[:, 0, k, :], ACT.Copy).then_inc(weight_head, 1)

        before((ahead_sync, ahead_pool, ahead_scalar))
        q_bank, k_bank, v_bank, s_bank, t_bank, o_bank = (
            s.ps(n, [P, GT]) for n in ("q_bank", "k_bank", "v_bank", "s_bank", "t_bank", "o_bank"))
        y_bank = s.ps("y_bank", [P, CH, GT])

        with nc.Block() as block:

            @block.sync
            def _(sp):
                load(sp, 1, 1)
                with sp.Fori(1, PAIRS // 2) as i:
                    load(sp, 2 * i, 0)
                    load(sp, 2 * i + 1, 1)

            @block.gpsimd
            def _(pool):
                def body(pair, w, more=True):
                    for u in range(UNITS):
                        n, j = pair * UNITS + u, u % 2
                        if more:
                            for k in pieces(u):
                                whole(pool, pair + 1, 1 - w, k)
                        pool.wait_ge(inverse_made, n + 1)
                        nc.gpsimd.tensor_tensor(PR[:, j, :, :], PR[:, j, :, :],
                                                RS[:, j, :].unsqueeze(2).to_broadcast([P, GB, T]),
                                                ALU.mult).then_inc(probs_made, 1)
                        if more:
                            for k in pieces(u):
                                rest(pool, pair + 1, 1 - w, k)

                body(0, 0)
                with pool.Fori(0, PAIRS // 2 - 1) as i:
                    body(2 * i + 1, 1)
                    body(2 * i + 2, 0)
                body(PAIRS - 1, 1, more=False)

            @block.tensor
            def _(pe):
                def product(out, a_head, a_rest, b_head, b_rest, first, last):
                    nc.tensor.matmul(out, a_head, b_head, start=first, stop=False)
                    nc.tensor.matmul(out, a_rest, b_head, start=False, stop=False)
                    return nc.tensor.matmul(out, a_head, b_rest, start=False, stop=last)

                def project_out(n, m, w, j):
                    wait(pe, oh_kept, n + 1)
                    wait(pe, ol_kept, n + 1)
                    if j == 0:
                        wait(pe, y_kept, m)
                    for c in range(CH):
                        cols = slice(c * P, (c + 1) * P)
                        last = product(y_bank[:, c, :], WH[:, w, 6 + j, cols], WL[:, w, 6 + j, cols],
                                       OH[:, j, :], OL[:, j, :], j == 0, j == 1)
                    last.then_inc(out_made, 1)

                def turn(n, j):
                    pe.wait_ge(probs_made, n + 1)
                    wait(pe, t_kept, n)
                    for b in range(GB):
                        last = nc.tensor.transpose(t_bank[:, b * T:(b + 1) * T], PR[:, j, b, :], ident[:, :])
                    last.then_inc(t_made, 1)

                def apply(n, g, j):
                    pe.wait_ge(t_kept, n + 1)
                    pe.wait_ge(v_kept, n + 2 - j)
                    wait(pe, ol_kept, n)
                    for b in range(GB):
                        last = nc.tensor.matmul(o_bank[:, b * T:(b + 1) * T], V[:, g % 2, b, j, :], PT[:, j, b, :],
                                                start=True, stop=True)
                    last.then_inc(o_made, 1)

                def body(pair, w):
                    pe.wait_ge(weight_head, (pair + 1) * PIECES)
                    pe.wait_ge(weight_rest, (pair + 1) * PIECES)
                    for u in range(UNITS):
                        n, g, j = pair * UNITS + u, u // 2, u % 2
                        whole = not (isinstance(pair, int) and pair == 0)
                        wait(pe, v_kept, n)
                        for k in range(2):
                            b = GB * g + 2 * j + k
                            for c in range(CH):
                                nc.tensor.matmul(v_bank[:, k * PW:(k + 1) * PW], XH[:, c, b, :], WH[:, w, 4 + c, :],
                                                 start=c == 0, stop=False)
                                nc.tensor.matmul(v_bank[:, k * PW:(k + 1) * PW], XL[:, c, b, :], WH[:, w, 4 + c, :],
                                                 start=False, stop=False)
                                last = nc.tensor.matmul(v_bank[:, k * PW:(k + 1) * PW], XH[:, c, b, :],
                                                        WL[:, w, 4 + c, :], start=False, stop=c == CH - 1)
                        last.then_inc(v_made, 1)
                        for bank, at, kept, made in ((q_bank, 0, q_kept, q_made), (k_bank, 2, k_kept, k_made)):
                            wait(pe, kept, n)
                            for c in range(CH):
                                cols = slice(j * DH, (j + 1) * DH)
                                last = product(bank[:, :], WH[:, w, at + c, cols], WL[:, w, at + c, cols],
                                               XH[:, c, GB * g:GB * g + GB, :], XL[:, c, GB * g:GB * g + GB, :],
                                               c == 0, c == CH - 1)
                            last.then_inc(made, 1)
                        if whole or u >= 2:
                            project_out(n - 2, pair * NG + u // 2 - 1, w if u >= 2 else 1 - w, j)
                        if whole or u >= 1:
                            turn(n - 1, 1 - j)
                        pe.wait_ge(q_kept, n + 1)
                        pe.wait_ge(k_kept, n + 1)
                        wait(pe, exp_made, n)
                        for b in range(GB):
                            last = nc.tensor.matmul(s_bank[:, b * T:(b + 1) * T], QT[:, j, b, :], KT[:, j, b, :],
                                                    start=True, stop=True)
                        last.then_inc(s_made, 1)
                        if whole or u >= 1:
                            apply(n - 1, (u - 1) % UNITS // 2, 1 - j)

                over_pairs(pe, body)
                project_out(LAST - 2, LAST // 2 - 1, 1, 0)
                turn(LAST - 1, 1)
                apply(LAST - 1, NG - 1, 1)
                project_out(LAST - 1, LAST // 2 - 1, 1, 1)

            @block.vector
            def _(dve):
                def head(pair, w, k):
                    dve.wait_ge(weight_whole, pair * PIECES + k + 1)
                    wait(dve, k_made, (pair - 1) * UNITS)
                    if k >= 6:
                        wait(dve, out_made, (pair - 1) * UNITS)
                    nc.vector.tensor_copy(WH[:, w, k, :], codes[:, w, k, :]).then_inc(weight_head, 1)

                def keep_out(n, m, g):
                    dve.wait_ge(out_made, n + 1)
                    wait(dve, y_kept, m)
                    nc.vector.tensor_tensor(YT[:, :, GB * g:GB * g + GB, :], YT[:, :, GB * g:GB * g + GB, :],
                                            y_bank[:, :, :].rearrange("p c (b t) -> p c b t", b=GB),
                                            ALU.add).then_inc(y_kept, 1)

                def rest_of_heads(n, j):
                    dve.wait_ge(oh_kept, n + 1)
                    wait(dve, out_made, n - 1)
                    nc.vector.tensor_tensor(OL[:, j, :], o_bank[:, :], OH[:, j, :].bitcast(F32),
                                            ALU.subtract).then_inc(ol_kept, 1)

                dve.wait_ge(bias_in, 64)
                nc.vector.tensor_scalar(bq_sb[:, :], bq_sb[:, :], SCALE, None, ALU.mult).then_inc(biases_set, 1)
                for c in range(CH):
                    nc.vector.tensor_copy(YT[:, c, :, :].rearrange("p b t -> p (b t)"),
                                          bo_sb[:, c:c + 1].to_broadcast([P, NB * T])).then_inc(biases_set, 1)
                dve.wait_ge(biases_set, 1 + CH)

                def body(pair, w, more=True):
                    for u in range(UNITS):
                        n, g, j = pair * UNITS + u, u // 2, u % 2
                        whole = not (isinstance(pair, int) and pair == 0)
                        dve.wait_ge(v_made, n + 1)
                        wait(dve, o_made, n - j - 2)
                        nc.vector.tensor_tensor(
                            V[:, g % 2, 2 * j:2 * j + 2, :, :].rearrange("p k a d -> p k (a d)"),
                            v_bank[:, :].rearrange("p (k f) -> p k f", k=2),
                            bv_sb[:, bass.ds(pair * PW, PW)].unsqueeze(1).to_broadcast([P, 2, PW]),
                            ALU.add).then_inc(v_kept, 1)
                        dve.wait_ge(k_made, n + 1)
                        wait(dve, s_made, n - 1)
                        nc.vector.tensor_scalar(KT[:, j, :, :], k_bank[:, :].rearrange("p (b t) -> p b t", b=GB),
                                                bk_sb[:, bass.ds(pair * 2 + j, 1)], None,
                                                ALU.add).then_inc(k_kept, 1)
                        if j == 1 and (whole or u >= 2):
                            keep_out(n - 2, pair * NG + g - 1, (g - 1) % NG)
                        dve.wait_ge(s_made, n + 1)
                        wait(dve, exp_made, n - 1)
                        nc.vector.tensor_reduce(NM[:, j, :], s_bank[:, :].rearrange("p (b t) -> p b t", b=GB),
                                                AX.X, ALU.max, negate=True).then_inc(max_made, 1)
                        if more:
                            for k in pieces(u):
                                head(pair + 1, 1 - w, k)
                        dve.wait_ge(exp_made, n + 1)
                        wait(dve, probs_made, n - 1)
                        nc.vector.reciprocal(RS[:, j, :], SM[:, j, :]).then_inc(inverse_made, 1)
                        if whole or u >= 1:
                            rest_of_heads(n - 1, 1 - j)

                body(0, 0)
                with dve.Fori(0, PAIRS // 2 - 1) as i:
                    body(2 * i + 1, 1)
                    body(2 * i + 2, 0)
                body(PAIRS - 1, 1, more=False)
                rest_of_heads(LAST - 1, 1)
                keep_out(LAST - 1, LAST // 2 - 1, NG - 1)

            @block.scalar
            def _(act):
                def keep_turned(n, j):
                    act.wait_ge(t_made, n + 1)
                    wait(act, o_made, n - 1)
                    nc.scalar.activation(PT[:, j, :, :], t_bank[:, :].rearrange("p (b t) -> p b t", b=GB),
                                         ACT.Copy).then_inc(t_kept, 1)

                def head_of_heads(n, j):
                    act.wait_ge(o_made, n + 1)
                    wait(act, out_made, n - 1)
                    nc.scalar.activation(OH[:, j, :], o_bank[:, :], ACT.Copy).then_inc(oh_kept, 1)

                act.wait_ge(biases_set, 1)

                def body(pair, w):
                    nc.scalar.activation(bq_pair[:, w, :], bq_sb[:, bass.ds(pair * 2, 2)], ACT.Copy).then_inc(bq_picked, 1)
                    act.wait_ge(bq_picked, pair + 1)
                    for u in range(UNITS):
                        n, j = pair * UNITS + u, u % 2
                        whole = not (isinstance(pair, int) and pair == 0)
                        act.wait_ge(q_made, n + 1)
                        wait(act, s_made, n - 1)
                        nc.scalar.activation(QT[:, j, :, :], q_bank[:, :].rearrange("p (b t) -> p b t", b=GB),
                                             ACT.Identity, bias=bq_pair[:, w, j:j + 1],
                                             scale=SCALE).then_inc(q_kept, 1)
                        if whole or u >= 1:
                            keep_turned(n - 1, 1 - j)
                        act.wait_ge(max_made, n + 1)
                        wait(act, t_made, n - 1)
                        wait(act, inverse_made, n - 1)
                        for b in range(GB):
                            last = nc.scalar.activation(PR[:, j, b, :], s_bank[:, b * T:(b + 1) * T], ACT.Exp,
                                                        bias=NM[:, j, b:b + 1], accum_out=SM[:, j, b:b + 1])
                        last.then_inc(exp_made, 1)
                        if whole or u >= 1:
                            head_of_heads(n - 1, 1 - j)

                over_pairs(act, body)
                keep_turned(LAST - 1, 1)
                head_of_heads(LAST - 1, 1)


def stage_wkv(nc, time_decay, time_first, XT, CT, YT):
    HALF = NB // 2
    N = HALF * T
    CHUNKS = CH * 2
    with ExitStack() as ctx:
        s = Space(nc, ctx, "wkv")
        w_sb, u_sb = s.sb("decay", [P, CH]), s.sb("first", [P, CH])
        decay = s.sb("decays", [P, CH, HALF, T])
        peak = s.sb("peak", [P, 2, N + 1])
        to_peak, e_old, e_new, y_old, y_new, value, spare = (
            s.sb(n, [P, 2, N]) for n in ("to_peak", "e_old", "e_new", "y_old", "y_new", "value", "spare"))
        num, den = s.sb("num", [P, 2, N + 1]), s.sb("den", [P, 2, N + 1])
        above, below, inverse = (s.sb(n, [P, 2, N]) for n in ("above", "below", "inverse"))
        (in_, w_set, ordered, peaked, old_made, new_made, forgot, top_made, y_new_made, y_old_made,
         carried, weighed, value_made, fresh_made, den_made, aged, below_made, guessed, corrected, divided) = (
            s.sem(n) for n in (
             "in", "w_set", "ordered", "peaked", "old_made", "new_made", "forgot", "top_made", "y_new_made",
             "y_old_made", "carried", "weighed", "value_made", "fresh_made", "den_made", "aged", "below_made",
             "guessed", "corrected", "divided"))

        def flat(tensor, k):
            h = k % 2
            return tensor[:, k // 2, HALF * h:HALF * h + HALF, :].rearrange("p b t -> p (b t)")

        def starts(buffer):
            return buffer.rearrange("p (b t) -> p b t", b=HALF)[:, :, 0]

        with nc.Block() as block:

            @block.sync
            def _(sp):
                sp.dma_start(w_sb[:, :], time_decay).then_inc(in_, 16)
                sp.dma_start(u_sb[:, :], time_first).then_inc(in_, 16)

            @block.scalar
            def _(act):
                act.wait_ge(in_, 32)
                nc.scalar.activation(w_sb[:, :], w_sb[:, :], ACT.Exp).then_inc(w_set, 1)
                def exponentials(k):
                    r = k % 2
                    act.wait_ge(forgot, k + 1)
                    nc.scalar.activation(e_old[:, r, :], e_old[:, r, :], ACT.Exp).then_inc(carried, 1)
                    act.wait_ge(new_made, k + 1)
                    nc.scalar.activation(e_new[:, r, :], e_new[:, r, :], ACT.Exp).then_inc(carried, 1)
                    act.wait_ge(y_new_made, k + 1)
                    nc.scalar.activation(y_new[:, r, :], y_new[:, r, :], ACT.Exp).then_inc(weighed, 1)
                    act.wait_ge(y_old_made, k + 1)
                    nc.scalar.activation(y_old[:, r, :], y_old[:, r, :], ACT.Exp).then_inc(weighed, 1)

                def guess(k):
                    r = k % 2
                    act.wait_ge(below_made, k + 1)
                    wait(act, divided, k - 1)
                    nc.scalar.activation(inverse[:, r, :], below[:, r, :], ACT.Ln).then_inc(guessed, 1)
                    act.wait_ge(guessed, 2 * k + 1)
                    nc.scalar.activation(inverse[:, r, :], inverse[:, r, :], ACT.Exp, scale=-1.0).then_inc(guessed, 1)

                for k in range(CHUNKS + 1):
                    if k < CHUNKS:
                        exponentials(k)
                    if k:
                        guess(k - 1)

            @block.gpsimd
            def _(pool):
                def newest(k):
                    r = k % 2
                    pool.wait_ge(peaked, k + 1)
                    wait(pool, below_made, k - 1)
                    nc.gpsimd.tensor_tensor(e_new[:, r, :], flat(XT, k), peak[:, r, 1:N + 1],
                                            ALU.subtract).then_inc(new_made, 1)

                def oldest(k):
                    r = k % 2
                    pool.wait_ge(top_made, k + 1)
                    nc.gpsimd.tensor_tensor(y_old[:, r, :], peak[:, r, 0:N], to_peak[:, r, :],
                                            ALU.subtract).then_inc(y_old_made, 1)

                def products(k):
                    r = k % 2
                    pool.wait_ge(carried, 2 * k + 2)
                    nc.gpsimd.tensor_tensor(value[:, r, :], e_new[:, r, :], flat(CT, k), ALU.mult).then_inc(value_made, 1)
                    pool.wait_ge(weighed, 2 * k + 2)
                    nc.gpsimd.tensor_tensor(spare[:, r, :], y_new[:, r, :], flat(CT, k), ALU.mult).then_inc(fresh_made, 1)

                def age(k):
                    r = k % 2
                    pool.wait_ge(den_made, k + 1)
                    pool.wait_ge(value_made, k + 1)
                    nc.gpsimd.tensor_tensor(e_new[:, r, :], y_old[:, r, :], den[:, r, 0:N], ALU.mult).then_inc(aged, 1)

                def correct(k):
                    r = k % 2
                    pool.wait_ge(guessed, 2 * k + 2)
                    nc.gpsimd.tensor_tensor(below[:, r, :], below[:, r, :], inverse[:, r, :],
                                            ALU.mult).then_inc(corrected, 1)

                for k in range(CHUNKS + 2):
                    if k < CHUNKS:
                        newest(k)
                    if 1 <= k <= CHUNKS:
                        products(k - 1)
                    if k < CHUNKS:
                        oldest(k)
                    if 1 <= k <= CHUNKS:
                        age(k - 1)
                    if k >= 2:
                        correct(k - 2)

            @block.vector
            def _(dve):
                step = Chain(dve, ordered)
                dve.wait_ge(w_set, 1)
                step(nc.vector.tensor_scalar(w_sb[:, :], w_sb[:, :], -1.0, None, ALU.mult))
                for c in range(CH):
                    step(nc.vector.tensor_copy(decay[:, c, :, :].rearrange("p b t -> p (b t)"),
                                               w_sb[:, c:c + 1].to_broadcast([P, N])))
                step(nc.vector.memset(decay[:, :, :, 0], FAR))
                for r in range(2):
                    nc.vector.memset(peak[:, r, 0:1], FAR)
                    nc.vector.memset(num[:, r, 0:1], 0.0)
                    step(nc.vector.memset(den[:, r, 0:1], 0.0))

                def peaks(k):
                    r, c = k % 2, k // 2
                    keys = flat(XT, k)
                    wait(dve, aged, k - 1)
                    nc.vector.tensor_tensor_scan(peak[:, r, 1:N + 1], decay[:, c, :, :].rearrange("p b t -> p (b t)"),
                                                 keys, FAR, ALU.add, ALU.max).then_inc(peaked, 1)
                    dve.wait_ge(peaked, k + 1)
                    nc.vector.scalar_tensor_tensor(e_old[:, r, :], peak[:, r, 0:N], w_sb[:, c:c + 1],
                                                   peak[:, r, 1:N + 1], ALU.add, ALU.subtract).then_inc(old_made, 1)

                def before_exp(k):
                    r, c = k % 2, k // 2
                    keys = flat(XT, k)
                    dve.wait_ge(old_made, k + 1)
                    dve.wait_ge(new_made, k + 1)
                    step(nc.vector.memset(starts(peak[:, r, 0:N]), FAR))
                    nc.vector.memset(starts(e_old[:, r, :]), FAR).then_inc(forgot, 1)
                    nc.vector.scalar_tensor_tensor(to_peak[:, r, :], keys, u_sb[:, c:c + 1], peak[:, r, 0:N],
                                                   ALU.add, ALU.max).then_inc(top_made, 1)
                    dve.wait_ge(top_made, k + 1)
                    nc.vector.scalar_tensor_tensor(y_new[:, r, :], keys, u_sb[:, c:c + 1], to_peak[:, r, :],
                                                   ALU.add, ALU.subtract).then_inc(y_new_made, 1)

                def after_exp(k):
                    r = k % 2
                    dve.wait_ge(carried, 2 * k + 2)
                    nc.vector.tensor_tensor_scan(den[:, r, 1:N + 1], e_old[:, r, :], e_new[:, r, :], 0.0,
                                                 ALU.mult, ALU.add).then_inc(den_made, 1)
                    dve.wait_ge(value_made, k + 1)
                    step(nc.vector.tensor_tensor_scan(num[:, r, 1:N + 1], e_old[:, r, :], value[:, r, :], 0.0,
                                                      ALU.mult, ALU.add))
                    dve.wait_ge(weighed, 2 * k + 2)
                    step(nc.vector.tensor_tensor(value[:, r, :], y_old[:, r, :], num[:, r, 0:N], ALU.mult))
                    dve.wait_ge(fresh_made, k + 1)
                    step(nc.vector.tensor_tensor(above[:, r, :], value[:, r, :], spare[:, r, :], ALU.add))
                    dve.wait_ge(aged, k + 1)
                    nc.vector.tensor_tensor(below[:, r, :], e_new[:, r, :], y_new[:, r, :],
                                            ALU.add).then_inc(below_made, 1)

                def divide(k):
                    r = k % 2
                    dve.wait_ge(corrected, k + 1)
                    step(nc.vector.scalar_tensor_tensor(below[:, r, :], below[:, r, :], 2.0, inverse[:, r, :],
                                                        ALU.subtract, ALU.mult))
                    nc.vector.scalar_tensor_tensor(flat(YT, k), above[:, r, :], -1.0, below[:, r, :],
                                                   ALU.mult, ALU.mult).then_inc(divided, 1)

                peaks(0)
                for k in range(CHUNKS + 2):
                    if k < CHUNKS:
                        before_exp(k)
                    if 1 <= k <= CHUNKS:
                        after_exp(k - 1)
                    if k + 1 < CHUNKS:
                        peaks(k + 1)
                    if k >= 2:
                        divide(k - 2)


def stage_ternary_ffn(nc, w1, b1, ln_g, ln_b, w2, b2, X, YT, ident, identb, eps, ones):
    H = 1024
    HC = H // P
    LEVELS = 127.0
    COUNT = float(H * D)
    with ExitStack() as ctx:
        s = Space(nc, ctx, "ffn")
        HB = s.sb("hidden", [P, NB, H])
        W1, W2 = s.sb("w1", [P, HC, D]), s.sb("w2", [P, CH, H])
        B1, B2, G, B = s.sb("b1", [P, H]), s.sb("b2", [P, D]), s.sb("gain", [P, H]), s.sb("shift", [P, H])
        Q1, Q2 = s.sb("w1_ternary", [P, HC, D], BF16), s.sb("w2_ternary", [P, CH, H], BF16)
        W1T, W2T = s.sb("w1_turned", [P, CH, H], BF16), s.sb("w2_turned", [P, HC, D], BF16)
        size, unit, scale = s.sb("size", [P, 2]), s.sb("unit", [P, 2]), s.sb("scale", [P, 2])
        st, mv = s.sb("st", [P, NB, 6]), s.sb("mv", [P, NB, 2])
        hst, hmv = s.sb("hst", [P, NB, 2, 6]), s.sb("hmv", [P, NB, 2])
        rstd, high, low, size1, fac1, dq1 = (s.sb(n, [P, NB]) for n in ("rstd", "high", "low", "size1", "fac1", "dq1"))
        hrstd, ssq, size2, fac2, dq2, root = (s.sb(n, [P, NB]) for n in ("hrstd", "ssq", "size2", "fac2", "dq2", "root"))
        steps = s.sb("steps", [P, 2, D])
        q = s.sb("q", [P, 2, D], BF16)
        qT = s.sb("q_turned", [P, 2, CH, T], BF16)
        wide, square = s.sb("wide", [P, H]), s.sb("square", [P, H])
        shift = s.sb("shift_by_mean", [P, NB])
        q2 = s.sb("q2", [P, 2, H], BF16)
        q2T = s.sb("q2_turned", [P, 2, HC, T], BF16)
        (in1, in2, in_rows, sized, ternary, turned, kept, rooted, step_done, rounded, q_turned, q_kept,
         z_made, z_kept, silu_done, gelu_done, stats, aggregated, residual_read, shifted, h_normed, squared, measured,
         widened, rounded2, q2_turned, q2_kept, y_made, y_kept) = (s.sem(n) for n in (
             "in1", "in2", "in_rows", "sized", "ternary", "turned", "kept", "rooted", "step", "rounded",
             "q_turned", "q_kept", "z_made", "z_kept", "silu", "gelu", "stats", "aggregated", "residual_read", "shifted",
             "h_normed", "squared", "measured", "widened", "rounded2", "q2_turned", "q2_kept", "y_made", "y_kept"))

        distance = HB[:, NB // 2:NB // 2 + NB * D // H, :].rearrange("p k (b d) -> p (k b) d", d=D)
        negated, apart, farthest_made = (s.sem(n) for n in ("negated", "apart", "farthest_made"))
        y_turned, y_added, w2_ternary, w2_turned, w2_kept, scaled, shift_made, centred, gained = (s.sem(n) for n in (
            "y_turned", "y_added", "w2_ternary", "w2_turned", "w2_kept", "scaled", "shift_made", "centred", "gained"))

        with ExitStack() as banks, nc.Block() as block:
            back = [banks.enter_context(nc.psum_tensor(f"ffn_back{k}", [P, GB, D], F32)) for k in range(2)]
            w_bank = [banks.enter_context(nc.psum_tensor(f"ffn_w_bank{k}", [P, H], BF16)) for k in range(CH)]
            sum_bank = banks.enter_context(nc.psum_tensor("ffn_sum_bank", [P, 2], F32))

            @block.sync
            def _(sp):
                sp.dma_start(W1[:, :, :], w1.rearrange("(o p) d -> p o d", p=P)).then_inc(in1, 16)
                sp.dma_start(W2[:, :, :], w2.rearrange("(o p) h -> p o h", p=P)).then_inc(in2, 16)
                for to, row in ((B1, b1), (B2, b2), (G, ln_g), (B, ln_b)):
                    sp.dma_start(to[:, :], row.partition_broadcast(P)).then_inc(in_rows, 16)
                sp.wait_ge(in_rows, 64)

            @block.scalar
            def _(act):
                act.wait_ge(in1, 16)
                nc.scalar.activation(HB[:, 0:2, :], W1[:, :, :].rearrange("p (k o) d -> p k (o d)", k=2), ACT.Abs,
                                     accum_out=size[:, 0:1]).then_inc(sized, 1)
                act.wait_ge(in2, 16)
                nc.scalar.activation(HB[:, 2:4, :], W2[:, :, :], ACT.Abs, accum_out=size[:, 1:2]).then_inc(sized, 1)
                for g in range(NG):
                    act.wait_ge(negated, g + 1)
                    for b in range(GB * g, GB * g + GB):
                        last = nc.scalar.activation(distance[:, b, :], X[:, b, :], ACT.Abs, bias=low[:, b:b + 1])
                    last.then_inc(apart, 1)
                for c in range(CH):
                    act.wait_ge(turned, 2 + c)
                    nc.scalar.activation(W1T[:, c, :], w_bank[c][:, :], ACT.Copy).then_inc(kept, 1)

            @block.tensor
            def _(pe):
                def turn_back(g):
                    wait(pe, y_added, g - 1)
                    for b in range(GB):
                        for c in range(CH):
                            last = nc.tensor.transpose(back[g % 2][:, b, c * P:(c + 1) * P], YT[:, c, GB * g + b, :],
                                                       ident[:, :])
                    last.then_inc(y_turned, 1)

                turn_back(0)
                turn_back(1)
                pe.wait_ge(sized, 2)
                nc.tensor.matmul(sum_bank[:, :], ones[:, :], size[:, :], start=True, stop=True).then_inc(turned, 1)
                turn_back(2)
                turn_back(3)
                pe.wait_ge(ternary, 1)
                for c in range(CH):
                    for o in range(HC):
                        last = nc.tensor.transpose(w_bank[c][:, o * P:(o + 1) * P], Q1[:, o, c * P:(c + 1) * P],
                                                   identb[:, :])
                    last.then_inc(turned, 1)

            @block.vector
            def _(dve):
                step = Chain(dve, step_done)

                def update(g):
                    part = slice(GB * g, GB * g + GB)
                    dve.wait_ge(y_turned, g + 1)
                    nc.vector.tensor_tensor(X[:, part, :], X[:, part, :], back[g % 2][:, :, :],
                                            ALU.add).then_inc(y_added, 1)
                    dve.wait_ge(y_added, g + 1)
                    for b in range(GB * g, GB * g + GB):
                        nc.vector.bn_stats(st[:, b, :], X[:, b, :]).then_inc(stats, 1)
                    dve.wait_ge(stats, GB * (g + 1))
                    for b in range(GB * g, GB * g + GB):
                        nc.vector.bn_aggr(mv[:, b, :], st[:, b, :]).then_inc(aggregated, 1)
                    dve.wait_ge(aggregated, GB * (g + 1))
                    nc.vector.tensor_scalar(low[:, part], mv[:, part, 0], -1.0, None, ALU.mult).then_inc(negated, 1)

                def farthest(g):
                    part = slice(GB * g, GB * g + GB)
                    dve.wait_ge(apart, g + 1)
                    nc.vector.tensor_reduce(size1[:, part], distance[:, part, :], AX.X, ALU.max).then_inc(farthest_made, 1)

                update(0)
                update(1)
                farthest(0)
                dve.wait_ge(turned, 1)
                step(nc.vector.tensor_scalar(unit[:, :], sum_bank[:, :], 1.0 / COUNT, 1e-5, ALU.mult, ALU.max))
                nc.vector.reciprocal(scale[:, :], unit[:, :]).then_inc(scaled, 1)
                dve.wait_ge(scaled, 1)
                step(nc.vector.tensor_scalar(W1[:, :, :], W1[:, :, :], scale[:, 0:1], ROUND, ALU.mult, ALU.add))
                step(nc.vector.tensor_scalar(W1[:, :, :], W1[:, :, :], ROUND, 1.0, ALU.subtract, ALU.min))
                nc.vector.tensor_scalar(Q1[:, :, :], W1[:, :, :], -1.0, None, ALU.max).then_inc(ternary, 1)
                update(2)
                farthest(1)
                update(3)
                farthest(2)
                farthest(3)

        with ExitStack() as banks, nc.Block() as block:
            turn_bank = [banks.enter_context(nc.psum_tensor(f"ffn_turn_bank{k}", [P, H], BF16)) for k in range(2)]
            z_bank = [banks.enter_context(nc.psum_tensor(f"ffn_z_bank{k}", [P, H], F32)) for k in range(2)]
            y_bank = [banks.enter_context(nc.psum_tensor(f"ffn_y_bank{k}", [P, D], F32)) for k in range(2)]

            def tiles(eng, body):
                body(0, 0)
                body(1, 1)
                with eng.Fori(1, NB // 2) as i:
                    body(2 * i, 0)
                    body(2 * i + 1, 1)

            def lagging(first, second):
                def body(n, r):
                    first(n, r)
                    if not (isinstance(n, int) and n == 0):
                        second(n - 1, 1 - r)
                return body

            def leading(first, second):
                def body(n, r):
                    first(n, r)
                    if not (isinstance(n, int) and n < 2):
                        second(n - 2, r)
                return body

            @block.vector
            def _(dve):
                step = Chain(dve, step_done)
                step.n = 1 + 2
                var = mv[:, :, 1]
                dve.wait_ge(rooted, 1)
                step(nc.vector.reciprocal(rstd[:, :], root[:, :]))
                step(nc.vector.tensor_tensor(low[:, :], var, rstd[:, :], ALU.mult))
                nc.vector.tensor_tensor(low[:, :], low[:, :], rstd[:, :], ALU.mult).then_inc(measured, 1)
                dve.wait_ge(rooted, 2)
                step(nc.vector.reciprocal(high[:, :], root[:, :]))
                step(nc.vector.tensor_tensor(rstd[:, :], rstd[:, :], high[:, :], ALU.mult))
                step(nc.vector.tensor_tensor(size1[:, :], size1[:, :], rstd[:, :], ALU.mult))
                step(nc.vector.tensor_scalar(dq1[:, :], size1[:, :], 1e-5, 1.0 / LEVELS, ALU.max, ALU.mult))
                step(nc.vector.reciprocal(fac1[:, :], dq1[:, :]))
                step(nc.vector.tensor_tensor(fac1[:, :], fac1[:, :], rstd[:, :], ALU.mult))
                step(nc.vector.tensor_scalar(dq1[:, :], dq1[:, :], unit[:, 0:1], None, ALU.mult))

                def quantise(n, r):
                    wait(dve, q_turned, n - 1)
                    nc.vector.tensor_scalar(steps[:, r, :], X[:, n, :], mv[:, n, 0:1], fac1[:, bass.ds(n, 1)],
                                            ALU.subtract, ALU.mult).then_inc(residual_read, 1)
                    dve.wait_ge(residual_read, n + 1)
                    nc.vector.tensor_scalar(q[:, r, :], steps[:, r, :], ROUND, ROUND,
                                            ALU.add, ALU.subtract).then_inc(rounded, 1)

                def dequantise(n, r):
                    dve.wait_ge(z_made, n + 1)
                    nc.vector.scalar_tensor_tensor(HB[:, n, :], z_bank[r][:, :], dq1[:, bass.ds(n, 1)], B1[:, :],
                                                   ALU.mult, ALU.add).then_inc(z_kept, 1)

                tiles(dve, leading(quantise, dequantise))
                dequantise(NB - 2, 0)
                dequantise(NB - 1, 1)

                def gather(n, r):
                    dve.wait_ge(gelu_done, n + 1)
                    for k in range(2):
                        nc.vector.bn_stats(hst[:, n, k, :], HB[:, n, k * H // 2:(k + 1) * H // 2]).then_inc(stats, 1)
                tiles(dve, gather)
                dve.wait_ge(stats, NB + 2 * NB)
                for b in range(NB):
                    nc.vector.bn_aggr(hmv[:, b, :], hst[:, b, :, :].rearrange("p k n -> p (k n)")).then_inc(aggregated, 1)
                dve.wait_ge(rooted, 3)
                step(nc.vector.reciprocal(hrstd[:, :], root[:, :]))
                nc.vector.scalar_tensor_tensor(shift[:, :], hmv[:, :, 0], -1.0, hrstd[:, :], ALU.mult,
                                               ALU.mult).then_inc(shift_made, 1)

                def normalise(n, r):
                    dve.wait_ge(gained, n + 1)
                    nc.vector.tensor_tensor(HB[:, n, :], HB[:, n, :], B[:, :], ALU.add).then_inc(h_normed, 1)
                    dve.wait_ge(h_normed, n + 1)
                    nc.vector.tensor_reduce(size2[:, bass.ds(n, 1)], HB[:, n, :], AX.X, ALU.max,
                                            apply_absolute_value=True).then_inc(measured, 1)
                tiles(dve, normalise)
                dve.wait_ge(measured, 1 + NB)
                dve.wait_ge(rooted, 4)
                step(nc.vector.reciprocal(hrstd[:, :], root[:, :]))
                step(nc.vector.tensor_tensor(size2[:, :], size2[:, :], hrstd[:, :], ALU.mult))
                step(nc.vector.tensor_scalar(dq2[:, :], size2[:, :], 1e-5, 1.0 / LEVELS, ALU.max, ALU.mult))
                step(nc.vector.reciprocal(fac2[:, :], dq2[:, :]))
                step(nc.vector.tensor_tensor(fac2[:, :], fac2[:, :], hrstd[:, :], ALU.mult))
                step(nc.vector.tensor_scalar(dq2[:, :], dq2[:, :], unit[:, 1:2], None, ALU.mult))
                dve.wait_ge(shifted, 1)

                def quantise2(n, r):
                    wait(dve, q2_turned, n - 1)
                    wait(dve, rounded2, n)
                    nc.vector.tensor_scalar(wide[:, :], HB[:, n, :], fac2[:, bass.ds(n, 1)], ROUND,
                                            ALU.mult, ALU.add).then_inc(widened, 1)
                    dve.wait_ge(widened, n + 1)
                    nc.vector.tensor_scalar(q2[:, r, :], wide[:, :], ROUND, None, ALU.subtract).then_inc(rounded2, 1)

                def add(n, r):
                    dve.wait_ge(y_made, n + 1)
                    nc.vector.scalar_tensor_tensor(X[:, n, :], y_bank[r][:, :], dq2[:, bass.ds(n, 1)], X[:, n, :],
                                                   ALU.mult, ALU.add).then_inc(y_kept, 1)

                tiles(dve, leading(quantise2, add))
                add(NB - 2, 0)
                add(NB - 1, 1)

            @block.gpsimd
            def _(pool):
                pool.wait_ge(scaled, 1)
                nc.gpsimd.tensor_scalar(W2[:, :, :], W2[:, :, :], scale[:, 1:2], ROUND, ALU.mult,
                                        ALU.add).then_inc(w2_ternary, 1)
                pool.wait_ge(w2_ternary, 1)
                nc.gpsimd.tensor_scalar(W2[:, :, :], W2[:, :, :], ROUND, 1.0, ALU.subtract,
                                        ALU.min).then_inc(w2_ternary, 1)
                pool.wait_ge(w2_ternary, 2)
                nc.gpsimd.tensor_scalar(Q2[:, :, :], W2[:, :, :], -1.0, None, ALU.max).then_inc(w2_ternary, 1)
                pool.wait_ge(residual_read, NB)
                nc.gpsimd.tensor_tensor(X[:, :, :], X[:, :, :], B2[:, :].unsqueeze(1).to_broadcast([P, NB, D]),
                                        ALU.add).then_inc(shifted, 1)
                for n in range(NB):
                    pool.wait_ge(centred, n + 1)
                    nc.gpsimd.tensor_tensor(HB[:, n, :], HB[:, n, :], G[:, :], ALU.mult).then_inc(gained, 1)

            @block.tensor
            def _(pe):
                def turn(n, r):
                    pe.wait_ge(rounded, n + 1)
                    wait(pe, q_kept, n - 1)
                    for c in range(CH):
                        last = nc.tensor.transpose(turn_bank[r][:, c * T:(c + 1) * T], q[:, r, c * P:(c + 1) * P],
                                                   identb[:, :])
                    last.then_inc(q_turned, 1)

                def up(n, r):
                    pe.wait_ge(q_kept, n + 1)
                    wait(pe, z_kept, n - 1)
                    for k in range(2):
                        cols = slice(k * H // 2, (k + 1) * H // 2)
                        for c in range(CH):
                            last = nc.tensor.matmul(z_bank[r][:, cols], qT[:, r, c, :], W1T[:, c, cols],
                                                    start=c == 0, stop=c == CH - 1)
                    last.then_inc(z_made, 1)

                def turn2(n, r):
                    pe.wait_ge(rounded2, n + 1)
                    wait(pe, q2_kept, n - 1)
                    for c in range(HC):
                        last = nc.tensor.transpose(turn_bank[r][:, c * T:(c + 1) * T], q2[:, r, c * P:(c + 1) * P],
                                                   identb[:, :])
                    last.then_inc(q2_turned, 1)

                def down(n, r):
                    pe.wait_ge(q2_kept, n + 1)
                    wait(pe, y_kept, n - 1)
                    for c in range(HC):
                        last = nc.tensor.matmul(y_bank[r][:, :], q2T[:, r, c, :], W2T[:, c, :],
                                                start=c == 0, stop=c == HC - 1)
                    last.then_inc(y_made, 1)

                tiles(pe, lagging(turn, up))
                up(NB - 1, 1)
                pe.wait_ge(q_kept, NB)
                pe.wait_ge(w2_ternary, 3)
                for o in range(CH):
                    for c in range(HC):
                        last = nc.tensor.transpose(turn_bank[o][:, c * P:(c + 1) * P], Q2[:, o, c * P:(c + 1) * P],
                                                   identb[:, :])
                    last.then_inc(w2_turned, 1)
                pe.wait_ge(w2_kept, CH)
                tiles(pe, lagging(turn2, down))
                down(NB - 1, 1)

            @block.scalar
            def _(act):
                act.wait_ge(aggregated, NB)
                nc.scalar.activation(root[:, :], mv[:, :, 1], ACT.Sqrt, bias=eps[:, :]).then_inc(rooted, 1)
                act.wait_ge(measured, 1)
                nc.scalar.activation(root[:, :], low[:, :], ACT.Sqrt, bias=eps[:, :]).then_inc(rooted, 1)

                def keep(n, r):
                    wait(act, z_made, n - 1)
                    act.wait_ge(q_turned, n + 1)
                    nc.scalar.activation(qT[:, r, :, :], turn_bank[r][:, 0:CH * T].rearrange("p (c t) -> p c t", c=CH),
                                         ACT.Copy).then_inc(q_kept, 1)

                def silu(n, r):
                    act.wait_ge(z_kept, n + 1)
                    act.wait_ge(rooted, 2)
                    nc.scalar.activation(HB[:, n, :], HB[:, n, :], ACT.Silu).then_inc(silu_done, 1)

                def gelu(n, r):
                    nc.scalar.activation(HB[:, n, :], HB[:, n, :], ACT.Gelu).then_inc(gelu_done, 1)

                tiles(act, lagging(keep, silu))
                silu(NB - 1, 1)
                for o in range(CH):
                    act.wait_ge(w2_turned, o + 1)
                    nc.scalar.activation(W2T[:, :, o * P:(o + 1) * P],
                                         turn_bank[o][:, :].rearrange("p (c o) -> p c o", c=HC),
                                         ACT.Copy).then_inc(w2_kept, 1)
                act.wait_ge(silu_done, NB)
                tiles(act, gelu)
                act.wait_ge(aggregated, 2 * NB)
                nc.scalar.activation(root[:, :], hmv[:, :, 1], ACT.Sqrt, bias=eps[:, :]).then_inc(rooted, 1)

                def centre(n):
                    nc.scalar.activation(HB[:, n, :], HB[:, n, :], ACT.Identity, bias=shift[:, n:n + 1],
                                         scale=hrstd[:, n:n + 1]).then_inc(centred, 1)

                def squares(n):
                    wait(act, squared, n)
                    act.wait_ge(h_normed, n + 1)
                    nc.scalar.activation(square[:, :], HB[:, n, :], ACT.Square,
                                         accum_out=ssq[:, n:n + 1]).then_inc(squared, 1)

                act.wait_ge(shift_made, 1)
                for n in range(NB + 3):
                    if n < NB:
                        centre(n)
                    if n >= 3:
                        squares(n - 3)
                act.wait_ge(squared, NB)
                nc.scalar.activation(root[:, :], ssq[:, :], ACT.Sqrt, bias=eps[:, :], scale=1.0 / H).then_inc(rooted, 1)

                def keep2(n, r):
                    wait(act, y_made, n - 1)
                    act.wait_ge(q2_turned, n + 1)
                    nc.scalar.activation(q2T[:, r, :, :], turn_bank[r][:, :].rearrange("p (c t) -> p c t", c=HC),
                                         ACT.Copy).then_inc(q2_kept, 1)
                tiles(act, keep2)


def stage_s6(nc, x_proj, dt_proj, dt_bias, A_log, D_skip, out_proj, out_bias, XT, YT, ident, before):
    STATES, RANK = 16, 128
    BC = 2 * STATES
    with ExitStack() as ctx:
        s = Space(nc, ctx, "s6")
        XP, XP2 = s.sb("x_proj", [RANK, D]), s.sb("x_proj_bc", [BC, D])
        DP, WO = s.sb("dt_proj", [P, CH, RANK]), s.sb("out_proj", [P, CH, D])
        DPT, WBC = s.sb("dt_proj_turned", [RANK, D]), s.sb("bc_turned", [P, CH, BC])
        WDT, WOT = s.sb("dt_weight", [P, CH, D]), s.sb("out_proj_turned", [P, CH, D])
        bias, ob, skip = s.sb("dt_bias", [P, CH]), s.sb("out_bias", [P, CH]), s.sb("skip", [P, CH])
        A = s.sb("a", [P, CH, STATES])
        delta, dx = s.sb("delta", [P, CH, NB, T]), s.sb("dx", [P, CH, NB, T])
        parts = s.sb("bc_parts", [2 * BC, NB * T], F32R)
        eye = s.sb("eye", [2 * BC, BC], F32R)
        (in_, turned, kept, a_made, step_done, dt_made, bc_made, sized, exped, head_kept, rest_kept, logged, summed,
         dx_made, cut) = (s.sem(n) for n in (
             "in", "turned", "kept", "a_made", "step", "dt_made", "bc_made", "sized", "exped", "head_kept",
             "rest_kept", "logged", "summed", "dx_made", "cut"))

        def ahead_sync(sp):
            for to, source in ((XP[:, :], x_proj[0:RANK, :]), (XP2[:, :], x_proj[RANK:RANK + BC, :]),
                               (DP[:, :, :], dt_proj.rearrange("(c p) r -> p c r", p=P)),
                               (WO[:, :, :], out_proj.rearrange("(c p) d -> p c d", p=P)),
                               (A[:, :, :], A_log.rearrange("(c p) n -> p c n", p=P)),
                               (bias[:, :], dt_bias), (ob[:, :], out_bias), (skip[:, :], D_skip)):
                sp.dma_start(to, source).then_inc(in_, 16)

        before((ahead_sync,))

        with ExitStack() as banks, nc.Block() as block:
            w_bank = [banks.enter_context(nc.psum_tensor(f"s6_w_bank{k}", [P, 512], F32)) for k in range(3)]
            dt_bank = [banks.enter_context(nc.psum_tensor(f"s6_dt_bank{k}", [P, CH, GT], F32)) for k in range(2)]
            bc_bank = [banks.enter_context(nc.psum_tensor("s6_bc_bank", [BC, GT], F32)), w_bank[0][0:BC, :]]
            positive = banks.enter_context(nc.sbuf_tensor("s6_positive", [P, NG, CH, GT], F32))

            def times_x(eng, arithmetic, g):
                here = slice(GB * g, GB * g + GB)
                eng.wait_ge(summed, g + 1)
                arithmetic.tensor_tensor(dx[:, :, here, :], delta[:, :, here, :], XT[:, :, here, :],
                                         ALU.mult).then_inc(dx_made, 1)

            @block.tensor
            def _(pe):
                pe.wait_ge(in_, 128)
                for c in range(CH):
                    nc.tensor.transpose(w_bank[0][:, c * P:(c + 1) * P], DP[:, c, :], ident[:, :])
                for c in range(CH):
                    last = nc.tensor.transpose(w_bank[0][:, D + c * BC:D + (c + 1) * BC], XP2[:, c * P:(c + 1) * P],
                                               ident[0:BC, 0:BC])
                last.then_inc(turned, 1)
                for o in range(CH):
                    for c in range(CH):
                        last = nc.tensor.transpose(w_bank[1][:, c * D + o * P:c * D + (o + 1) * P],
                                                   WO[:, o, c * P:(c + 1) * P], ident[:, :])
                last.then_inc(turned, 1)
                pe.wait_ge(kept, 1)
                for c in range(CH):
                    last = nc.tensor.matmul(w_bank[2][:, c * D:(c + 1) * D], XP[:, c * P:(c + 1) * P], DPT[:, :],
                                            start=True, stop=True)
                last.then_inc(turned, 1)
                pe.wait_ge(kept, 4)
                for g in range(NG):
                    wait(pe, sized, 2 * (g - 1))
                    wait(pe, cut, 2 * (g - 1))
                    for e in range(CH):
                        for c in range(CH):
                            last = nc.tensor.matmul(dt_bank[g % 2][:, e, :], WDT[:, c, e * P:(e + 1) * P],
                                                    XT[:, c, GB * g:GB * g + GB, :], start=c == 0, stop=c == CH - 1)
                    last.then_inc(dt_made, 1)
                for g in range(NG):
                    wait(pe, rest_kept, g - 1)
                    for c in range(CH):
                        last = nc.tensor.matmul(bc_bank[g % 2][:, :], WBC[:, c, :], XT[:, c, GB * g:GB * g + GB, :],
                                                start=c == 0, stop=c == CH - 1)
                    last.then_inc(bc_made, 1)

            @block.scalar
            def _(act):
                act.wait_ge(turned, 1)
                nc.scalar.activation(DPT[:, :], w_bank[0][:, 0:D], ACT.Copy).then_inc(kept, 1)
                nc.scalar.activation(WBC[:, :, :], w_bank[0][:, D:D + CH * BC].rearrange("p (c n) -> p c n", c=CH),
                                     ACT.Copy).then_inc(kept, 1)
                act.wait_ge(turned, 2)
                nc.scalar.activation(WOT[:, :, :], w_bank[1][:, :].rearrange("p (c d) -> p c d", c=CH),
                                     ACT.Copy).then_inc(kept, 1)
                act.wait_ge(turned, 3)
                nc.scalar.activation(WDT[:, :, :], w_bank[2][:, :].rearrange("p (c d) -> p c d", c=CH),
                                     ACT.Copy).then_inc(kept, 1)
                act.wait_ge(in_, 128)
                nc.scalar.activation(A[:, :, :], A[:, :, :], ACT.Exp).then_inc(a_made, 1)
                def keep_bc(g):
                    act.wait_ge(bc_made, g + 1)
                    nc.scalar.activation(parts[0:BC, g * GT:(g + 1) * GT], bc_bank[g % 2][:, :],
                                         ACT.Copy).then_inc(head_kept, 1)

                for first in range(0, NG, 2):
                    two = range(first, first + 2)
                    here = {g: delta[:, :, GB * g:GB * g + GB, :] for g in two}
                    for g in two:
                        act.wait_ge(dt_made, g + 1)
                        for c in range(CH):
                            nc.scalar.activation(here[g][:, c].rearrange("p b t -> p (b t)"), dt_bank[g % 2][:, c, :],
                                                 ACT.Abs, bias=bias[:, c:c + 1]).then_inc(sized, 1)
                    if first:
                        for g in range(first):
                            keep_bc(g)
                    for g in two:
                        act.wait_ge(sized, 2 * (g + 1))
                        nc.scalar.activation(here[g], here[g], ACT.Exp, scale=-1.0).then_inc(exped, 1)
                    for g in two:
                        act.wait_ge(exped, g + 1)
                        nc.scalar.activation(here[g], here[g], ACT.Ln, bias=1.0).then_inc(logged, 1)
                for g in range(NG - 2, NG):
                    keep_bc(g)

            @block.vector
            def _(dve):
                step = Chain(dve, step_done)
                dve.wait_ge(a_made, 1)
                step(nc.vector.tensor_scalar(A[:, :, :], A[:, :, :], -1.0, None, ALU.mult))
                for k in range(2):
                    step(nc.vector.tensor_copy(eye[k * BC:(k + 1) * BC, :],
                                               ident[k * BC:(k + 1) * BC, k * BC:(k + 1) * BC]))

                def above_zero(g):
                    dve.wait_ge(dt_made, g + 1)
                    dve.wait_ge(sized, 2 * (g + 1))
                    for c in range(CH):
                        nc.vector.tensor_scalar(positive[:, g, c, :], dt_bank[g % 2][:, c, :], bias[:, c:c + 1], 0.0,
                                                ALU.add, ALU.max).then_inc(cut, 1)

                def softplus_end(g):
                    here = slice(GB * g, GB * g + GB)
                    dve.wait_ge(logged, g + 1)
                    dve.wait_ge(cut, 2 * (g + 1))
                    nc.vector.tensor_tensor(delta[:, :, here, :], delta[:, :, here, :],
                                            positive[:, g, :, :].rearrange("p c (b t) -> p c b t", b=GB),
                                            ALU.add).then_inc(summed, 1)

                def rest_of_bc(g):
                    dve.wait_ge(head_kept, g + 1)
                    nc.vector.tensor_tensor(parts[BC:2 * BC, g * GT:(g + 1) * GT], bc_bank[g % 2][:, :],
                                            parts[0:BC, g * GT:(g + 1) * GT].bitcast(F32),
                                            ALU.subtract).then_inc(rest_kept, 1)

                for stage in (above_zero, softplus_end):
                    for g in range(2):
                        stage(g)
                for stage, groups in ((above_zero, (2, 3)), (rest_of_bc, (0, 1)), (softplus_end, (2, 3)),
                                      (rest_of_bc, (2, 3))):
                    for g in groups:
                        stage(g)
                times_x(dve, nc.vector, NG - 1)

            @block.gpsimd
            def _(pool):
                for g in range(NG - 1):
                    times_x(pool, nc.gpsimd, g)

        RING = 4
        UNITS = NG * STATES
        decay, u = (s.sb(n, [P, RING, CH, GT]) for n in ("decay", "u"))
        h, hc = (s.sb(n, [P, 2, CH, GT]) for n in ("h", "hc"))
        b_rows = s.sb("b_rows", [P, 2 * RING, GT])
        AHEAD = 3
        y, r = s.sb("y", [P, CH, GT]), s.sb("r", [P, CH, GT])
        (b_made, c_made, b_kept, decayed, cleared, u_made, scanned, weighed, y_made, y_kept, o_made, o_kept, added) = (
            s.sem(n) for n in ("b_made", "c_made", "b_kept", "decayed", "cleared", "u_made", "scanned", "weighed",
                               "y_made", "y_kept", "o_made", "o_kept", "added"))
        b_bank = [s.ps(f"b_bank{k}", [P, GT]) for k in range(2)]
        c_bank = [s.ps(f"c_bank{k}", [P, GT]) for k in range(2)]
        y_bank, o_bank = s.ps("y_bank", [P, CH, GT]), s.ps("o_bank", [P, CH, GT])

        with nc.Block() as block:

            @block.tensor
            def _(pe):
                def spread(k, first, bank, free, made):
                    g, n = k // STATES, k % STATES
                    wait(pe, free, k - 1)
                    nc.tensor.matmul(bank[n % 2][:, :], eye[:, first + n:first + n + 1].to_broadcast([2 * BC, P]),
                                     parts[:, g * GT:(g + 1) * GT], start=True, stop=True).then_inc(made, 1)

                def sum_states(n, k):
                    pe.wait_ge(weighed, k + 1)
                    for c in range(CH):
                        last = nc.tensor.matmul(y_bank[:, c, :], ident[:, :], hc[:, n % 2, c, :],
                                                start=n == 0, stop=n == STATES - 1)
                    last.then_inc(y_made, 1)

                def project(g):
                    pe.wait_ge(y_kept, g + 1)
                    wait(pe, o_kept, g)
                    for e in range(CH):
                        for c in range(CH):
                            last = nc.tensor.matmul(o_bank[:, e, :], WOT[:, c, e * P:(e + 1) * P], y[:, c, :],
                                                    start=c == 0, stop=c == CH - 1)
                    last.then_inc(o_made, 1)

                for k in range(-AHEAD - 1, UNITS):
                    if k + AHEAD + 1 < UNITS:
                        spread(k + AHEAD + 1, 0, b_bank, b_kept, b_made)
                    if 0 <= k + 1 < UNITS:
                        spread(k + 1, STATES, c_bank, weighed, c_made)
                    if k >= 0:
                        g, n = k // STATES, k % STATES
                        if n == 0:
                            wait(pe, y_kept, g)
                        sum_states(n, k)
                        if n == 1 and g:
                            project(g - 1)
                project(NG - 1)

            @block.scalar
            def _(act):
                def keep_y(g):
                    wait(act, o_made, g)
                    act.wait_ge(y_made, (g + 1) * STATES)
                    nc.scalar.activation(y[:, :, :], y_bank[:, :, :], ACT.Copy).then_inc(y_kept, 1)

                def relu(g):
                    wait(act, added, g)
                    act.wait_ge(o_made, g + 1)
                    for e in range(CH):
                        last = nc.scalar.activation(r[:, e, :], o_bank[:, e, :], ACT.Relu, bias=ob[:, e:e + 1])
                    last.then_inc(o_kept, 1)

                def keep_b(k):
                    act.wait_ge(b_made, k + 1)
                    wait(act, u_made, k - 2 * RING + 1)
                    nc.scalar.activation(b_rows[:, k % (2 * RING), :], b_bank[k % 2][:, :], ACT.Copy).then_inc(b_kept, 1)

                act.wait_ge(cleared, 1)
                for k in range(UNITS):
                    g, n = k // STATES, k % STATES
                    keep_b(k)
                    wait(act, scanned, k - RING + 1)
                    for c in range(CH):
                        last = nc.scalar.activation(
                            decay[:, k % RING, c, :].rearrange("p (b t) -> p b t", b=GB)[:, :, 1:T],
                            delta[:, c, GB * g:GB * g + GB, 1:T], ACT.Exp, scale=A[:, c, n:n + 1])
                    last.then_inc(decayed, 1)
                    if n == 6 and g:
                        relu(g - 1)
                    if n == 2 and g:
                        keep_y(g - 1)
                keep_y(NG - 1)
                relu(NG - 1)

            @block.gpsimd
            def _(pool):
                pool.memset(decay[:, :, :, :].rearrange("p r c (b t) -> p (r c b) t", b=GB)[:, :, 0:1],
                            0.0).then_inc(cleared, 1)

                def body(g):
                    for n in range(STATES):
                        k = g * STATES + n
                        wait(pool, scanned, k - RING + 1)
                        pool.wait_ge(b_kept, k + 1)
                        pool.wait_ge(cleared, 1)
                        nc.gpsimd.tensor_tensor(
                            u[:, n % RING, :, :].rearrange("p c (b t) -> p c b t", b=GB),
                            dx[:, :, bass.ds(g * GB, GB), :],
                            b_rows[:, n % (2 * RING), :].rearrange("p (b t) -> p b t", b=GB).unsqueeze(1)
                            .to_broadcast([P, CH, GB, T]), ALU.mult).then_inc(u_made, 1)
                for g in range(NG):
                    body(g)

            @block.vector
            def _(dve):
                def finish(g):
                    dve.wait_ge(o_kept, g + 1)
                    here = bass.ds(g * GB, GB)
                    for c in range(CH):
                        last = nc.vector.scalar_tensor_tensor(
                            YT[:, c, here, :], XT[:, c, here, :], skip[:, c:c + 1],
                            r[:, c, :].rearrange("p (b t) -> p b t", b=GB), ALU.mult, ALU.add)
                    last.then_inc(added, 1)

                def body(g):
                    for n in range(STATES):
                        k = g * STATES + n
                        dve.wait_ge(decayed, k + 1)
                        dve.wait_ge(u_made, k + 1)
                        wait(dve, weighed, k - 1)
                        nc.vector.tensor_tensor_scan(
                            h[:, n % 2, :, :].rearrange("p c t -> p (c t)"),
                            decay[:, n % RING, :, :].rearrange("p c t -> p (c t)"),
                            u[:, n % RING, :, :].rearrange("p c t -> p (c t)"), 0.0, ALU.mult, ALU.add).then_inc(scanned, 1)
                        dve.wait_ge(scanned, k + 1)
                        dve.wait_ge(c_made, k + 1)
                        wait(dve, y_made, k - 1)
                        nc.vector.tensor_tensor(hc[:, n % 2, :, :], h[:, n % 2, :, :],
                                                c_bank[n % 2][:, :].unsqueeze(1).to_broadcast([P, CH, GT]),
                                                ALU.mult).then_inc(weighed, 1)
                        if n == 8 and g:
                            finish(g - 1)

                for g in range(NG):
                    body(g)
                finish(NG - 1)


def stage_long_conv(nc, kernels, D_skip, XT, CT, YT, anti, ident, before):
    HD = 8
    HEADS = T // HD
    PAIRS = HD * (HD + 1) // 2
    QB = 4
    QUARTERS = NB // QB
    STEPS = CH * QUARTERS
    SHARED = HD - 2
    at = [d * HD - d * (d - 1) // 2 for d in range(HD)]
    with ExitStack() as ctx:
        s = Space(nc, ctx, "conv")
        hankel = s.sb("hankel", [P, HEADS, D])
        toeplitz = s.sb("toeplitz", [P, HEADS, D])
        skip = s.sb("skip", [P, HEADS])
        kv = s.sb("kv", [P, CH, NB, HEADS, PAIRS])
        kv_rows = [kv[:, c, :, :, :].rearrange("p b h n -> p (b h) n") for c in range(CH)]
        xt_rows = [XT[:, c, :, :].rearrange("p b (h i) -> p (b h) i", i=HD) for c in range(CH)]
        ct_rows = [CT[:, c, :, :].rearrange("p b (h i) -> p (b h) i", i=HD) for c in range(CH)]
        yt_rows = [YT[:, c, :, :].rearrange("p b (h j) -> p (b h) j", j=HD) for c in range(CH)]
        AHEAD = 2
        paired = [s.sem(f"paired{k}") for k in range(QUARTERS)]
        in_, flipped, ready, made, kept, query_old, query_new, summed = (
            s.sem(n) for n in ("in", "flipped", "ready", "made", "kept", "query_old", "query_new", "summed"))
        UNITS = QUARTERS * HEADS
        FLIPS = HEADS // 4

        def pair_up(eng, quarter):
            rows = slice(quarter * QB * HEADS, (quarter + 1) * QB * HEADS)
            for c in range(CH):
                for d in range(HD):
                    last = eng.tensor_tensor(kv_rows[c][:, rows, at[d]:at[d] + HD - d],
                                             ct_rows[c][:, rows, 0:HD - d], ct_rows[c][:, rows, d:HD], ALU.mult)
            last.then_inc(paired[quarter], 1)

        def ahead_sync(sp):
            sp.dma_start(hankel[:, :, :], bass.AP(tensor=kernels.tensor, offset=1,
                                                  ap=[[1, P], [P + D, HEADS], [1, D]])).then_inc(in_, 16)
            sp.dma_start(skip[:, :], D_skip.partition_broadcast(P)).then_inc(in_, 16)

        def ahead_pool(pool):
            for quarter in range(AHEAD):
                pair_up(nc.gpsimd, quarter)

        before((ahead_sync, ahead_pool))
        weighed = s.sb("weighed", [P, 2, QB * HEADS, HD, HD])
        bank = [s.ps(f"bank{k}", [P, 2, 512]) for k in range(4)]

        with nc.Block() as block:

            @block.tensor
            def _(pe):
                pe.wait_ge(in_, 32)
                for k in range(FLIPS):
                    wait(pe, ready, 4 * (k - 3))
                    for j in range(2):
                        last = nc.tensor.matmul(bank[k % 4][:, j, :], anti[:, :],
                                                hankel[:, 4 * k + 2 * j:4 * k + 2 * j + 2, :], start=True, stop=True)
                    last.then_inc(flipped, 1)
                for unit in range(UNITS):
                    quarter, h = unit // HEADS, unit % HEADS
                    if unit < FLIPS:
                        pe.wait_ge(ready, 4 * (unit + 1))
                    pe.wait_ge(paired[quarter], 1)
                    wait(pe, kept, unit - 3)
                    here = slice(QB * quarter, QB * quarter + QB)
                    out = bank[unit % 4]
                    low, high = kv[:, 0, here, h, :], kv[:, 1, here, h, :]
                    n = QB * PAIRS
                    nc.tensor.matmul(out[:, 0, 0:n], toeplitz[:, h, 0:P], low, start=True, stop=True)
                    nc.tensor.matmul(out[:, 1, 0:n], toeplitz[:, h, P:D], low, start=True, stop=False)
                    nc.tensor.matmul(out[:, 1, 0:n], toeplitz[:, h, 0:P], high, start=False, stop=True).then_inc(made, 1)

            @block.scalar
            def _(act):
                for unit in range(UNITS):
                    quarter, h = unit // HEADS, unit % HEADS
                    act.wait_ge(made, unit + 1)
                    nc.scalar.activation(
                        kv[:, :, QB * quarter:QB * quarter + QB, h, :],
                        bank[unit % 4][:, :, 0:QB * PAIRS].rearrange("p c (b n) -> p c b n", b=QB),
                        ACT.Copy).then_inc(kept, 1)

            def step_of(k):
                quarter, c = k // CH, k % CH
                return c, slice(QB * HEADS * quarter, QB * HEADS * (quarter + 1)), HEADS * (quarter + 1)

            def weigh(eng, k, c, rows, d, query):
                out = weighed[:, k % 2, :, d - query:HD - query, query:HD - d + query]
                diagonal = bass.AP(tensor=out.tensor, offset=out.offset, ap=[out.ap[0], out.ap[1], [HD + 1, HD - d]])
                return eng.tensor_tensor(diagonal, kv_rows[c][:, rows, at[d]:at[d] + HD - d],
                                         xt_rows[c][:, rows, query:HD - d + query], ALU.mult)

            @block.vector
            def _(dve):
                dve.wait_ge(in_, 32)
                for k in range(FLIPS):
                    dve.wait_ge(flipped, k + 1)
                    for h in range(4 * k, 4 * k + 4):
                        source = bank[k % 4][:, (h % 4) // 2, (h % 2) * D:(h % 2 + 1) * D]
                        nc.vector.tensor_copy(toeplitz[:, h, P:D], source[:, P:D])
                        nc.vector.scalar_tensor_tensor(toeplitz[:, h, 0:P], ident[:, :], skip[:, h:h + 1],
                                                       source[:, 0:P], ALU.mult, ALU.add).then_inc(ready, 1)
                for quarter in range(AHEAD, QUARTERS - 1):
                    pair_up(nc.vector, quarter)
                for k in range(STEPS):
                    c, rows, units = step_of(k)
                    dve.wait_ge(kept, units)
                    for d in range(1, SHARED):
                        last = weigh(nc.vector, k, c, rows, d, 0)
                    last.then_inc(query_old, 1)
                    dve.wait_ge(query_old, k + 1)
                    dve.wait_ge(query_new, k + 1)
                    nc.vector.tensor_reduce(yt_rows[c][:, rows, :], weighed[:, k % 2, :, :, :], AX.X,
                                            ALU.add).then_inc(summed, 1)

            @block.gpsimd
            def _(pool):
                pair_up(nc.gpsimd, QUARTERS - 1)
                for k in range(STEPS):
                    c, rows, units = step_of(k)
                    pool.wait_ge(kept, units)
                    wait(pool, summed, k - 1)
                    for d in range(HD):
                        last = weigh(nc.gpsimd, k, c, rows, d, d)
                    for d in range(SHARED, HD):
                        last = weigh(nc.gpsimd, k, c, rows, d, 0)
                    last.then_inc(query_new, 1)


def stage_experts(nc, gate_w, up_gate, up_value, down, rows_of, XH, XL, YT, ident, before):
    EXPERTS, TOP, ROWS = 16, 4, 32
    UNUSED, CHOSEN = -1.0, -2.0
    TILES, BLOCKS = 5, 5
    UNITS = NG * TILES
    BH = TILES * P
    UP, VALUE, DOWN, WIDTH = 0, CH * BH, 2 * CH * BH, 2 * CH * BH + TILES * D
    PIECES = 16
    PW = WIDTH // PIECES
    LAST = BLOCKS * UNITS
    with ExitStack() as ctx:
        s = Space(nc, ctx, "moe")
        raw, raw_rows = s.sb("raw", [P, WIDTH]), s.sb("raw_rows", [2 * ROWS, BH])
        WH, WL = s.sb("weight_head", [P, 2, WIDTH], F32R), s.sb("weight_rest", [P, 2, WIDTH], F32R)
        pick = s.sb("pick", [2 * ROWS, 2, BH], F32R)
        parts = s.sb("combine_parts", [2 * ROWS, NB * T], F32R)
        weights_in, rows_in, rows_set, head_set, rest_set = (
            s.sem(n) for n in ("weights_in", "rows_in", "rows_set", "head_set", "rest_set"))

        def load(sp, block):
            wait(sp, rest_set, block * PIECES)
            wait(sp, rows_set, block)
            cols = bass.ds(block * BH, BH)
            for at, source in ((UP, up_gate), (VALUE, up_value)):
                sp.dma_start(raw[:, at:at + CH * BH].rearrange("p (c f) -> p c f", c=CH),
                             source.rearrange("(c p) f -> p c f", p=P)[:, :, cols]).then_inc(weights_in, 16)
            sp.dma_start(raw[:, DOWN:WIDTH].rearrange("p (t f) -> p t f", t=TILES),
                         down.rearrange("(a t p) f -> a p t f", t=TILES, p=P)[block]).then_inc(weights_in, 16)
            for k in range(2):
                sp.dma_start(raw_rows[k * ROWS:(k + 1) * ROWS, :], rows_of[:, cols]).then_inc(rows_in, 16)

        def set_rows(act, block, w):
            act.wait_ge(rows_in, 32 * (block + 1))
            nc.scalar.activation(pick[:, w, :], raw_rows[:, :], ACT.Copy).then_inc(rows_set, 1)

        def set_head(act, block, w, k):
            act.wait_ge(weights_in, 48 * (block + 1))
            nc.scalar.activation(WH[:, w, k * PW:(k + 1) * PW], raw[:, k * PW:(k + 1) * PW],
                                 ACT.Copy).then_inc(head_set, 1)

        def set_rest(pool, block, w, k):
            pool.wait_ge(head_set, block * PIECES + k + 1)
            nc.gpsimd.tensor_tensor(WL[:, w, k * PW:(k + 1) * PW], raw[:, k * PW:(k + 1) * PW],
                                    WH[:, w, k * PW:(k + 1) * PW].bitcast(F32), ALU.subtract).then_inc(rest_set, 1)

        gw, gate_in = s.sb("gate_w", [EXPERTS, D]), s.sem("gate_in")

        def ahead_sync(sp):
            sp.dma_start(gw[:, :], gate_w).then_inc(gate_in, 16)
            load(sp, 0)

        before((ahead_sync,))
        with ExitStack() as part, nc.Block() as block:
            def sb(name, shape, dt=F32):
                return part.enter_context(nc.sbuf_tensor(f"moe_{name}", shape, dt))

            gh, gl = sb("gate_head", [P, CH, EXPERTS], F32R), sb("gate_rest", [P, CH, EXPERTS], F32R)
            padded, replaced = sb("score", [P, NB, EXPERTS + 8 - TOP]), sb("replaced", [P, NB, EXPERTS + 8 - TOP])
            score, top = padded[:, :, 0:EXPERTS], sb("top", [P, NB, 8])
            chosen, logits = sb("chosen", [P, NB, ROWS]), sb("logits", [EXPERTS, NG, GT])
            row, row2, row3 = sb("row", [P, NB]), sb("row2", [P, NB]), sb("row3", [P, NB])
            g_bank = part.enter_context(nc.psum_tensor("moe_g_bank", [P, CH * EXPERTS], F32))
            e_bank = [part.enter_context(nc.psum_tensor(f"moe_e_bank{k}", [EXPERTS, GT], F32)) for k in range(2)]
            l_bank = part.enter_context(nc.psum_tensor("moe_l_bank", [P, NB, EXPERTS], F32))
            c_bank = [part.enter_context(nc.psum_tensor(f"moe_c_bank{k}", [ROWS, GT], F32)) for k in range(NG)]
            gate_turned, gate_kept, logits_made, step_done, shifted, exped, by_expert, e_kept, ranked, combined, turned, split = (
                s.sem(n) for n in ("gate_turned", "gate_kept", "logits_made", "step", "shifted", "exped",
                                   "by_expert", "e_kept", "ranked", "combined", "turned", "split"))

            @block.gpsimd
            def _(pool):
                for k in range(PIECES):
                    set_rest(pool, 0, 0, k)

            @block.tensor
            def _(pe):
                pe.wait_ge(gate_in, 16)
                for c in range(CH):
                    last = nc.tensor.transpose(g_bank[:, c * EXPERTS:(c + 1) * EXPERTS], gw[:, c * P:(c + 1) * P],
                                               ident[0:EXPERTS, 0:EXPERTS])
                last.then_inc(gate_turned, 1)
                pe.wait_ge(gate_kept, 2)
                for g in range(NG):
                    wait(pe, e_kept, g - 1)
                    here = slice(GB * g, GB * g + GB)
                    for c in range(CH):
                        nc.tensor.matmul(e_bank[g % 2][:, :], gh[:, c, :], XH[:, c, here, :], start=c == 0, stop=False)
                        nc.tensor.matmul(e_bank[g % 2][:, :], gh[:, c, :], XL[:, c, here, :], start=False, stop=False)
                        last = nc.tensor.matmul(e_bank[g % 2][:, :], gl[:, c, :], XH[:, c, here, :],
                                                start=False, stop=c == CH - 1)
                    last.then_inc(by_expert, 1)
                for g in range(NG):
                    pe.wait_ge(e_kept, g + 1)
                    for b in range(GB):
                        last = nc.tensor.transpose(l_bank[:, GB * g + b, :], logits[:, g, b * T:(b + 1) * T],
                                                   ident[0:EXPERTS, 0:EXPERTS])
                last.then_inc(logits_made, 1)
                pe.wait_ge(combined, 1)
                for g in range(NG):
                    for b in range(GB):
                        last = nc.tensor.transpose(c_bank[g][:, b * T:(b + 1) * T], chosen[:, GB * g + b, :], ident[:, :])
                    last.then_inc(turned, 1)

            @block.scalar
            def _(act):
                act.wait_ge(gate_turned, 1)
                nc.scalar.activation(gh[:, :, :], g_bank[:, :].rearrange("p (c e) -> p c e", c=CH),
                                     ACT.Copy).then_inc(gate_kept, 1)
                for g in range(NG):
                    act.wait_ge(by_expert, g + 1)
                    nc.scalar.activation(logits[:, g, :], e_bank[g % 2][:, :], ACT.Copy).then_inc(e_kept, 1)
                set_rows(act, 0, 0)
                for k in range(2):
                    set_head(act, 0, 0, k)
                act.wait_ge(shifted, 1)
                nc.scalar.activation(score, score, ACT.Exp).then_inc(exped, 1)
                for k in range(2, PIECES):
                    set_head(act, 0, 0, k)
                for g in range(NG):
                    act.wait_ge(turned, g + 1)
                    nc.scalar.activation(parts[0:ROWS, g * GT:(g + 1) * GT], c_bank[g][:, :], ACT.Copy).then_inc(split, 1)

            @block.vector
            def _(dve):
                step = Chain(dve, step_done)
                dve.wait_ge(gate_kept, 1)
                nc.vector.tensor_tensor(gl[:, :, :], g_bank[:, :].rearrange("p (c e) -> p c e", c=CH),
                                        gh[:, :, :].bitcast(F32), ALU.subtract).then_inc(gate_kept, 1)
                wide = [P, NB, EXPERTS]
                nc.vector.memset(padded[:, :, EXPERTS:], UNUSED)
                nc.vector.memset(chosen[:, :, EXPERTS + 1:ROWS], 0.0)
                step(nc.vector.memset(chosen[:, :, EXPERTS:EXPERTS + 1], 1.0))
                dve.wait_ge(logits_made, 1)
                step(nc.vector.tensor_reduce(row[:, :], l_bank[:, :, :], AX.X, ALU.max))
                nc.vector.tensor_tensor(score, l_bank[:, :, :], row[:, :].unsqueeze(2).to_broadcast(wide),
                                        ALU.subtract).then_inc(shifted, 1)
                dve.wait_ge(exped, 1)
                step(nc.vector.tensor_reduce(row2[:, :], score, AX.X, ALU.add))
                step(nc.vector.reciprocal(row2[:, :], row2[:, :]))
                step(nc.vector.tensor_tensor(score, score, row2[:, :].unsqueeze(2).to_broadcast(wide),
                                             ALU.mult))
                for b in range(NB):
                    nc.vector.max(top[:, b, :], padded[:, b, 0:EXPERTS]).then_inc(ranked, 1)
                dve.wait_ge(ranked, NB)
                step(nc.vector.memset(top[:, :, TOP:8], UNUSED))
                for b in range(NB):
                    nc.vector.match_replace(replaced[:, b, :], top[:, b, :], padded[:, b, :], CHOSEN).then_inc(ranked, 1)
                dve.wait_ge(ranked, 2 * NB)
                step(nc.vector.scalar_tensor_tensor(score, replaced[:, :, 0:EXPERTS], CHOSEN, score,
                                                    ALU.is_equal, ALU.mult))
                step(nc.vector.tensor_reduce(row3[:, :], score, AX.X, ALU.add))
                step(nc.vector.reciprocal(row3[:, :], row3[:, :]))
                nc.vector.tensor_tensor(chosen[:, :, 0:EXPERTS], score,
                                        row3[:, :].unsqueeze(2).to_broadcast(wide), ALU.mult).then_inc(combined, 1)
                for g in range(NG):
                    dve.wait_ge(split, g + 1)
                    nc.vector.tensor_tensor(parts[ROWS:2 * ROWS, g * GT:(g + 1) * GT], c_bank[g][:, :],
                                            parts[0:ROWS, g * GT:(g + 1) * GT].bitcast(F32), ALU.subtract)

        silu, scaled, hidden = (s.sb(n, [P, 2, GT]) for n in ("silu", "scaled", "hidden"))
        HH, HL = s.sb("hidden_head", [P, 2, GT], F32R), s.sb("hidden_rest", [P, 2, GT], F32R)
        gate_bank, value_bank, weight_bank = (
            [s.ps(f"{n}{k}", [P, GT]) for k in range(2)] for n in ("gate_bank", "value_bank", "weight_bank"))
        y_bank = s.ps("y_bank", [P, CH, GT])
        gate_made, value_made, weight_made, silu_made, scaled_made, hidden_made, hh_made, hl_made, down_made, y_kept, cleared = (
            s.sem(n) for n in ("gate_made", "value_made", "weight_made", "silu_made", "scaled_made", "hidden_made",
                               "hh_made", "hl_made", "down_made", "y_kept", "cleared"))

        with nc.Block() as block:

            def blocks(eng, body):
                body(0, 0)
                with eng.Fori(0, BLOCKS // 2) as i:
                    body(2 * i + 1, 1)
                    body(2 * i + 2, 0)

            def begun(b, u, lag):
                return u >= lag or not isinstance(b, int) or b > 0

            @block.sync
            def _(sp):
                load(sp, 1)
                with sp.Fori(2, BLOCKS) as b:
                    load(sp, b)

            @block.tensor
            def _(pe):
                def product(out, a_head, a_rest, b_head, b_rest, first, last):
                    nc.tensor.matmul(out, a_head, b_head, start=first, stop=False)
                    nc.tensor.matmul(out, a_rest, b_head, start=False, stop=False)
                    return nc.tensor.matmul(out, a_head, b_rest, start=False, stop=last)

                def project(n, m, w, t, r):
                    pe.wait_ge(hh_made, n + 1)
                    pe.wait_ge(hl_made, n + 1)
                    if t == 0:
                        wait(pe, y_kept, m)
                    for c in range(CH):
                        cols = slice(DOWN + t * D + c * P, DOWN + t * D + (c + 1) * P)
                        last = product(y_bank[:, c, :], WH[:, w, cols], WL[:, w, cols], HH[:, r, :], HL[:, r, :],
                                       t == 0, t == TILES - 1)
                    last.then_inc(down_made, 1)

                def body(b, w):
                    pe.wait_ge(head_set, (b + 1) * PIECES)
                    pe.wait_ge(rest_set, (b + 1) * PIECES)
                    pe.wait_ge(rows_set, b + 1)
                    for u in range(UNITS):
                        n, g, t, r = b * UNITS + u, u // TILES, u % TILES, u % 2
                        for bank, at, free, made in ((gate_bank, UP, silu_made, gate_made),
                                                     (value_bank, VALUE, scaled_made, value_made)):
                            wait(pe, free, n - 1)
                            for c in range(CH):
                                cols = slice(at + c * BH + t * P, at + c * BH + (t + 1) * P)
                                last = product(bank[r][:, :], WH[:, w, cols], WL[:, w, cols],
                                               XH[:, c, GB * g:GB * g + GB, :], XL[:, c, GB * g:GB * g + GB, :],
                                               c == 0, c == CH - 1)
                            last.then_inc(made, 1)
                        wait(pe, hidden_made, n - 1)
                        nc.tensor.matmul(weight_bank[r][:, :], pick[:, w, t * P:(t + 1) * P],
                                         parts[:, g * GT:(g + 1) * GT], start=True, stop=True).then_inc(weight_made, 1)
                        if begun(b, u, 2):
                            v = (u - 2) % UNITS
                            project(n - 2, b * NG + (u - 2) // TILES, w if u >= 2 else 1 - w, v % TILES, r)

                blocks(pe, body)
                for u in range(UNITS - 2, UNITS):
                    project(LAST - UNITS + u, BLOCKS * NG - 1, 0, u % TILES, u % 2)

            @block.scalar
            def _(act):
                def head(n, r):
                    act.wait_ge(hidden_made, n + 1)
                    wait(act, down_made, n - 1)
                    nc.scalar.activation(HH[:, r, :], hidden[:, r, :], ACT.Copy).then_inc(hh_made, 1)

                def body(b, w, more=True):
                    for u in range(UNITS):
                        n, r = b * UNITS + u, u % 2
                        act.wait_ge(gate_made, n + 1)
                        wait(act, scaled_made, n - 1)
                        nc.scalar.activation(silu[:, r, :], gate_bank[r][:, :], ACT.Silu).then_inc(silu_made, 1)
                        if begun(b, u, 1):
                            head(n - 1, 1 - r)
                        if more and u == 3:
                            wait(act, down_made, b * UNITS)
                            set_rows(act, b + 1, 1 - w)
                        if more and u >= 4:
                            set_head(act, b + 1, 1 - w, u - 4)

                body(0, 0)
                with act.Fori(0, BLOCKS // 2 - 1) as i:
                    body(2 * i + 1, 1)
                    body(2 * i + 2, 0)
                body(BLOCKS - 2, 1)
                body(BLOCKS - 1, 0, more=False)
                head(LAST - 1, 1)

            @block.gpsimd
            def _(pool):
                def rest(n, r):
                    pool.wait_ge(hh_made, n + 1)
                    wait(pool, down_made, n - 1)
                    nc.gpsimd.tensor_tensor(HL[:, r, :], hidden[:, r, :], HH[:, r, :].bitcast(F32),
                                            ALU.subtract).then_inc(hl_made, 1)

                def body(b, w, more=True):
                    for u in range(UNITS):
                        n, r = b * UNITS + u, u % 2
                        if begun(b, u, 1):
                            rest(n - 1, 1 - r)
                        if more and u >= 4:
                            set_rest(pool, b + 1, 1 - w, u - 4)

                body(0, 0)
                with pool.Fori(0, BLOCKS // 2 - 1) as i:
                    body(2 * i + 1, 1)
                    body(2 * i + 2, 0)
                body(BLOCKS - 2, 1)
                body(BLOCKS - 1, 0, more=False)
                rest(LAST - 1, 1)

            @block.vector
            def _(dve):
                def keep(n, m, g):
                    here = YT[:, :, GB * g:GB * g + GB, :]
                    y = y_bank[:, :, :].rearrange("p c (b t) -> p c b t", b=GB)
                    dve.wait_ge(down_made, n + 1)
                    wait(dve, y_kept, m)
                    nc.vector.tensor_tensor(here, here, y, ALU.add).then_inc(y_kept, 1)

                def body(b, w):
                    for u in range(UNITS):
                        n, r = b * UNITS + u, u % 2
                        if u % TILES == 2 and begun(b, u, 3):
                            g = u // TILES - 1
                            keep(n - 3, b * NG + g, g % NG)
                        dve.wait_ge(silu_made, n + 1)
                        dve.wait_ge(value_made, n + 1)
                        wait(dve, hidden_made, n - 1)
                        nc.vector.tensor_tensor(scaled[:, r, :], silu[:, r, :], value_bank[r][:, :],
                                                ALU.mult).then_inc(scaled_made, 1)
                        dve.wait_ge(scaled_made, n + 1)
                        dve.wait_ge(weight_made, n + 1)
                        wait(dve, hl_made, n - 1)
                        nc.vector.tensor_tensor(hidden[:, r, :], scaled[:, r, :], weight_bank[r][:, :],
                                                ALU.mult).then_inc(hidden_made, 1)

                nc.vector.memset(YT[:, :, :, :], 0.0).then_inc(cleared, 1)
                dve.wait_ge(cleared, 1)
                blocks(dve, body)
                keep(LAST - 1, BLOCKS * NG - 1, NG - 1)


def build(nc, a, out):
    with ExitStack() as ctx:
        s = Space(nc, ctx, "all")
        X = s.sb("x", [P, NB, D])
        YT = s.sb("y", [P, CH, NB, T])
        ident, anti, identb = s.sb("ident", [P, P]), s.sb("anti", [P, P]), s.sb("identb", [P, P], BF16)
        eps, ones = s.sb("eps", [P, 1]), s.sb("ones", [P, P])
        with ExitStack() as layers:
            CT = layers.enter_context(nc.sbuf_tensor("context", [P, CH, NB, T], F32))
            with ExitStack() as part:
                XH = part.enter_context(nc.sbuf_tensor("attn_xh", [P, CH, NB, T], F32R))
                XL = part.enter_context(nc.sbuf_tensor("attn_xl", [P, CH, NB, T], F32R))

                def begin(ahead):
                    x_in, c_in = [s.sem(f"x_in{g}") for g in range(NG)], s.sem("c_in")
                    C = YT[:, :, :, :].rearrange("p c b t -> p (c b t)").rearrange("p (b d) -> p b d", b=NB)
                    stage_load(nc, a["x"], a["ctx_2048"], X, C, x_in, c_in, ident, identb, anti, eps, ones)
                    stage_renorm(nc, "norm0", X, ident, eps, XH=XH, XL=XL, ahead=ahead, x_in=x_in,
                                 context=(C, c_in, CT))

                stage_attention(nc, *(a[f"L0_attn_{n}"] for n in ("wq_codes", "wq_scales", "bq", "wk_codes", "wk_scales",
                                                                  "bk", "wv_codes", "wv_scales", "bv", "wo_codes",
                                                                  "wo_scales", "bo")),
                                XH, XL, YT, ident,
                                before=begin)
            with ExitStack() as part:
                XT = part.enter_context(nc.sbuf_tensor("wkv_xt", [P, CH, NB, T], F32))
                stage_renorm(nc, "norm1", X, ident, eps, YT=YT, XT=XT)
                stage_wkv(nc, a["L0_xattn_time_decay"], a["L0_xattn_time_first"], XT, CT, YT)
            stage_ternary_ffn(nc, *(a[f"L0_ffn_{n}"] for n in ("w1", "b1", "ln_g", "ln_b", "w2", "b2")),
                              X, YT, ident, identb, eps, ones)
            with ExitStack() as part:
                XT = part.enter_context(nc.sbuf_tensor("s6_xt", [P, CH, NB, T], F32))
                stage_s6(nc, *(a[f"L1_attn_{n}"] for n in ("x_proj_weight", "dt_proj_weight", "dt_proj_bias", "A_log", "D",
                                                           "out_proj_weight", "out_proj_bias")),
                         XT, YT, ident, before=lambda ahead: stage_renorm(nc, "norm3", X, ident, eps, XT=XT, ahead=ahead))
            with ExitStack() as part:
                XT = part.enter_context(nc.sbuf_tensor("conv_xt", [P, CH, NB, T], F32))
                stage_long_conv(nc, a["L1_xattn_ssm_kernel"], a["L1_xattn_D"], XT, CT, YT, anti, ident,
                                before=lambda ahead: stage_renorm(nc, "norm4", X, ident, eps, YT=YT, XT=XT, ahead=ahead))
        with ExitStack() as part:
            XH = part.enter_context(nc.sbuf_tensor("moe_xh", [P, CH, NB, T], F32R))
            XL = part.enter_context(nc.sbuf_tensor("moe_xl", [P, CH, NB, T], F32R))
            stage_experts(nc, a["L1_ffn_gate_w"], a["moe_gate"], a["moe_value"], a["moe_down"], a["moe_rows"],
                          XH, XL, YT, ident,
                          before=lambda ahead: stage_renorm(nc, "norm5", X, ident, eps, YT=YT, XH=XH, XL=XL, ahead=ahead))
        stage_renorm(nc, "end", X, ident, eps, YT=YT, out=out)


def kernel(**inputs):
    import numpy as _np
    import concourse.bacc as _bacc
    from concourse import mybir as _mybir
    from concourse.bass_utils import run_bass_kernel_spmd as _run

    nc = _bacc.Bacc("TRN2", target_bir_lowering=False, num_devices=1)
    arrays, args = {}, {}
    columns = ("L0_attn_bq", "L0_attn_bk", "L0_attn_bo", "L0_xattn_time_decay", "L0_xattn_time_first",
               "L1_attn_dt_proj_bias", "L1_attn_D", "L1_attn_out_proj_bias")
    inputs = {name: _np.asarray(value) for name, value in inputs.items()}
    routed = [inputs.pop(f"L1_ffn_{n}") for n in ("w_gate", "w_up", "w_down")]
    shared = [inputs.pop(f"L1_ffn_{n}") for n in ("sw_gate", "sw_up", "sw_down")]
    experts, _, width = routed[0].shape
    units = experts * width + shared[0].shape[1]
    padded = -(-units // P) * P
    zeros = _np.zeros((D, padded - units), routed[0].dtype)
    for name, own, all_ in zip(("moe_gate", "moe_value"), routed, shared):
        inputs[name] = _np.concatenate([own.transpose(1, 0, 2).reshape(D, experts * width), all_, zeros], axis=1)
    inputs["moe_down"] = _np.concatenate([routed[2].reshape(experts * width, D), shared[2], zeros.T], axis=0)
    owner = _np.minimum(_np.arange(padded) // width, experts)
    inputs["moe_rows"] = (owner[None, :] == _np.arange(32)[:, None]).astype(_np.float32)
    for name, value in inputs.items():
        a = _np.asarray(value)
        if name in columns:
            a = a.reshape(-1, P).T
        if name == "L1_xattn_ssm_kernel":
            a = _np.pad(a, ((0, 0), (P, 0)))
        a = _np.ascontiguousarray(a)
        arrays[f"in_{name}"] = a
        args[name] = nc.dram_tensor(f"in_{name}", a.shape, _mybir.dt.from_np(a.dtype), kind="ExternalInput").ap()
    out = nc.dram_tensor("out", (NB, T, D), F32, kind="ExternalOutput").ap()
    build(nc, args, out)
    r = _run(nc, [arrays], core_ids=[0])
    return r.results[0]["out"]
```
